# Optimizing a Trainium2 kernel written in Bass

```python
import numpy as np
import jax
import jax.numpy as jnp

def _softmax(x, axis=-1):
    return jax.nn.softmax(x, axis=axis)

def _gelu(x):
    return jax.nn.gelu(x, approximate=True)

def _silu(x):
    return jax.nn.silu(x)

def _sigmoid(x):
    return jax.nn.sigmoid(x)

def _layernorm(x, axis=-1, eps=1e-05):
    m = jnp.mean(x, axis=axis, keepdims=True)
    v = jnp.var(x, axis=axis, keepdims=True)
    return (x - m) / jnp.sqrt(v + eps)

def _scatter_add(tgt, idx, src, axis=0):
    return tgt.at[idx].add(src)

def _segment_sum(src, seg, n):
    return jax.ops.segment_sum(src, seg, n)
kernel_name = 'mk_gnn_resnorm_d4_gnn_r64_1de653'

def setup_inputs(seed: int=0):
    np.random.seed(seed)
    _w = jnp.asarray

    def _rec_inputs():
        import jax
        import jax.numpy as jnp
        _gk = jax.random.key(seed)
        x = -0.0005121 + 1.001 * jax.random.normal(jax.random.fold_in(_gk, 1), (100000, 32), jnp.float32)
        src = jax.random.randint(jax.random.fold_in(_gk, 2), (25000,), 0, 100000, jnp.int32)
        dst = jax.random.randint(jax.random.fold_in(_gk, 3), (25000,), 0, 100000, jnp.int32)
        _o = jnp.argsort(dst, stable=True)
        src = src[_o]
        dst = dst[_o]
        edge_attr_16 = 0.000196303 + 1.00016 * jax.random.normal(jax.random.fold_in(_gk, 12), (25000, 16), jnp.float32)
        edge_attr_32 = -8.16379e-05 + 0.999858 * jax.random.normal(jax.random.fold_in(_gk, 13), (25000, 32), jnp.float32)
        edge_weight = jax.random.uniform(jax.random.fold_in(_gk, 15), (25000,), jnp.float32, 0.0, 1)
        return (x, src, dst, edge_attr_16, edge_attr_32, edge_weight)
    x, src, dst, edge_attr_16, edge_attr_32, edge_weight = _rec_inputs()

    def _L0_gnn_setup():
        import jax, jax.numpy as jnp
        import numpy as np
        N_NODES = 100000
        N_EDGES = 25000
        D_NODE = 32
        D_EDGE = 16
        D_HID = 64
        D_OUT = 32
        key = jax.random.key(seed)
        ks = jax.random.split(key, 7)
        x = jax.random.normal(ks[0], (N_NODES, D_NODE), dtype=jnp.float32)
        edge_index = jax.random.randint(ks[1], (2, N_EDGES), 0, N_NODES, dtype=jnp.int64)
        edge_attr = jax.random.normal(ks[2], (N_EDGES, D_EDGE), dtype=jnp.float32)
        W1 = jax.random.normal(ks[3], (D_NODE + D_EDGE, D_HID), dtype=jnp.float32) * (2.0 / (D_NODE + D_EDGE)) ** 0.5
        b1 = jnp.zeros((D_HID,), dtype=jnp.float32)
        W2 = jax.random.normal(ks[4], (D_HID, D_OUT), dtype=jnp.float32) * (2.0 / D_HID) ** 0.5
        b2 = jnp.zeros((D_OUT,), dtype=jnp.float32)
        return {'x': x, 'edge_index': edge_index, 'edge_attr': edge_attr, 'W1': W1, 'b1': b1, 'W2': W2, 'b2': b2}
    _L0_gnn_all = _L0_gnn_setup()
    _L0_gnn_in = {k: v for k, v in _L0_gnn_all.items() if k in ('W1', 'b1', 'W2', 'b2')}
    del _L0_gnn_all

    def _L1_gnn_setup():
        import jax, jax.numpy as jnp
        import numpy as np
        N_NODES = 50000
        DEG = 16
        N_HEAD = 4
        F_IN = 32
        F_OUT = 32
        key = jax.random.key(seed)
        k_h, k_w, k_fw, k_fb = jax.random.split(key, 4)
        h = jax.random.normal(k_h, (N_NODES, F_IN), dtype=jnp.float32)
        src = jnp.repeat(jnp.arange(N_NODES, dtype=jnp.int64), DEG)
        offs = (jnp.arange(DEG, dtype=jnp.int64) + 1) * 97
        dst = (src.reshape(N_NODES, DEG) + offs[None, :]).reshape(-1) % N_NODES
        edge_index = jnp.stack([src, dst], axis=0)
        gain = 1.414
        bound_w = gain * np.sqrt(6.0 / (F_IN + F_OUT))
        w = jax.random.uniform(k_w, (N_HEAD, F_IN, F_OUT), jnp.float32, -bound_w, bound_w)
        bound_fc = np.sqrt(1.0 / (2 * F_OUT))
        fc_w = jax.random.uniform(k_fw, (1, 2 * F_OUT), jnp.float32, -bound_fc, bound_fc)
        fc_b = jax.random.uniform(k_fb, (1,), jnp.float32, -bound_fc, bound_fc)
        bias = jnp.zeros((F_OUT,), jnp.float32)
        return {'h': h, 'edge_index': edge_index, 'w': w, 'fc_w': fc_w, 'fc_b': fc_b, 'bias': bias}
    _L1_gnn_all = _L1_gnn_setup()
    _L1_gnn_in = {k: v for k, v in _L1_gnn_all.items() if k in ('w', 'fc_w', 'fc_b', 'bias')}
    del _L1_gnn_all

    def _L2_gnn_setup():
        import jax, jax.numpy as jnp
        import numpy as np
        N_NODES = 100000
        N_EDGES = 25000
        F_IN = 32
        F_OUT = 32
        key = jax.random.key(seed)
        kx, kr, kc, kv, kw = jax.random.split(key, 5)
        x = jax.random.normal(kx, (N_NODES, F_IN), dtype=jnp.float32)
        rows = jnp.sort(jax.random.randint(kr, (N_EDGES,), 0, N_NODES, dtype=jnp.int64))
        cols = jax.random.randint(kc, (N_EDGES,), 0, N_NODES, dtype=jnp.int64)
        vals = jax.random.uniform(kv, (N_EDGES,), dtype=jnp.float32)
        weight = jax.random.normal(kw, (F_IN, F_OUT), dtype=jnp.float32) / np.sqrt(F_IN)
        return {'x': x, 'rows': rows, 'cols': cols, 'vals': vals, 'weight': weight}
    _L2_gnn_all = _L2_gnn_setup()
    _L2_gnn_in = {k: v for k, v in _L2_gnn_all.items() if k in ('weight',)}
    del _L2_gnn_all

    def _L3_gnn_setup():
        import jax, jax.numpy as jnp
        import numpy as np
        N_NODES = 100000
        N_EDGES = 50000
        D = 32
        N_LAYERS = 5

        def _gine_layer(x, edge_attr, src, dst, eps_l, W1_l, b1_l, W2_l, b2_l, n_nodes):
            msg = jax.nn.relu(x[src] + edge_attr)
            agg = jax.ops.segment_sum(msg, dst, num_segments=n_nodes)
            h = (1.0 + eps_l) * x + agg
            h = jax.nn.relu(h @ W1_l.T + b1_l)
            return h @ W2_l.T + b2_l
        key = jax.random.key(seed)
        ks = jax.random.split(key, 8)
        x = jax.random.normal(ks[0], (N_NODES, D), dtype=jnp.float32)
        edge_attr = jax.random.normal(ks[1], (N_EDGES, D), dtype=jnp.float32)
        edge_index = jax.random.randint(ks[2], (2, N_EDGES), 0, N_NODES, dtype=jnp.int64)
        eps = jnp.zeros((N_LAYERS,), dtype=jnp.float32)
        scale = 1.0 / np.sqrt(D)
        W1 = jax.random.normal(ks[3], (N_LAYERS, D, D), dtype=jnp.float32) * scale
        b1 = jax.random.normal(ks[4], (N_LAYERS, D), dtype=jnp.float32) * scale
        W2 = jax.random.normal(ks[5], (N_LAYERS, D, D), dtype=jnp.float32) * scale
        b2 = jax.random.normal(ks[6], (N_LAYERS, D), dtype=jnp.float32) * scale
        return {'x': x, 'edge_attr': edge_attr, 'eps': eps, 'W1': W1, 'b1': b1, 'W2': W2, 'b2': b2, 'edge_index': edge_index}
    _L3_gnn_all = _L3_gnn_setup()
    _L3_gnn_in = {k: v for k, v in _L3_gnn_all.items() if k in ('eps', 'W1', 'b1', 'W2', 'b2')}
    del _L3_gnn_all
    return {'x': x, 'src': src, 'dst': dst, 'edge_attr_16': edge_attr_16, 'edge_attr_32': edge_attr_32, 'edge_weight': edge_weight, 'L0_gnn_W1': _L0_gnn_in['W1'], 'L0_gnn_b1': _L0_gnn_in['b1'], 'L0_gnn_W2': _L0_gnn_in['W2'], 'L0_gnn_b2': _L0_gnn_in['b2'], 'L1_gnn_w': _L1_gnn_in['w'], 'L1_gnn_fc_w': _L1_gnn_in['fc_w'], 'L1_gnn_fc_b': _L1_gnn_in['fc_b'], 'L1_gnn_bias': _L1_gnn_in['bias'], 'L2_gnn_weight': _L2_gnn_in['weight'], 'L3_gnn_eps': _L3_gnn_in['eps'], 'L3_gnn_W1': _L3_gnn_in['W1'], 'L3_gnn_b1': _L3_gnn_in['b1'], 'L3_gnn_W2': _L3_gnn_in['W2'], 'L3_gnn_b2': _L3_gnn_in['b2']}

def reference(x, src, dst, edge_attr_16, edge_attr_32, edge_weight, L0_gnn_W1, L0_gnn_b1, L0_gnn_W2, L0_gnn_b2, L1_gnn_w, L1_gnn_fc_w, L1_gnn_fc_b, L1_gnn_bias, L2_gnn_weight, L3_gnn_eps, L3_gnn_W1, L3_gnn_b1, L3_gnn_W2, L3_gnn_b2):
    import jax
    import jax.numpy as jnp

    def _L0_gnn_ref(x, edge_index, edge_attr, W1, b1, W2, b2):
        import jax, jax.numpy as jnp
        import numpy as np
        N_NODES = 100000
        N_EDGES = 25000
        D_NODE = 32
        D_EDGE = 16
        D_HID = 64
        D_OUT = 32
        row, col = (edge_index[0], edge_index[1])
        inp = jnp.concatenate([x[col], edge_attr], axis=1)
        h = jax.nn.relu(inp @ W1 + b1)
        messages = h @ W2 + b2
        message = jax.ops.segment_sum(messages, row, num_segments=x.shape[0])
        return message

    def _L1_gnn_ref(h, edge_index, w, fc_w, fc_b, bias):
        import jax, jax.numpy as jnp
        import numpy as np
        N_NODES = 50000
        DEG = 16
        N_HEAD = 4
        F_IN = 32
        F_OUT = 32
        n_head, f_in, f_out = w.shape
        n = h.shape[0]
        src, dst = (edge_index[0], edge_index[1])
        hp = jnp.einsum('nf,hfo->hno', h, w)
        w_src = fc_w[0, :f_out]
        w_dst = fc_w[0, f_out:]
        a_src = jnp.einsum('hnf,f->hn', hp, w_src)
        a_dst = jnp.einsum('hnf,f->hn', hp, w_dst)
        e = a_src[:, src] + a_dst[:, dst] + fc_b[0]
        e = jax.nn.leaky_relu(e, negative_slope=0.2)
        seg_max = jax.ops.segment_max(e.T, src, num_segments=n)
        e = jnp.exp(e - seg_max.T[:, src])
        seg_sum = jax.ops.segment_sum(e.T, src, num_segments=n)
        att = e / seg_sum.T[:, src]
        msg = att[:, :, None] * hp[:, dst, :]
        agg = jax.vmap(lambda m: jax.ops.segment_sum(m, src, num_segments=n))(msg)
        out = agg.mean(axis=0) + bias
        return out

    def _L2_gnn_ref(x, rows, cols, vals, weight):
        import jax, jax.numpy as jnp
        import numpy as np
        N_NODES = 100000
        N_EDGES = 25000
        F_IN = 32
        F_OUT = 32
        gathered = x[cols] * vals[:, None]
        z = jax.ops.segment_sum(gathered, rows, num_segments=x.shape[0])
        return z @ weight

    def _L3_gnn_ref(x, edge_attr, eps, W1, b1, W2, b2, edge_index):
        import jax, jax.numpy as jnp
        import numpy as np
        N_NODES = 100000
        N_EDGES = 50000
        D = 32
        N_LAYERS = 5

        def _gine_layer(x, edge_attr, src, dst, eps_l, W1_l, b1_l, W2_l, b2_l, n_nodes):
            msg = jax.nn.relu(x[src] + edge_attr)
            agg = jax.ops.segment_sum(msg, dst, num_segments=n_nodes)
            h = (1.0 + eps_l) * x + agg
            h = jax.nn.relu(h @ W1_l.T + b1_l)
            return h @ W2_l.T + b2_l
        src = edge_index[0]
        dst = edge_index[1]
        n_nodes = x.shape[0]
        out = x
        for l in range(N_LAYERS):
            out = jax.nn.relu(_gine_layer(x, edge_attr, src, dst, eps[l], W1[l], b1[l], W2[l], b2[l], n_nodes))
        return out
    edge_index = jnp.stack([src, dst])
    x = _layernorm(x + _L0_gnn_ref(x, edge_index, edge_attr_16, L0_gnn_W1, L0_gnn_b1, L0_gnn_W2, L0_gnn_b2), axis=-1)
    x = _layernorm(x + _L1_gnn_ref(x, edge_index, L1_gnn_w, L1_gnn_fc_w, L1_gnn_fc_b, L1_gnn_bias), axis=-1)
    x = _layernorm(x + _L2_gnn_ref(x, src, dst, edge_weight, L2_gnn_weight), axis=-1)
    x = _layernorm(x + _L3_gnn_ref(x, edge_attr_32, L3_gnn_eps, L3_gnn_W1, L3_gnn_b1, L3_gnn_W2, L3_gnn_b2, edge_index), axis=-1)
    return x

_drawn_inputs = setup_inputs


def setup_inputs(seed=0):
    import zlib

    import numpy as np

    out = dict(_drawn_inputs(seed))
    spreads = {'L0_gnn_b1': (0.0, 0.342),
     'L0_gnn_b2': (0.0, 0.271),
     'L1_gnn_bias': (0.0, 0.1),
     'L3_gnn_eps': (0.0, 0.8)}
    factors = {'L1_gnn_fc_w': 3.234}
    for name, (base, spread) in spreads.items():
        noise = np.random.default_rng([zlib.crc32(name.encode()), seed]).standard_normal(out[name].shape)
        drawn = base * np.exp(spread * noise) if base else spread * noise
        out[name] = jnp.asarray(drawn.astype(out[name].dtype))
    for name, factor in factors.items():
        out[name] = (out[name] * factor).astype(out[name].dtype)
    return out
```

```python
from contextlib import ExitStack

import concourse.bass as bass
from concourse import mybir

F32 = mybir.dt.float32
I32 = mybir.dt.int32
U8 = mybir.dt.uint8
I8 = mybir.dt.int8
ALU = mybir.AluOpType
ACT = mybir.ActivationFunctionType
AXX = mybir.AxisListType.X

P = 128
NODES, EDGES, F = 100000, 25000, 32
C = P // F
NT = -(-EDGES // (C * P))
J = NT * P
ROWS = C * J
KB = 7
NB = NT // KB
W = KB * P
HALF = 32768
SC = HALF // P
EP, ER = 125, 200
ATT = 16 + 32 + 1 + 1
ROW4 = 3 * F + 1
NEG = -1.0e30
EPS = 1e-5
SPLIT, PAD, FAR = 51000.0, 110000.0, 30000.0
HID = 64
GINE = 1
NL = 3 + GINE
DJ = NODES // C
ND = -(-DJ // W)
BG = 14
PER = -(-ND // NL) + -(-ND // NL) % 2
DENSE = [(min(i * PER, ND), min((i + 1) * PER, ND)) for i in range(NL)]
NW = 9 * C + 5
N_CONST = 12
assert ND % 2 == 0 and NT % KB == 0 and ROWS % (P * BG) == 0


STEPS = {
    "turn_in": (1, 1, 0, 0, 0), "rows_in": (1, 1, 0, 1, 0), "rows_out": (1, 1, 0, 0, 1), "final_out": (1, 1, 0, 0, 0), "last_in": (1, 1, 0, 0, 0),
    "ln": (2, 3, 1, 0, 0), "mlp": (2, 1, 1, 0, 0), "edge": (4, 4, 1, 0, 0), "score": (1, 1, 1, 0, 0),
    "attend": (8, 0, 5, 0, 0), "scale": (1, 1, 1, 0, 0), "gine": (0, 1, 1, 0, 0), "to_row4": (2, 4, 0, 0, 0),
    "from_row4": (3, 6, 0, 0, 0),
}


class Count:

    def __init__(self, pe=0, act=0, dve=0, load=0, store=0):
        self.pe, self.act, self.dve, self.load, self.store = pe, act, dve, load, store


def count_steps():
    before, now = {}, [(0,) * 5, (0,) * 5]

    def step(lane, kind, *key):
        assert key not in before
        before[key] = Count(*now[lane])
        now[lane] = tuple(a + b for a, b in zip(now[lane], STEPS[kind]))

    for s in range(2):
        for b in range(NB):
            step(b % 2, "turn_in", "turn", s, b)
    for L in range(NL):
        if L == 1:
            for b in range(NB):
                step(b % 2, "score", "score", b)
        for b in range(NB):
            step(b % 2, ("edge", "attend", "scale", "gine")[min(L, 3)], "msg", L, b)
        before["sums", L] = Count(*now[1])
        if L < NL - 1:
            for b in range(NB):
                step(b % 2, "rows_out", "table", L, b)
        before["back", L] = Count(*now[1])
        for i in range(*DENSE[L]):
            for n, kind in enumerate(["rows_in"] + ["ln"] * 3 + ["mlp"] * GINE + ["ln", "rows_out"]):
                step(i % 2, kind, "dense", i, n)
        for b in range(NB):
            step(b % 2, "ln" if L < 3 else "mlp", "local", L, b)
        for b in range(NB):
            if L < NL - 1:
                step(b % 2, "rows_in", "update", L, b)
            step(b % 2, "ln" if L < 3 else "mlp", "other", L, b)
        if L == 2:
            for b in range(NB):
                step(b % 2, "to_row4", "to4", b)
            for b in range(NB):
                step(b % 2, "from_row4", "from4", b)
    for s in range(2):
        for b in range(NB):
            step(b % 2, "last_in", "last_in", s, b)
            step(b % 2, "ln", "last_ln", s, b)
            step(b % 2, "final_out", "last_out", s, b)
    return before, now


def build(nc, x, src, dst, ea16, ea32, ew, w1a, b1a, w2a, b2a, watt, fcw, fcb, batt, wz, wzt, eps, wg, bg, out):
    ctx = ExitStack()
    with ctx:
        def sb(name, shape, dt=F32):
            return ctx.enter_context(nc.sbuf_tensor(name, shape, dt))

        def sem(name):
            return ctx.enter_context(nc.semaphore(name))

        def dram(name, shape, dt=F32):
            return nc.dram_tensor(name, shape, dt, kind="Internal").ap()

        attN = dram("attN", (EDGES, ATT))
        attS = dram("attS", (ROWS, ATT))
        row4 = dram("row4", (ROWS, ROW4))
        row4d = dram("row4d", (ROWS, ROW4))
        table = dram("table", (ROWS, F))
        upd = [dram("upd_d", (ROWS, F)), dram("upd_s", (ROWS, F))]
        sorted_d = [dram(f"sorted{i}", (HALF + 2, 1)) for i in range(2)]
        list_d = [dram(f"list{i}", (HALF, 1)) for i in range(2)]
        mask_d = [dram(f"mask{i}", (2, ROWS), U8) for i in range(2)]

        big = sb("big", [P, 4 * J])
        S, D, T1, T2 = (big[:, i * J:(i + 1) * J] for i in range(4))
        rest = sb("rest", [P, J])
        EA = rest[:, :]
        at = [0]

        def part(n):
            a = rest[:, at[0]:at[0] + n]
            at[0] += n
            assert at[0] <= J
            return a

        flips = part(16 * 2 * SC // 4).bitcast(I8).rearrange("p (k w) -> p k w", k=16)
        va, vb, t0, t1, t2, t3 = (part(2 * SC) for _ in range(6))
        srt = [part(SC), part(SC)]
        iop = part(SC)
        nat32, nat16, nat_w = big[0:EP, 0:6400], big[0:EP, 6400:9600], big[0:EP, 9600:9800]
        nat_dst, nat_src = (big[0:EP, a:a + 200].bitcast(I32) for a in (9800, 10000))
        index2, gray = (big[:, a:a + 2 * SC].bitcast(I32) for a in (10240, 10752))
        nat_att = big[0:EP, 2 * J:2 * J + ER * ATT]
        NS, NE, PF, QB = (sb(n, [P, J], U8) for n in ("not_start", "not_end", "first_seg", "last_seg"))
        RI = [sb(f"rows{i}", [P, W]) for i in range(2)]
        AB = [sb(f"arg{i}", [P, W]) for i in range(2)]
        HB = [sb(f"hid{i}", [P, W]) for i in range(2)]
        X3 = [sb(f"res{i}", [P, W]) for i in range(2)]
        RA = sb("edge_rows", [P, KB * C * ATT])
        mask8 = RA[:, 0:98].bitcast(U8).rearrange("p (m f) -> p m f", m=2)
        RA4 = RA[:, :].rearrange("p (k c w) -> p k c w", k=KB, c=C)
        G = [RA[:, i * BG * F:(i + 1) * BG * F] for i in range(2)]
        ident = sb("ident", [P, P])
        center = sb("center", [P, P])
        mean = sb("mean", [P, P])
        shf = sb("shf", [P, P])
        shb = sb("shb", [P, P])
        ltri = part(P)
        wA = sb("wA", [P, 2, P])
        wE = sb("wE", [64, 2, P])
        wB = sb("wB", [P, 2, P])
        wH = sb("wH", [P, 4, P])
        wSel = sb("wSel", [P, 4, P])
        wSc = sb("wSc", [P, 2, P])
        wZ = sb("wZ", [P, 2, P])
        wG = sb("wG", [P, 2 * GINE, P])
        wX = sb("wX", [P, GINE, P])
        cols = sb("cols", [P, 32])
        zero_c, eps_c, cb_c, fcb_c, b1a_c, b2a_c, batt_c = (cols[:, i:i + 1] for i in range(7))
        carry, ctmp, p40, p56 = (cols[:, i:i + 1] for i in range(7, 11))
        bg_c = cols[:, 11:11 + 2 * GINE]
        eps_g = cols[:, 21:21 + GINE]
        rs_c = cols[:, 26:28]
        cy_c = cols[:, 28:30]
        rm_c = cols[:, 30:32]
        fcr = sb("fcr", [P, 2 * F])
        wat = sb("wat", [P, 4 * F])
        wtmp = part(4 * F)
        rowb = X3[0][0:1, 0:2 * P + 1]
        sG, dG, jI = (sb(n, [P, C * NT], I32) for n in ("src_id", "dst_id", "src_row"))
        sU = sb("src_end", [P, C * NT])
        dUI = sb("dst_end", [P, C * NT], I32)
        sUI = sG
        hI = [sb(f"home{i}", [P, C * NT], I32) for i in range(2)]
        aI = [sb(f"from{i}", [P, C * NT], I32) for i in range(2)]
        eI = aI[0]

        ps = [[ctx.enter_context(nc.psum_tensor(f"ps{l}{u}", [P, 1024], F32)) for u in range(2)] for l in range(2)]
        pi = ps[1][0]
        pc = ps[1][1][:, 1000:1008]

        consts = sem("consts")
        w_zero = sem("weights_cleared")
        w_in = sem("weights_in")
        src_in = sem("src_in")
        nat_in = sem("natural_in")
        nat_rows = sem("natural_rows")
        attn_out = sem("attn_out")
        ready = sem("weights_ready")
        wz_mm = sem("wz_mm")
        turn_rdy, turned = sem("turn_ready"), sem("turned")
        small_rdy, small_mm = sem("small_ready"), sem("small_mm")
        dchain = sem("dve_chain")
        srt_rdy = sem("sorted_ready")
        srt_out = sem("sorted_out")
        nb_in = sem("neighbours_in")
        mask_rdy, mask_out, mask_in = sem("mask_ready"), sem("mask_out"), sem("mask_in")
        idx_rdy = sem("index_ready")
        pool_ok = sem("pool_chain")
        ga = [sem("att_rows0"), sem("att_rows1")]
        dcol = sem("dst_col")
        atts_out = [sem("atts_out0"), sem("atts_out1")]
        gx = [sem("x_src_rows"), sem("x_dst_rows")]
        pe_n = [sem("pe_lane0"), sem("pe_lane1")]
        act_n = [sem("act_lane0"), sem("act_lane1")]
        dve_n = [sem("dve_lane0"), sem("dve_lane1")]
        ld_n = [sem("load_lane0"), sem("load_lane1")]
        st_n = [sem("store_lane0"), sem("store_lane1")]
        ra_in = sem("edge_rows_in")
        msg_act = sem("msg_act")
        e_rdy, e_exp = sem("exp_ready"), sem("exp_done")
        att_rdy = sem("att_ready")
        fix_n = sem("prefix_ready")
        tot_n = sem("total_ready")
        cr_rdy, cr_mm, cr_used = sem("carry_ready"), sem("carry_shifted"), sem("carry_used")
        gs = [sem("picked_in0"), sem("picked_in1")]
        ss = [sem("put_out0"), sem("put_out1")]
        upd_n = sem("updates_out")
        zero_rdy, zeroed = sem("zero_ready"), sem("zeroed")
        r4_out = [sem("row4_out0"), sem("row4_out1")]
        table_out = sem("table_out")
        dense_out = sem("dense_out")
        last_in = [sem("last_in0"), sem("last_in1")]
        g4 = [sem("row4_in0"), sem("row4_in1")]
        d4 = [sem("row4d_out0"), sem("row4d_out1")]
        sux = sem("src_end_ready")
        fin = [sem("final_put0"), sem("final_put1")]

        block = ctx.enter_context(nc.Block())

        def blk(t, b):
            return t[:, b * W:(b + 1) * W]

        def rows128(t, b):
            return t.rearrange("(b k p c) w -> b p k (c w)", b=NB, k=KB, p=P, c=C)[b]

        def xrows(t, i):
            j0 = min(i * W, DJ - W)
            return t.rearrange("(j c) f -> j (c f)", c=C)[j0:j0 + W, :].rearrange("(p r) q -> p (r q)", r=KB)


        NA = KB * C * ATT
        att_buf = [T1[:, i * NA:(i + 1) * NA] for i in range(2)]
        N4 = KB * C * ROW4
        r4_buf = [T1[:, i * N4:(i + 1) * N4] for i in range(2)]
        g4_buf = [T2[:, i * N4:(i + 1) * N4] for i in range(2)]
        before, total = count_steps()

        def kview(t):
            return t.rearrange("p (k w) -> p k w", k=KB)

        def puts(s, b):
            return s * uses(NB + 1 - b % 2) + uses(b)

        def uses(b):
            return b // 2

        @block.sync
        def _(sp):
            sp.wait_ge(consts, N_CONST)
            sp.wait_ge(w_zero, 1)
            n = 0

            def win(o, i):
                nonlocal n
                sp.dma_start(o, i).then_inc(w_in, 16)
                n += 1

            def column(v):
                return v.rearrange("(f o) -> f o", o=1)

            with nc.allow_non_contiguous_dma(reason="small weights"):
                for c in range(C):
                    q = slice(F * c, F * c + F)
                    g, h = divmod(c, 2)
                    win(wA[q, g, HID * h:HID * h + HID], w1a[0:F, :])
                    win(wE[16 * c:16 * c + 16, g, HID * h:HID * h + HID], w1a[F:F + 16, :])
                    win(wB[HID * h:HID * h + HID, g, q], w2a)
                    win(wat[q, :], watt.rearrange("f h o -> f (h o)"))
                    win(wZ[q, 0, q], wzt)
                    win(wG[q, :, q], wg[:, 8:10, :])
                    win(bg_c[q, :], bg[:, 8:10])
                    win(b2a_c[q, :], column(b2a))
                    win(batt_c[q, :], column(batt))
                for h in range(2):
                    win(b1a_c[HID * h:HID * h + HID, :], column(b1a))
                win(fcr[:, :], fcw.to_broadcast([P, 2 * F]))
                win(fcb_c, fcb.rearrange("(o w) -> o w", o=1).to_broadcast([P, 1]))
                win(eps_g, eps.rearrange("(o w) -> o w", o=1)[:, 4:5].to_broadcast([P, GINE]))
            assert n == NW

            sp.dma_start(nat_src, src.rearrange("(p r) -> p r", r=ER)).then_inc(src_in, 16)
            sp.dma_start(nat_dst, dst.rearrange("(p r) -> p r", r=ER)).then_inc(nat_in, 16)
            sp.dma_start(nat_w, ew.rearrange("(p r) -> p r", r=ER)).then_inc(nat_in, 16)
            sp.dma_start(nat16, ea16.rearrange("(p r) w -> p (r w)", r=ER)).then_inc(nat_in, 16)
            sp.dma_start(nat32, ea32.rearrange("(p r) w -> p (r w)", r=ER)).then_inc(nat_in, 16)
            sp.wait_ge(nat_rows, 4)
            sp.dma_start(attN.rearrange("(p r) w -> p (r w)", r=ER), nat_att).then_inc(attn_out, 16)
            for u in upd:
                for b in range(NB):
                    sp.dma_start(u.rearrange("(b p r) w -> b p (r w)", b=NB, p=P)[b], RI[0][:, :]).then_inc(zeroed, 16)
            with nc.allow_non_contiguous_dma(reason="end marks"):
                for i in range(2):
                    sp.dma_start(sorted_d[i][0:1, :], zero_c[0:1, :]).then_inc(zeroed, 16)
                    sp.dma_start(sorted_d[i][HALF + 1:HALF + 2, :], zero_c[0:1, :]).then_inc(zeroed, 16)
            sp.wait_ge(zeroed, 16 * (2 * NB + 4))

            def after_sort(i, k):
                sp.wait_ge(srt_rdy, k)
                sp.dma_start(sorted_d[i][1:HALF + 1, :].rearrange("(p f) o -> p (f o)", p=P), srt[i]).then_inc(srt_out, 16)
                sp.wait_ge(srt_out, 16 * k)
                base = sorted_d[i].rearrange("n o -> (n o)")
                for off, o in ((1, t0), (2, t1)):
                    sp.dma_start(o[0:98, 0:256].rearrange("q (g p) -> q g p", g=2),
                                 base[off:off + ROWS].rearrange("(g q p) -> q g p", g=2, q=98)).then_inc(nb_in, 16)
                for off, o in ((0, t2[:, 0:196]), (1, t2[:, 256:452]), (2, t3[:, 0:196])):
                    sp.dma_start(o, base[off:off + ROWS].rearrange("(p f) -> p f", p=P)).then_inc(nb_in, 16)

            def masks_out(i):
                sp.wait_ge(mask_rdy, i + 1)
                with nc.allow_non_contiguous_dma(reason="rows of 196 bytes"):
                    sp.dma_start(mask_d[i].rearrange("m (p f) -> p m f", p=P), mask8).then_inc(mask_out, 16)
                sp.wait_ge(mask_out, 16 * (i + 1))

            def masks_in(i):
                for m, o in ((0, NS), (1, NE)):
                    for c in range(C):
                        sp.dma_start(o[F * c:F * c + F, :],
                                     mask_d[i][m:m + 1, c * J:(c + 1) * J].to_broadcast([F, J])).then_inc(mask_in, 16)

            def after_list(i, k):
                sp.wait_ge(srt_rdy, k)
                sp.dma_start(list_d[i].rearrange("(p f) o -> p (f o)", p=P), t0[:, 0:256]).then_inc(srt_out, 16)
                sp.wait_ge(srt_out, 16 * k)
                sp.dma_start(t1[0:98, 0:256].rearrange("q (g p) -> q g p", g=2),
                             list_d[i].rearrange("n o -> (n o)")[0:ROWS].rearrange("(g q p) -> q g p", g=2, q=98)).then_inc(nb_in, 16)

            after_sort(0, 1)
            masks_out(0)
            masks_in(0)
            for b in range(NB):
                sp.wait_ge(ga[b % 2], 16 * C * KB * (uses(b) + 1))
                sp.dma_start(rows128(attS, b), kview(att_buf[b % 2])).then_inc(atts_out[b % 2], 16)
            after_sort(1, 2)
            masks_out(1)
            after_list(0, 3)
            for i in range(2):
                sp.wait_ge(atts_out[i], 16 * uses(NB + 1 - i))

            def lane_done(l, n):
                if n.pe:
                    sp.wait_ge(pe_n[l], n.pe)
                if n.act:
                    sp.wait_ge(act_n[l], n.act)
                if n.store:
                    sp.wait_ge(st_n[l], 16 * n.store)

            def load(l, n, ap):
                lane_done(l, n)
                sp.dma_start(kview(RI[l][:, :]) if len(ap.shape) == 3 else RI[l][:, :], ap).then_inc(ld_n[l], 16)

            def store(l, n, ap):
                sp.wait_ge(act_n[l], n.act + 1)
                sp.dma_start(ap, kview(RI[l][:, :]) if len(ap.shape) == 3 else RI[l][:, :]).then_inc(st_n[l], 16)

            def edge_rows(b, free):
                free(b)
                sp.dma_start(kview(RA[:, :]), rows128(attS, b)).then_inc(ra_in, 16)

            for L in range(NL):
                def read_before(b):
                    if b:
                        sp.wait_ge(act_n[(b - 1) % 2], before["msg", L, b - 1].act + 1)
                if L in (0, 2):
                    for b in range(NB):
                        edge_rows(b, read_before)
                if L < NL - 1:
                    for b in range(NB):
                        store(b % 2, before["table", L, b], rows128(table, b))
                    for b in range(2):
                        sp.wait_ge(st_n[b], 16 * (before["table", L, NB - 2 + (NB - b) % 2].store + 1))
                    sp.sem_inc(table_out, 1)
                for i0 in range(*DENSE[L], 2):
                    pair = (i0, i0 + 1)
                    for i in pair:
                        load(i % 2, before["dense", i, 0], xrows(x, i))
                    for i in pair:
                        l, n = i % 2, before["dense", i, 6]
                        if i == ND - 1:
                            sp.wait_ge(st_n[1 - l], 16 * (before["dense", i - 1, 6].store + 1))
                            if n.store:
                                sp.wait_ge(st_n[l], 16 * n.store)
                        store(l, n, xrows(out, i))
                if L < NL - 1:
                    sp.wait_ge(upd_n, L + 1)
                    for b in range(NB):
                        load(b % 2, before["update", L, b], rows128(upd[0 if L < 3 else 1], b))
                if L == 2:
                    def read4(b):
                        if b:
                            sp.wait_ge(act_n[(b - 1) % 2], before["to4", b - 1].act + 4)
                        else:
                            sp.wait_ge(act_n[(NB - 1) % 2], before["msg", 2, NB - 1].act + 1)
                    for b in range(NB):
                        edge_rows(b, read4)
                        sp.wait_ge(act_n[b % 2], before["to4", b].act + 4)
                        sp.dma_start(rows128(row4, b), kview(r4_buf[b % 2])).then_inc(r4_out[b % 2], 16)
                    masks_in(1)
                    for b in range(NB):
                        sp.wait_ge(g4[b % 2], 16 * C * KB * (uses(b) + 1))
                        sp.dma_start(rows128(row4d, b), kview(g4_buf[b % 2])).then_inc(d4[b % 2], 16)
                    for i in range(2):
                        sp.wait_ge(d4[i], 16 * uses(NB + 1 - i))
            for l in range(2):
                sp.wait_ge(st_n[l], 16 * total[l][4])
            sp.sem_inc(dense_out, 1)
            for s in range(2):
                for b in range(NB):
                    l, n, put = b % 2, before["last_in", s, b], puts(s, b)
                    lane_done(l, n)
                    if put:
                        sp.wait_ge(fin[l], 16 * C * KB * put)
                    r = row4d.rearrange("(b k p c) w -> b k p c w", b=NB, k=KB, p=P, c=C)[b]
                    for k in range(KB):
                        sp.dma_start(RI[l][:, k * P:(k + 1) * P].rearrange("p (c f) -> p c f", c=C),
                                     r[k][:, :, F * s:F * s + F]).then_inc(last_in[l], 16)
            for l in range(2):
                sp.wait_ge(fin[l], 16 * C * KB * 2 * uses(NB + 1 - l))

        @block.gpsimd
        def _(pool):
            done = [0]

            def const(i):
                done[0] += 1
                i.then_inc(consts, 1)
                pool.wait_ge(consts, done[0])

            def bands(t, c, value):
                q = slice(F * c, F * c + F)
                const(nc.gpsimd.memset(t[q, q], value))

            for i, (t, value) in enumerate(((ident, 0.0), (ltri, 1.0), (mean, 0.0))):
                nc.gpsimd.memset(t[:, :], value).then_inc(pool_ok, 1)
                pool.wait_ge(pool_ok, i + 1)
            const(nc.gpsimd.affine_select(out=ident[:, :], in_=ident[:, :], compare_op=ALU.not_equal, fill=1.0,
                                          base=0, pattern=[[-1, P]], channel_multiplier=1))
            const(nc.gpsimd.affine_select(out=ltri[:, :], in_=ltri[:, :], compare_op=ALU.is_gt, fill=0.0,
                                          base=0, pattern=[[1, P]], channel_multiplier=-1))
            for c in range(C):
                bands(mean, c, 1.0 / F)
            const(nc.gpsimd.iota(index2[:, 0:SC], pattern=[[1, SC]], base=0, channel_multiplier=SC))
            const(nc.gpsimd.iota(index2[:, SC:2 * SC], pattern=[[1, SC]], base=HALF, channel_multiplier=SC))
            const(nc.gpsimd.iota(hI[1][:, :], pattern=[[P, C * NT]], base=1, channel_multiplier=1))
            const(nc.gpsimd.iota(aI[1][:, :], pattern=[[1, C * NT]], base=0, channel_multiplier=ER))
            const(nc.gpsimd.iota(aI[0][:, 0:4], pattern=[[1, 4]], base=ER - 4, channel_multiplier=ER))
            const(nc.gpsimd.memset(cols[:, :], 0.0))
            assert done[0] == N_CONST

            def gather(o, t, index, m, signal):
                nc.gpsimd.indirect_dma_start(
                    out=o, out_offset=None, in_=t, in_offset=bass.IndirectOffsetOnAxis(ap=index[:, m:m + 1], axis=0),
                    bounds_check=t.shape[0] - 1, oob_is_err=False).then_inc(signal, 16)

            def scatter(t, index, m, i, signal):
                nc.gpsimd.indirect_dma_start(
                    out=t, out_offset=bass.IndirectOffsetOnAxis(ap=index[:, m:m + 1], axis=0), in_=i, in_offset=None,
                    bounds_check=t.shape[0] - 1, oob_is_err=False).then_inc(signal, 16)

            def tiles(b):
                return [(k * C + c, c * NT + b * KB + k) for k in range(KB) for c in range(C)]

            pool.wait_ge(attn_out, 16)
            pool.wait_ge(idx_rdy, 1)
            for b in range(NB):
                if b >= 2:
                    pool.wait_ge(atts_out[b % 2], 16 * uses(b))
                    pool.wait_ge(dcol, b - 1)
                for i, m in tiles(b):
                    gather(att_buf[b % 2][:, i * ATT:(i + 1) * ATT], attN, eI, m, ga[b % 2])
            for b in range(NB):
                for i, m in tiles(b):
                    gather(D[:, b * W + i * F:b * W + (i + 1) * F], x, sG, m, gx[0])
            pool.wait_ge(dcol, NB + 1)
            for b in range(NB):
                for i, m in tiles(b):
                    gather(T2[:, b * W + i * F:b * W + (i + 1) * F], x, dG, m, gx[1])

            def updates(L):
                pool.wait_ge(table_out, L + 1)
                j = 0 if L < 3 else 1
                nb = C * NT // BG
                if L in (0, 3):
                    pool.wait_ge(idx_rdy, 3 + j)
                for i in range(nb + 1):
                    if i < nb:
                        k = L * nb + i
                        q = k % 2
                        if k >= 2:
                            pool.wait_ge(ss[q], 16 * BG * (k // 2))
                        for m in range(BG):
                            gather(G[q][:, m * F:(m + 1) * F], table, aI[j], i * BG + m, gs[q])
                    if i >= 1:
                        k = L * nb + i - 1
                        q = k % 2
                        pool.wait_ge(gs[q], 16 * BG * (k // 2 + 1))
                        for m in range(BG):
                            scatter(upd[j], hI[j], (i - 1) * BG + m, G[q][:, m * F:(m + 1) * F], ss[q])
                last = (L + 1) * nb
                for q in range(2):
                    pool.wait_ge(ss[q], 16 * BG * ((last + 1 - q) // 2))
                pool.sem_inc(upd_n, 1)

            for L in range(NL - 1):
                updates(L)
                if L == 2:
                    for b in range(2):
                        pool.wait_ge(r4_out[b], 16 * uses(NB + 1 - b))
                    for b in range(NB):
                        if b >= 2:
                            pool.wait_ge(act_n[b % 2], before["from4", b - 2].act + 3)
                            pool.wait_ge(sux, b - 1)
                            pool.wait_ge(d4[b % 2], 16 * uses(b))
                        for i, m in tiles(b):
                            gather(g4_buf[b % 2][:, i * ROW4:(i + 1) * ROW4], row4, jI, m, g4[b % 2])
            pool.wait_ge(dense_out, 1)
            for s, index in ((0, sUI), (1, dUI)):
                if s:
                    for l in range(2):
                        pool.wait_ge(fin[l], 16 * C * KB * uses(NB + 1 - l))
                for b in range(NB):
                    pool.wait_ge(act_n[b % 2], before["last_out", s, b].act + 1)
                    for i, m in tiles(b):
                        scatter(out, index, m, RI[b % 2][:, i * F:(i + 1) * F], fin[b % 2])

        @block.scalar
        def _(act):
            def one(i, l):
                i.then_inc(act_n[l], 1)

            def wait_pe(l, v):
                act.wait_ge(pe_n[l], v)

            def copy(l, o, i):
                one(nc.scalar.activation(o, i, ACT.Copy), l)

            def act_rows_in(l, n, o):
                wait_pe(l, n.pe + 1)
                copy(l, o, ps[l][0][:, 0:W])

            def act_rows_out(l, n, free=None):
                wait_pe(l, n.pe + 1)
                if n.store:
                    act.wait_ge(st_n[l], 16 * n.store)
                copy(l, RI[l][:, :], ps[l][1][:, 0:W])

            def act_ln(l, n, shift):
                wait_pe(l, n.pe + 1)
                one(nc.scalar.activation(HB[l][:, :], ps[l][0][:, 0:W], ACT.Square, bias=shift), l)
                wait_pe(l, n.pe + 2)
                one(nc.scalar.activation(HB[l][:, :], ps[l][1][:, 0:W], ACT.Ln, bias=eps_c), l)
                act.wait_ge(act_n[l], n.act + 2)
                one(nc.scalar.activation(HB[l][:, :], HB[l][:, :], ACT.Exp, scale=-0.5), l)

            def act_relu(l, v, o, u, bias):
                wait_pe(l, v)
                one(nc.scalar.activation(o, ps[l][u][:, 0:W], ACT.Relu, bias=bias), l)

            act.wait_ge(nat_in, 16 * 4)
            rows = nat_att.rearrange("p (r w) -> p r w", w=ATT)
            nc.scalar.activation(rows[:, :, 0:16], nat16.rearrange("p (r w) -> p r w", w=16), ACT.Copy).then_inc(nat_rows, 1)
            nc.scalar.activation(rows[:, :, 16:48], nat32.rearrange("p (r w) -> p r w", w=32), ACT.Copy).then_inc(nat_rows, 1)
            nc.scalar.activation(rows[:, :, 48], nat_w, ACT.Copy).then_inc(nat_rows, 1)
            nc.scalar.activation(rows[:, :, 49], nat_dst, ACT.Copy).then_inc(nat_rows, 1)
            act.wait_ge(ready, 1)
            for s, o in ((0, S), (1, D)):
                for b in range(NB):
                    act_rows_in(b % 2, before["turn", s, b], blk(o, b))
            for L in range(NL):
                if L == 1:
                    for b in range(NB):
                        l, n = b % 2, before["score", b]
                        wait_pe(l, n.pe + 1)
                        one(nc.scalar.activation(AB[l][:, :], ps[l][0][:, 0:W], ACT.Identity, bias=fcb_c), l)
                    for b in range(NB):
                        act.wait_ge(e_rdy, b + 1)
                        nc.scalar.activation(blk(T1, b), blk(T1, b), ACT.Exp).then_inc(e_exp, 1)
                for b in range(NB):
                    l, n = b % 2, before["msg", L, b]
                    def lane_free():
                        if n.pe:
                            wait_pe(l, n.pe)
                        if n.dve:
                            act.wait_ge(dve_n[l], n.dve)
                    if L == 0:
                        lane_free()
                        act.wait_ge(ra_in, 16 * (b + 1))
                        copy(l, HB[l][:, 0:KB * 64].rearrange("p (m w) -> p m w", w=16),
                             RA[:, :].rearrange("p (m w) -> p m w", w=ATT)[:, :, 0:16])
                        wait_pe(l, n.pe + 1)
                        copy(l, AB[l][0:64, :], ps[l][0][0:64, 0:W])
                        act_relu(l, n.pe + 2, HB[l][:, :], 1, b1a_c)
                        act_relu(l, n.pe + 3, X3[l][:, :], 0, b1a_c)
                    elif L == 2:
                        lane_free()
                        act.wait_ge(ra_in, 16 * (NB + b + 1))
                        copy(l, HB[l][:, :].rearrange("p (m f) -> p m f", f=F),
                             RA[:, :].rearrange("p (m w) -> p m w", w=ATT)[:, :, 48:49].to_broadcast([P, KB * C, F]))
                    elif L >= 3:
                        act.wait_ge(dve_n[l], n.dve + 1)
                        one(nc.scalar.activation(blk(T1, b), blk(T1, b), ACT.Relu), l)
                if L < NL - 1:
                    for b in range(NB):
                        act_rows_out(b % 2, before["table", L, b])
                for i0 in range(*DENSE[L], 2):
                    for n in range(7):
                        for i in (i0, i0 + 1):
                            l, c = i % 2, before["dense", i, n]
                            if n == 0:
                                act_rows_in(l, c, AB[l][:, :])
                            elif n in (1, 2, 3, 5):
                                act_ln(l, c, cb_c if n == 2 else zero_c)
                            elif n == 4:
                                act_relu(l, c.pe + 1, HB[l][:, :], 0, bg_c[:, 2 * (n - 4):2 * (n - 4) + 1])
                            else:
                                act_rows_out(l, c)
                shift = cb_c if L == 1 else zero_c
                b1 = bg_c[:, 2 * (L - 3):2 * (L - 3) + 1] if L >= 3 else None
                for b in range(NB):
                    l, n = b % 2, before["local", L, b]
                    act_ln(l, n, shift) if L < 3 else act_relu(l, n.pe + 1, HB[l][:, :], 0, b1)
                for b in range(NB):
                    l, n = b % 2, before["other", L, b]
                    if L < NL - 1:
                        act_rows_in(l, before["update", L, b], AB[l][:, :])
                    act_ln(l, n, shift) if L < 3 else act_relu(l, n.pe + 1, HB[l][:, :], 0, b1)
                if L == 2:
                    for b in range(NB):
                        l, n = b % 2, before["to4", b]
                        o = r4_buf[l].rearrange("p (m w) -> p m w", w=ROW4)
                        if b >= 2:
                            act.wait_ge(r4_out[l], 16 * uses(b))
                        for u in range(2):
                            wait_pe(l, n.pe + u + 1)
                            copy(l, o[:, :, u * F:(u + 1) * F], ps[l][u][:, 0:W].rearrange("p (m f) -> p m f", f=F))
                        act.wait_ge(ra_in, 16 * (2 * NB + b + 1))
                        copy(l, o[:, :, 2 * F:3 * F], RA[:, :].rearrange("p (m w) -> p m w", w=ATT)[:, :, 16:16 + F])
                        copy(l, o[:, :, 3 * F].rearrange("p (k c) -> p k c", c=C),
                             sU[:, :].rearrange("p (c k) -> p k c", c=C)[:, b * KB:(b + 1) * KB, :])
                    for b in range(NB):
                        l, n = b % 2, before["from4", b]
                        wait_pe(l, n.pe)
                        act.wait_ge(g4[l], 16 * C * KB * (uses(b) + 1))
                        for v, o in enumerate((HB[l], X3[l], RI[l])):
                            copy(l, o[:, :].rearrange("p (m f) -> p m f", f=F),
                                 g4_buf[l].rearrange("p (m w) -> p m w", w=ROW4)[:, :, v * F:(v + 1) * F])
                        for v, o in enumerate((S, D, EA)):
                            wait_pe(l, n.pe + v + 1)
                            copy(l, blk(o, b), ps[l][v % 2][:, 0:W])
            for s in range(2):
                for b in range(NB):
                    l = b % 2
                    act_rows_in(l, before["last_in", s, b], AB[l][:, :])
                    act_ln(l, before["last_ln", s, b], zero_c)
                    n = before["last_out", s, b]
                    wait_pe(l, n.pe + 1)
                    copy(l, RI[l][:, :], ps[l][1][:, 0:W])

        @block.tensor
        def _(pe):
            def mm(o, w, i, start=True, stop=True):
                for a, e in ((0, 512), (512, W)):
                    r = nc.tensor.matmul(o[:, a:e], w, i[:, a:e], start=start, stop=stop)
                return r

            def begin(l, n):
                if n.act:
                    pe.wait_ge(act_n[l], n.act)
                if n.dve:
                    pe.wait_ge(dve_n[l], n.dve)

            def turn_tiles(l, u, tile, rows=P):
                for k in range(KB):
                    r = nc.tensor.transpose(ps[l][u][0:rows, k * P:(k + 1) * P], tile(k), ident[:, :])
                r.then_inc(pe_n[l], 1)

            def pe_rows_in(l, n):
                begin(l, n)
                pe.wait_ge(ld_n[l], 16 * (n.load + 1))
                turn_tiles(l, 0, lambda k: RI[l][:, k * P:(k + 1) * P])

            def pe_rows_out(l, n, t):
                begin(l, n)
                turn_tiles(l, 1, lambda k: t[:, k * P:(k + 1) * P])

            def pe_ln(l, n, t, a=None, wa=None):
                begin(l, n)
                r = mm(ps[l][0], center[:, :], t, stop=a is None)
                if a is not None:
                    r = mm(ps[l][0], wa, a, start=False)
                r.then_inc(pe_n[l], 1)
                pe.wait_ge(act_n[l], n.act + 1)
                mm(ps[l][1], mean[:, :], HB[l][:, :]).then_inc(pe_n[l], 1)

            def pe_mlp(l, n, g, t, a=None):
                begin(l, n)
                r = mm(ps[l][0], wX[:, g, :], t, stop=a is None)
                if a is not None:
                    r = mm(ps[l][0], wG[:, 2 * g, :], a, start=False)
                r.then_inc(pe_n[l], 1)
                pe.wait_ge(act_n[l], n.act + 1)
                mm(ps[l][1], wG[:, 2 * g + 1, :], HB[l][:, :]).then_inc(pe_n[l], 1)

            turns = [0]

            def net_turn(t, w):
                turns[0] += 1
                pe.wait_ge(turn_rdy, turns[0])
                for a in range(0, w, P):
                    r = nc.tensor.transpose(pi[:, a:a + P], t[:, a:a + P], ident[:, :])
                r.then_inc(turned, 1)

            def net_sort(h, top):
                cur, other = va, vb
                for k in range(1, top + 1):
                    if k == 16:
                        cur, other = other, cur
                    n1 = min(k, 15) - 8
                    if k > 8:
                        net_turn(cur, h * SC)
                        cur, other = (other, cur) if n1 % 2 == 0 else (cur, other)
                        net_turn(cur, h * SC)
                        cur, other = other, cur
                    elif k % 2:
                        cur, other = other, cur
                return cur

            small = [0]

            def small_wait():
                small[0] += 1
                pe.wait_ge(small_rdy, small[0])

            def index_tiles(arrays):
                small_wait()
                for o, t in enumerate(arrays):
                    for g in range(2):
                        r = nc.tensor.transpose(pi[:, 256 * o + 98 * g:256 * o + 98 * g + 98],
                                                t[0:98, g * P:(g + 1) * P], ident[0:98, 0:98])
                r.then_inc(small_mm, 1)

            def net_join():
                net_turn(va, SC)
                net_turn(va, SC)
                net_turn(va, 2 * SC)
                net_turn(va, 2 * SC)
                small_wait()
                nc.tensor.matmul(pi[:, 0:2], ltri[:, :], rs_c, start=True, stop=True)
                nc.tensor.matmul(pi[:, 2:3], shf[:, :], rs_c[:, 0:1], start=True, stop=True)
                for h in range(2):
                    r = nc.tensor.matmul(pi[0:1, 256 + h * P:256 + (h + 1) * P], rm_c[:, h:h + 1], ident[:, :], start=True, stop=True)
                r.then_inc(small_mm, 1)
                small_wait()
                for h in range(2):
                    r = nc.tensor.matmul(pi[:, 512 + h:513 + h], rowb[0:1, h * P:(h + 1) * P], ident[0:1, 0:1], start=True, stop=True)
                r.then_inc(small_mm, 1)

            pe.wait_ge(consts, N_CONST)
            net_sort(1, 15)
            index_tiles((t0, t1, t2))
            net_sort(1, 15)
            index_tiles((t0, t1, t2))
            net_join()
            net_sort(2, 16)
            index_tiles((t0, t2))
            pe.wait_ge(ready, 1)
            pe.wait_ge(idx_rdy, 3)
            nc.tensor.matmul(pi[:, 0:P], wZ[:, 0, :], center[:, :], start=True, stop=True)
            nc.tensor.matmul(pi[:, P:P + 1], center[:, :], batt_c, start=True, stop=True).then_inc(wz_mm, 1)
            pe.wait_ge(ready, 2)

            for s, rows in ((0, D), (1, T2)):
                pe.wait_ge(gx[s], 16 * C * NT)
                for b in range(NB):
                    begin(b % 2, before["turn", s, b])
                    turn_tiles(b % 2, 0, lambda k: rows[:, b * W + k * P:b * W + (k + 1) * P])

            shifts = [0]

            def carries(w):
                for i in range(C - 1):
                    if shifts[0]:
                        pe.wait_ge(cr_used, shifts[0])
                    shifts[0] += 1
                    pe.wait_ge(cr_rdy, shifts[0])
                    nc.tensor.matmul(pc[:, 0:1], w[:, :], ctmp, start=True, stop=True).then_inc(cr_mm, 1)
                pe.wait_ge(cr_used, shifts[0])

            for L in range(NL):
                fb, bb = (T2, T1) if L == 1 else (T1, T2)
                local, other = (S, D) if L < 3 else (D, S)
                if L == 1:
                    for b in range(NB):
                        l = b % 2
                        begin(l, before["score", b])
                        mm(ps[l][0], wSc[:, 0, :], blk(S, b), stop=False)
                        mm(ps[l][0], wSc[:, 1, :], blk(D, b), start=False).then_inc(pe_n[l], 1)
                    begin(1, before["msg", L, 1])
                    for w in (shf, shb, shf, shb):
                        carries(w)
                for b in range(NB):
                    l, n = b % 2, before["msg", L, b]
                    if L == 0:
                        begin(l, n)
                        pe.wait_ge(act_n[l], n.act + 1)
                        turn_tiles(l, 0, lambda k: HB[l][:, k * 64:(k + 1) * 64], 64)
                        for g in range(2):
                            o = ps[l][1 - g]
                            pe.wait_ge(act_n[l], n.act + 2)
                            mm(o, wA[:, g, :], blk(D, b), stop=False)
                            mm(o, wE[:, g, :], AB[l][0:64, :], start=False).then_inc(pe_n[l], 1)
                        pe.wait_ge(act_n[l], n.act + 4)
                        mm(ps[l][1], wB[:, 0, :], HB[l][:, :], stop=False)
                        mm(ps[l][1], wB[:, 1, :], X3[l][:, :], start=False).then_inc(pe_n[l], 1)
                    elif L == 1:
                        begin(l, n)
                        pe.wait_ge(att_rdy, b + 1)
                        for h in range(4):
                            if h:
                                pe.wait_ge(dve_n[l], n.dve + h)
                            mm(ps[l][0], wSel[:, h, :], blk(T1, b)).then_inc(pe_n[l], 1)
                            pe.wait_ge(dve_n[l], n.dve + h + 1)
                            mm(ps[l][1], wH[:, h, :], HB[l][:, :], start=(h == 0), stop=(h == 3)).then_inc(pe_n[l], 1)
                    elif L == 2:
                        begin(l, n)
                        pe.wait_ge(act_n[l], n.act + 1)
                        turn_tiles(l, 0, lambda k: HB[l][:, k * P:(k + 1) * P])
                begin(1, before["sums", L])
                carries(shf)
                if L < NL - 1:
                    for b in range(NB):
                        pe.wait_ge(fix_n, L * NB + b + 1)
                        pe_rows_out(b % 2, before["table", L, b], blk(fb, b))
                begin(1, before["back", L])
                carries(shb)
                for i0 in range(*DENSE[L], 2):
                    for n in range(7):
                        for i in (i0, i0 + 1):
                            l, c = i % 2, before["dense", i, n]
                            if n == 0:
                                pe_rows_in(l, c)
                            elif n in (1, 2, 3):
                                pe_ln(l, c, AB[l][:, :])
                            elif n == 5:
                                pe_ln(l, c, AB[l][:, :], X3[l][:, :], center[:, :])
                            elif n == 4:
                                pe_mlp(l, c, n - 4, X3[l][:, :] if n == 4 else AB[l][:, :])
                            else:
                                pe_rows_out(l, c, AB[l][:, :])
                wa = wZ[:, 1, :] if L == 2 else center[:, :]
                for b in range(NB):
                    l, n = b % 2, before["local", L, b]
                    pe.wait_ge(tot_n, L * NB + b + 1)
                    if L < 3:
                        pe_ln(l, n, blk(local, b), blk(bb, b), wa)
                    else:
                        pe_mlp(l, n, L - 3, blk(local, b), blk(bb, b))
                for b in range(NB):
                    l, n = b % 2, before["other", L, b]
                    a = None
                    if L < NL - 1:
                        pe_rows_in(l, before["update", L, b])
                        a = AB[l][:, :]
                    if L < 3:
                        pe_ln(l, n, blk(other, b), a, wa)
                    else:
                        pe_mlp(l, n, L - 3, blk(other, b), a)
                if L == 2:
                    for b in range(NB):
                        l = b % 2
                        begin(l, before["to4", b])
                        for u, t in enumerate((S, D)):
                            turn_tiles(l, u, lambda k: t[:, b * W + k * P:b * W + (k + 1) * P])
                    for b in range(NB):
                        l, n = b % 2, before["from4", b]
                        begin(l, n)
                        pe.wait_ge(act_n[l], n.act + 3)
                        for v, t in enumerate((HB[l], X3[l], RI[l])):
                            if v == 2:
                                pe.wait_ge(act_n[l], n.act + 4)
                            turn_tiles(l, v % 2, lambda k: t[:, k * P:(k + 1) * P])
            for s, t in ((0, S), (1, D)):
                for b in range(NB):
                    l, n = b % 2, before["last_in", s, b]
                    begin(l, n)
                    pe.wait_ge(last_in[l], 16 * KB * (puts(s, b) + 1))
                    turn_tiles(l, 0, lambda k: RI[l][:, k * P:(k + 1) * P])
                    pe_ln(l, before["last_ln", s, b], blk(t, b), AB[l][:, :], center[:, :])
                    pe_rows_out(l, before["last_out", s, b], blk(t, b))

        @block.vector
        def _(dve):
            v = nc.vector
            chain = [0]

            def link(i):
                chain[0] += 1
                i.then_inc(dchain, 1)
                dve.wait_ge(dchain, chain[0])

            for t in (wA, wE, wB, wH, wSc, wZ, wG):
                v.memset(t[:, :, :], 0.0)
            link(v.memset(RI[0][:, :], 0.0))
            dve.sem_inc(w_zero, 1)
            dve.wait_ge(consts, N_CONST)
            dve.wait_ge(w_in, 16 * NW)
            v.memset(eps_c, EPS)
            v.tensor_tensor(center[:, :], ident[:, :], mean[:, :], ALU.subtract)
            v.memset(shf[:, :], 1.0)
            for h in range(4):
                for c in range(C):
                    q = slice(F * c, F * c + F)
                    v.tensor_scalar(wH[q, h, q], wat[q, F * h:F * h + F], 0.25, None, ALU.mult)
                link(v.tensor_copy(wSel[:, h, :].rearrange("p (c f) -> p c f", f=F),
                                   ident[:, :].rearrange("p (c f) -> p c f", f=F)[:, :, h:h + 1].to_broadcast([P, C, F])))
            for s in range(2):
                link(v.tensor_tensor(wtmp[:, :].rearrange("p (h o) -> p h o", h=4), wat[:, :].rearrange("p (h o) -> p h o", h=4),
                                     fcr[:, s * F:(s + 1) * F].rearrange("p (h o) -> p h o", h=1).to_broadcast([P, 4, F]), ALU.mult))
                link(v.tensor_reduce(t0[:, 0:4], wtmp[:, :].rearrange("p (h o) -> p h o", h=4), AXX, ALU.add))
                for c in range(C):
                    q = slice(F * c, F * c + F)
                    link(v.tensor_copy(wSc[q, s, F * c:F * c + 4], t0[q, 0:4]))
            link(v.tensor_scalar(eps_g, eps_g, 1.0, None, ALU.add))
            for g in range(GINE):
                link(v.tensor_scalar(wX[:, g, :], wG[:, 2 * g, :], eps_g[:, g:g + 1], None, ALU.mult))
            link(v.memset(shb[:, :], 0.0))
            link(v.tensor_copy(shb[:, 0:P - F], ident[:, F:P]))
            dve.sem_inc(ready, 1)

            link(v.tensor_scalar(gray, index2, 1, None, ALU.logical_shift_right))
            link(v.tensor_tensor(gray, gray, index2, ALU.bitwise_xor))
            for k in range(1, 17):
                i, s = (index2, 1) if k == 1 else (gray, k - 1)
                link(v.tensor_scalar(t0.bitcast(I32), i, s, 1, ALU.logical_shift_right, ALU.bitwise_and))
                link(v.tensor_scalar(flips[:, k - 1, :], t0.bitcast(I32), -2.0, 1.0, ALU.mult, ALU.add))
            link(v.tensor_scalar(iop, index2[:, 0:SC], 1.0, None, ALU.add))

            def pack(field, low, o):
                link(v.tensor_copy(o.bitcast(I32), field))
                link(v.tensor_copy(low.bitcast(I32), low))
                link(v.tensor_scalar(o.bitcast(I32), o.bitcast(I32), 15, None, ALU.logical_shift_left))
                link(v.tensor_tensor(o.bitcast(I32), o.bitcast(I32), low.bitcast(I32), ALU.bitwise_or))

            def encode(key, pay, o, a, b):
                link(v.tensor_scalar(a, key, SPLIT, None, ALU.is_lt))
                link(v.tensor_scalar(b, key, -2.0, 181559.0, ALU.mult, ALU.add))
                link(v.tensor_tensor(b, b, a, ALU.mult))
                link(v.scalar_tensor_tensor(out=key, in0=key, scalar=-50744.0, in1=b, op0=ALU.add, op1=ALU.add))
                link(v.tensor_scalar(b, pay, -2.0, 32767.0, ALU.mult, ALU.add))
                link(v.tensor_tensor(b, b, a, ALU.mult))
                link(v.tensor_tensor(pay, pay, b, ALU.add))
                pack(key, pay, o)

            def field_of(bits, o):
                link(v.tensor_scalar(o.bitcast(I32), bits.bitcast(I32), 15, None, ALU.logical_shift_right))
                link(v.tensor_copy(o, o.bitcast(I32)))

            def decode(bits, field, low, a, b):
                field_of(bits, field)
                link(v.tensor_scalar(low.bitcast(I32), bits.bitcast(I32), 32767, None, ALU.bitwise_and))
                link(v.tensor_copy(low, low.bitcast(I32)))
                link(v.tensor_scalar(a, field, 65536.0, None, ALU.is_ge))
                link(v.tensor_scalar(b, low, -2.0, 32767.0, ALU.mult, ALU.add))
                link(v.tensor_tensor(b, b, a, ALU.mult))
                link(v.tensor_tensor(low, low, b, ALU.add))
                link(v.tensor_scalar(b, field, -2.0, 80071.0, ALU.mult, ALU.add))
                link(v.tensor_tensor(b, b, a, ALU.mult))
                link(v.scalar_tensor_tensor(out=field, in0=field, scalar=50744.0, in1=b, op0=ALU.add, op1=ALU.add))

            def to_row(pos, o, a):
                link(v.tensor_scalar(o, pos, 4.0, None, ALU.mult))
                for c in range(1, C):
                    link(v.tensor_scalar(a, pos, float(c * J), float(C * J - 1), ALU.is_ge, ALU.mult))
                    link(v.tensor_tensor(o, o, a, ALU.subtract))

            turns = [0]

            def net_turn(cur, o, w):
                turns[0] += 1
                dve.sem_inc(turn_rdy, 1)
                dve.wait_ge(turned, turns[0])
                link(v.tensor_copy(o[:, 0:w], pi[:, 0:w]))

            def compare(i, o, w, s):
                a = i[:, 0:w].rearrange("p (g two s) -> p g two s", two=2, s=s)
                b = o[:, 0:w].rearrange("p (g two s) -> p g two s", two=2, s=s)
                v.tensor_tensor(b[:, :, 0, :], a[:, :, 0, :], a[:, :, 1, :], ALU.min)
                link(v.tensor_tensor(b[:, :, 1, :], a[:, :, 0, :], a[:, :, 1, :], ALU.max))

            def merge_bits(cur, o, w, nbits):
                net_turn(cur, o, w)
                cur, o = o, cur
                for s in reversed(range(nbits)):
                    compare(cur, o, w, 2 ** s)
                    cur, o = o, cur
                net_turn(cur, o, w)
                cur, o = o, cur
                for s in reversed(range(8)):
                    compare(cur, o, w, 2 ** s)
                    cur, o = o, cur
                return cur, o

            def net_sort(h, top):
                w = h * SC
                cur, o = va, vb
                for k in range(1, top + 1):
                    link(v.tensor_tensor(cur[:, 0:w], cur[:, 0:w], flips[:, k - 1, 0:w], ALU.mult))
                    if k == 16:
                        v.tensor_tensor(o[:, 0:SC], cur[:, 0:SC], cur[:, SC:w], ALU.min)
                        link(v.tensor_tensor(o[:, SC:w], cur[:, 0:SC], cur[:, SC:w], ALU.max))
                        cur, o = o, cur
                    if k > 8:
                        cur, o = merge_bits(cur, o, w, min(k, 15) - 8)
                    else:
                        for s in reversed(range(k)):
                            compare(cur, o, w, 2 ** s)
                            cur, o = o, cur
                return cur

            small = [0]

            def small_mms():
                small[0] += 1
                dve.sem_inc(small_rdy, 1)
                dve.wait_ge(small_mm, small[0])

            dve.wait_ge(src_in, 16)
            key, pay = t0[:, 0:SC], t1[:, 0:SC]
            link(v.memset(key, PAD))
            link(v.tensor_scalar(key[0:EP, 0:ER], nat_src, 1000.0, None, ALU.add))
            link(v.memset(pay, 0.0))
            link(v.tensor_copy(pay[:, 0:C * NT], aI[1][:, :]))
            link(v.tensor_copy(pay[:, ER - 4:ER], aI[0][:, 0:4]))
            encode(key, pay, va[:, 0:SC], t2[:, 0:SC], t3[:, 0:SC])
            r = net_sort(1, 15)
            link(v.tensor_copy(srt[0], r[:, 0:SC]))
            dve.sem_inc(srt_rdy, 1)

            def after_sort(i, loads):
                dve.wait_ge(nb_in, 16 * loads)
                cur, prv, nxt = va[:, 0:196], va[:, 256:452], vb[:, 0:196]
                field_of(t2[:, 256:452], cur)
                field_of(t2[:, 0:196], prv)
                field_of(t3[:, 0:196], nxt)
                link(v.tensor_tensor(mask8[:, 0, :], cur, prv, ALU.is_equal))
                link(v.tensor_tensor(mask8[:, 1, :], cur, nxt, ALU.is_equal))
                dve.sem_inc(mask_rdy, 1)
                k, low, a, b = va[0:98, 0:SC], va[0:98, SC:2 * SC], vb[0:98, 0:SC], vb[0:98, SC:2 * SC]
                end = t3[0:98, 0:SC]
                field_of(t0[0:98, 0:SC], k)
                field_of(t1[0:98, 0:SC], a)
                link(v.tensor_tensor(end, k, a, ALU.not_equal))
                decode(t0[0:98, 0:SC], k, low, a, b)
                key, uniq, p_ = t0[0:98, 0:SC], t1[0:98, 0:SC], t2[0:98, 0:SC]
                link(v.tensor_scalar(key, k, -1000.0, None, ALU.add))
                link(v.tensor_scalar(uniq, key, -500000.0, None, ALU.add))
                link(v.tensor_tensor(uniq, uniq, end, ALU.mult))
                link(v.tensor_scalar(uniq, uniq, 500000.0, None, ALU.add))
                link(v.tensor_scalar(key, key, float(NODES - 1), None, ALU.min))
                if i == 0:
                    link(v.tensor_scalar(p_, low, float(EDGES - 1), None, ALU.min))
                else:
                    link(v.tensor_scalar(low, low, -1.0, 0.0, ALU.add, ALU.max))
                    to_row(low, p_, a)
                small_mms()

            after_sort(0, 5)
            v.tensor_copy(sG[:, :], pi[:, 0:196])
            v.tensor_copy(sU[:, :], pi[:, 256:452])
            link(v.tensor_copy(eI[:, :], pi[:, 512:708]))
            dve.sem_inc(idx_rdy, 1)

            def read_masks(i):
                dve.wait_ge(mask_in, 16 * 2 * C * (i + 1))
                link(v.memset(NE[P - F:P, J - 1:J], 0.0))
                v.tensor_tensor_scan(PF[:, :], NS[:, :], NS[:, :], 1.0, ALU.mult, ALU.min)
                link(v.tensor_tensor_scan(QB[:, ::-1], NE[:, ::-1], NE[:, ::-1], 1.0, ALU.mult, ALU.min))

            read_masks(0)

            dstf = hI[0][:, :].bitcast(F32)
            for b in range(NB):
                dve.wait_ge(ga[b % 2], 16 * C * KB * (uses(b) + 1))
                v.tensor_copy(dstf.rearrange("p (c k) -> p k c", c=C)[:, b * KB:(b + 1) * KB, :],
                              att_buf[b % 2].rearrange("p (k c w) -> p k c w", k=KB, c=C)[:, :, :, ATT - 1]).then_inc(dcol, 1)
            dve.wait_ge(dcol, NB)
            v.tensor_copy(dG[:, :], dstf).then_inc(dcol, 1)
            dve.wait_ge(dcol, NB + 1)

            link(v.memset(key, PAD))
            link(v.tensor_scalar(key[:, 0:C * NT], dstf, 1000.0, None, ALU.add))
            last = key[:, C * NT - 1:C * NT]
            link(v.tensor_scalar(p40, hI[1][:, C * NT - 1:C * NT], float(EDGES), None, ALU.is_gt))
            link(v.tensor_scalar(ctmp, last, -1.0, PAD, ALU.mult, ALU.add))
            link(v.tensor_tensor(ctmp, ctmp, p40, ALU.mult))
            link(v.tensor_tensor(last, last, ctmp, ALU.add))
            link(v.memset(pay, 0.0))
            link(v.tensor_copy(pay[:, 0:C * NT], hI[1][:, :]))
            encode(key, pay, va[:, 0:SC], t2[:, 0:SC], t3[:, 0:SC])
            r = net_sort(1, 15)
            link(v.tensor_copy(srt[1], r[:, 0:SC]))
            dve.sem_inc(srt_rdy, 1)
            after_sort(1, 10)
            v.tensor_copy(dUI[:, :], pi[:, 256:452])
            link(v.tensor_copy(jI[:, :], pi[:, 512:708]))
            dve.sem_inc(idx_rdy, 1)

            def net_join(tab, query, i, loads):
                x0 = t0[:, 0:SC]
                link(v.tensor_scalar(t1[:, 0:SC].bitcast(I32), tab.bitcast(I32), 31, 32767, ALU.arith_shift_right, ALU.bitwise_and))
                link(v.tensor_scalar(x0.bitcast(I32), tab.bitcast(I32), 15, None, ALU.logical_shift_right))
                link(v.tensor_scalar(x0.bitcast(I32), x0.bitcast(I32), 15, None, ALU.logical_shift_left))
                link(v.tensor_tensor(x0.bitcast(I32), x0.bitcast(I32), t1[:, 0:SC].bitcast(I32), ALU.bitwise_or))
                link(v.tensor_copy(va[:, 0:SC], query[:, ::-1]))
                net_turn(va, vb, SC)
                link(v.tensor_copy(va[:, 0:P], vb[:, 0:P][:, ::-1]))
                link(v.tensor_copy(va[:, P:SC], vb[:, P:SC][:, ::-1]))
                net_turn(va, vb, SC)
                v.tensor_tensor(va[:, 0:SC], x0, vb[:, 0:SC], ALU.min)
                link(v.tensor_tensor(va[:, SC:2 * SC], x0, vb[:, 0:SC], ALU.max))
                cur, o = merge_bits(va, vb, 2 * SC, 7)
                k, low = t0, t1
                decode(cur, k, low, o, t3)
                link(v.tensor_scalar(t2, low, 0.0, None, ALU.is_equal))
                link(v.tensor_scalar(cur, k, 1.0, None, ALU.add))
                link(v.tensor_tensor(cur, cur, t2, ALU.mult))
                link(v.tensor_scalar(cur, cur, -1.0, None, ALU.add))
                for h in range(2):
                    q = slice(h * SC, (h + 1) * SC)
                    link(v.tensor_tensor_scan(o[:, q], t2[:, q], t2[:, q], 0.0, ALU.add, ALU.max))
                    link(v.tensor_tensor_scan(t3[:, q], cur[:, q], cur[:, q], -1.0, ALU.max, ALU.max))
                    v.tensor_copy(rs_c[:, h:h + 1], o[:, (h + 1) * SC - 1:(h + 1) * SC])
                    link(v.tensor_copy(rm_c[:, h:h + 1], t3[:, (h + 1) * SC - 1:(h + 1) * SC]))
                small_mms()
                link(v.tensor_copy(cy_c, pi[:, 0:2]))
                link(v.tensor_tensor(cy_c[:, 1:2], cy_c[:, 1:2], pi[:, 2:3], ALU.add))
                link(v.memset(rowb[0:1, 0:1], -1.0))
                link(v.tensor_copy(cur[0:1, 0:2 * P], pi[0:1, 256:512]))
                link(v.tensor_tensor_scan(rowb[0:1, 1:2 * P + 1], cur[0:1, 0:2 * P], cur[0:1, 0:2 * P], -1.0, ALU.max, ALU.max))
                small_mms()
                link(v.tensor_copy(rm_c, pi[:, 512:514]))
                for h in range(2):
                    q = slice(h * SC, (h + 1) * SC)
                    link(v.tensor_scalar(o[:, q], o[:, q], cy_c[:, h:h + 1], -1.0, ALU.add, ALU.add))
                    link(v.tensor_scalar(t3[:, q], t3[:, q], rm_c[:, h:h + 1], None, ALU.max))
                link(v.tensor_tensor(t3, t3, k, ALU.is_equal))
                link(v.scalar_tensor_tensor(out=t3, in0=t2, scalar=0.0, in1=t3, op0=ALU.is_equal, op1=ALU.mult))
                link(v.scalar_tensor_tensor(out=t2, in0=k, scalar=105000.0, in1=t3, op0=ALU.is_lt, op1=ALU.mult))
                link(v.tensor_scalar(low, low, -1.0, None, ALU.add))
                to_row(low, t0, t3)
                to_row(o, cur, t3)
                link(v.tensor_scalar(t0, t0, 256.0 - 60000.0, None, ALU.add))
                link(v.tensor_tensor(t0, t0, t2, ALU.mult))
                link(v.tensor_scalar(t0, t0, 60000.0, None, ALU.add))
                link(v.tensor_scalar(t1, cur, -FAR, None, ALU.add))
                link(v.tensor_tensor(t1, t1, t2, ALU.mult))
                link(v.tensor_scalar(t1, t1, FAR, None, ALU.add))
                pack(t0, t1, va)
                r = net_sort(2, 16)
                link(v.tensor_copy(t0[:, 0:SC], r[:, 0:SC]))
                dve.sem_inc(srt_rdy, 1)
                dve.wait_ge(nb_in, 16 * loads)
                bits = t1[0:98, 0:SC]
                field_of(bits, t0[0:98, 0:SC])
                link(v.tensor_scalar(t0[0:98, 0:SC], t0[0:98, 0:SC], -256.0, None, ALU.add))
                link(v.tensor_scalar(t2[0:98, 0:SC].bitcast(I32), bits.bitcast(I32), 32767, None, ALU.bitwise_and))
                link(v.tensor_copy(t2[0:98, 0:SC], t2[0:98, 0:SC].bitcast(I32)))
                small_mms()
                v.tensor_copy(hI[i][:, :], pi[:, 0:196])
                link(v.tensor_copy(aI[i][:, :], pi[:, 256:452]))
                dve.sem_inc(idx_rdy, 1)

            net_join(srt[0], srt[1], 0, 11)
            link(v.memset(shf[:, :], 0.0))
            link(v.tensor_copy(shf[:, F:P], ident[:, 0:P - F]))
            dve.wait_ge(wz_mm, 1)
            v.tensor_copy(wZ[:, 1, :], pi[:, 0:P])
            link(v.tensor_copy(cb_c, pi[:, P:P + 1]))
            dve.sem_inc(ready, 1)

            def one(i, l):
                i.then_inc(dve_n[l], 1)

            def ln_out(l, n, o, shift):
                dve.wait_ge(act_n[l], n.act + 3)
                one(v.scalar_tensor_tensor(out=o, in0=ps[l][0][:, 0:W], scalar=shift, in1=HB[l][:, :],
                                           op0=ALU.add, op1=ALU.mult), l)

            def mlp_out(l, n, g, o):
                dve.wait_ge(pe_n[l], n.pe + 2)
                one(v.tensor_scalar(o, ps[l][1][:, 0:W], bg_c[:, 2 * g + 1:2 * g + 2], 0.0, ALU.add, ALU.max), l)

            shifts = [0]

            def carries(end, prod, largest):
                for i in range(C - 1):
                    if i == 0:
                        link(v.tensor_copy(ctmp, end))
                    elif largest:
                        link(v.tensor_scalar(p56, prod, -NEG, NEG, ALU.mult, ALU.add))
                        link(v.tensor_tensor(p56, p56, carry, ALU.add))
                        link(v.tensor_tensor(ctmp, p56, end, ALU.max))
                    else:
                        link(v.scalar_tensor_tensor(out=ctmp, in0=prod, scalar=carry, in1=end, op0=ALU.mult, op1=ALU.add))
                    shifts[0] += 1
                    dve.sem_inc(cr_rdy, 1)
                    dve.wait_ge(cr_mm, shifts[0])
                    link(v.tensor_copy(carry, pc[:, 0:1]))
                    dve.sem_inc(cr_used, 1)

            def scan_block(o, i, mask, b, back):
                d = slice(None, None, -1) if back else slice(None)
                first = b == (NB - 1 if back else 0)
                at = (b + 1) * W if back else b * W - 1
                link(v.tensor_tensor_scan(blk(o, b)[:, d], blk(mask, b)[:, d], blk(i, b)[:, d],
                                          0.0 if first else o[:, at:at + 1], ALU.mult, ALU.add))

            def max_block(o, i, mask, b, back):
                d = slice(None, None, -1) if back else slice(None)
                first = b == (NB - 1 if back else 0)
                at = (b + 1) * W if back else b * W - 1
                link(v.tensor_scalar(X3[0][:, :], blk(mask, b), -NEG, NEG, ALU.mult, ALU.add))
                link(v.tensor_tensor_scan(blk(o, b)[:, d], X3[0][:, d], blk(i, b)[:, d],
                                          NEG if first else o[:, at:at + 1], ALU.add, ALU.max))

            def max_fix(o, prod, b):
                link(v.tensor_scalar(X3[0][:, :], blk(prod, b), -NEG, NEG, ALU.mult, ALU.add))
                link(v.scalar_tensor_tensor(out=blk(o, b), in0=X3[0][:, :], scalar=carry, in1=blk(o, b), op0=ALU.add, op1=ALU.max))

            def sum_fix(o, prod, b):
                return v.scalar_tensor_tensor(out=blk(o, b), in0=blk(prod, b), scalar=carry, in1=blk(o, b),
                                              op0=ALU.mult, op1=ALU.add)

            def back_sums(o, i):
                for b in reversed(range(NB)):
                    link(v.scalar_tensor_tensor(out=blk(o, b), in0=blk(NE, b), scalar=0.0, in1=blk(i, b),
                                                op0=ALU.is_equal, op1=ALU.mult))
                    scan_block(o, o, NE, b, True)
                carries(o[:, 0:1], QB[:, 0:1], False)

            for L in range(NL):
                fb, bb = (T2, T1) if L == 1 else (T1, T2)
                local, other = (S, D) if L < 3 else (D, S)
                if L == 1:
                    for b in range(NB):
                        l, n = b % 2, before["score", b]
                        dve.wait_ge(act_n[l], n.act + 1)
                        one(v.scalar_tensor_tensor(out=blk(T1, b), in0=AB[l][:, :], scalar=0.2, in1=AB[l][:, :],
                                                   op0=ALU.mult, op1=ALU.max), l)
                    for l in range(2):
                        n = before["score", NB - 2 + (l + NB) % 2]
                        dve.wait_ge(dve_n[l], n.dve + 1)
                    for b in range(NB):
                        max_block(T2, T1, NS, b, False)
                    carries(T2[:, J - 1:J], PF[:, J - 1:J], True)
                    for b in range(NB):
                        max_fix(T2, PF, b)
                    for b in reversed(range(NB)):
                        max_block(T2, T2, NE, b, True)
                    carries(T2[:, 0:1], QB[:, 0:1], True)
                    for b in range(NB):
                        max_fix(T2, QB, b)
                        v.tensor_tensor(blk(T1, b), blk(T1, b), blk(T2, b), ALU.subtract).then_inc(e_rdy, 1)
                    for b in range(NB):
                        dve.wait_ge(e_exp, b + 1)
                        scan_block(T2, T1, NS, b, False)
                    carries(T2[:, J - 1:J], PF[:, J - 1:J], False)
                    for b in range(NB):
                        link(sum_fix(T2, PF, b))
                    back_sums(T2, T2)
                    for b in range(NB):
                        link(sum_fix(T2, QB, b))
                        link(v.reciprocal(blk(T2, b), blk(T2, b)))
                        v.tensor_tensor(blk(T1, b), blk(T1, b), blk(T2, b), ALU.mult).then_inc(att_rdy, 1)
                for b in range(NB):
                    l, n = b % 2, before["msg", L, b]
                    if L == 0:
                        dve.wait_ge(pe_n[l], n.pe + 4)
                        one(v.tensor_scalar(blk(T1, b), ps[l][1][:, 0:W], b2a_c, None, ALU.add), l)
                        dve.wait_ge(dve_n[l], n.dve + 1)
                    elif L == 1:
                        for h in range(4):
                            dve.wait_ge(pe_n[l], n.pe + 2 * h + 1)
                            one(v.tensor_tensor(HB[l][:, :], blk(D, b), ps[l][0][:, 0:W], ALU.mult), l)
                        dve.wait_ge(pe_n[l], n.pe + 8)
                        one(v.tensor_copy(blk(T2, b), ps[l][1][:, 0:W]), l)
                        dve.wait_ge(dve_n[l], n.dve + 5)
                    elif L == 2:
                        dve.wait_ge(pe_n[l], n.pe + 1)
                        one(v.tensor_tensor(blk(T1, b), blk(D, b), ps[l][0][:, 0:W], ALU.mult), l)
                        dve.wait_ge(dve_n[l], n.dve + 1)
                    else:
                        one(v.tensor_tensor(blk(T1, b), blk(S, b), blk(EA, b), ALU.add), l)
                        dve.wait_ge(act_n[l], n.act + 1)
                    scan_block(fb, fb, NS, b, False)
                carries(fb[:, J - 1:J], PF[:, J - 1:J], False)
                for b in range(NB):
                    sum_fix(fb, PF, b).then_inc(fix_n, 1)
                dve.wait_ge(fix_n, (L + 1) * NB)
                back_sums(bb, fb)
                for b in range(NB):
                    sum_fix(bb, QB, b).then_inc(tot_n, 1)
                for i0 in range(*DENSE[L], 2):
                    for n in range(7):
                        for i in (i0, i0 + 1):
                            l, c = i % 2, before["dense", i, n]
                            if n in (1, 2, 3, 5):
                                ln_out(l, c, X3[l][:, :] if n == 3 else AB[l][:, :], cb_c if n == 2 else zero_c)
                            elif n == 4:
                                mlp_out(l, c, n - 4, AB[l][:, :])
                shift = cb_c if L == 1 else zero_c
                for name, t in (("local", local), ("other", other)):
                    for b in range(NB):
                        l, n = b % 2, before[name, L, b]
                        ln_out(l, n, blk(t, b), shift) if L < 3 else mlp_out(l, n, L - 3, blk(t, b))
                for l in range(2):
                    dve.wait_ge(dve_n[l], before["other", L, NB - 2 + (l + NB) % 2].dve + 1)
                if L == 2:
                    for b in range(NB):
                        dve.wait_ge(g4[b % 2], 16 * C * KB * (uses(b) + 1))
                        v.tensor_copy(sUI[:, :].rearrange("p (c k) -> p k c", c=C)[:, b * KB:(b + 1) * KB, :],
                                      g4_buf[b % 2].rearrange("p (k c w) -> p k c w", k=KB, c=C)[:, :, :, ROW4 - 1]).then_inc(sux, 1)
                    read_masks(1)
                    for l in range(2):
                        dve.wait_ge(act_n[l], before["from4", NB - 2 + (l + NB) % 2].act + 6)
                        dve.wait_ge(d4[l], 16 * uses(NB + 1 - l))
            for s, t in ((0, S), (1, D)):
                for b in range(NB):
                    ln_out(b % 2, before["last_ln", s, b], blk(t, b), zero_c)


def kernel(**inputs):
    import numpy as _np
    import concourse.bacc as _bacc
    from concourse import mybir as _mybir
    from concourse.bass_utils import run_bass_kernel_spmd as _run

    a = {k: _np.asarray(v) for k, v in inputs.items()}
    gine = _np.stack([a["L3_gnn_W1"], a["L3_gnn_W2"]], axis=1).reshape(2 * 5, 32, 32)
    laid = [
        ("x", a["x"]), ("src", a["src"]), ("dst", a["dst"]), ("ea16", a["edge_attr_16"]), ("ea32", a["edge_attr_32"]),
        ("ew", a["edge_weight"]), ("w1a", a["L0_gnn_W1"]), ("b1a", a["L0_gnn_b1"]), ("w2a", a["L0_gnn_W2"]),
        ("b2a", a["L0_gnn_b2"]), ("watt", a["L1_gnn_w"].transpose(1, 0, 2)), ("fcw", a["L1_gnn_fc_w"]),
        ("fcb", a["L1_gnn_fc_b"]), ("batt", a["L1_gnn_bias"]), ("wz", a["L2_gnn_weight"]),
        ("wzt", a["L2_gnn_weight"].T), ("eps", a["L3_gnn_eps"]), ("wg", gine.transpose(2, 0, 1)),
        ("bg", _np.stack([a["L3_gnn_b1"], a["L3_gnn_b2"]], axis=1).reshape(10, 32).T),
    ]
    nc = _bacc.Bacc("TRN2", target_bir_lowering=False, num_devices=1)
    arrays, args = {}, []
    for name, v in laid:
        v = _np.ascontiguousarray(v)
        arrays[f"in_{name}"] = v
        args.append(nc.dram_tensor(f"in_{name}", v.shape, _mybir.dt.from_np(v.dtype), kind="ExternalInput").ap())
    args.append(nc.dram_tensor("out_0", (NODES, F), F32, kind="ExternalOutput").ap())
    build(nc, *args)
    r = _run(nc, [arrays], core_ids=[0])
    return r.results[0]["out_0"]
```

```python
from contextlib import ExitStack

import concourse.bass as bass
from concourse import mybir

F32 = mybir.dt.float32
I32 = mybir.dt.int32
U8 = mybir.dt.uint8
I8 = mybir.dt.int8
ALU = mybir.AluOpType
ACT = mybir.ActivationFunctionType
AXX = mybir.AxisListType.X

P = 128
NODES, EDGES, F = 100000, 25000, 32
C = P // F
NT = -(-EDGES // (C * P))
J = NT * P
ROWS = C * J
KB = 7
NB = NT // KB
W = KB * P
HALF = 32768
SC = HALF // P
EP, ER = 125, 200
ATT = 16 + 32 + 1 + 1
ROW4 = 2 * F
NEG = -1.0e30
EPS = 1e-5
SPLIT, PAD, FAR = 51000.0, 110000.0, 30000.0
HID = 64
GINE = 1
NL = 3 + GINE
DJ = NODES // C
DW = 512
DR = DW // P
ND = -(-DJ // DW)
DL = 3
BG = 7
NW = 9 * C + 5
N_CONST = 12
assert NT % KB == 0 and ROWS % (P * BG) == 0


STEPS = {
    "turn_in": (1, 1, 0, 0, 0), "rows_in": (1, 1, 0, 1, 0), "rows_out": (1, 1, 0, 0, 1), "ln": (2, 3, 1, 0, 0),
    "mlp": (2, 1, 1, 0, 0), "edge": (4, 4, 1, 0, 0), "score": (1, 1, 1, 0, 0), "attend": (8, 0, 5, 0, 0),
    "scale": (1, 1, 1, 0, 0), "to_row4": (2, 2, 1, 0, 0), "from_row4": (2, 4, 0, 0, 0), "final": (1, 3, 2, 0, 0),
}


D_PE, D_ACT, D_DVE, D_STEPS = 4, 12, 9, 10


def dense_order():
    order = []
    for k in range(D_STEPS * (-(-ND // DL)) + 6):
        for lane in range(DL):
            u, n = divmod(k - 3 * lane, D_STEPS)
            if u >= 0 and DL * u + lane < ND:
                order.append((DL * u + lane, n))
    return order


FILL = (0, 35, 7)


class Count:

    def __init__(self, pe=0, act=0, dve=0, load=0, store=0):
        self.pe, self.act, self.dve, self.load, self.store = pe, act, dve, load, store


def count_steps():
    before, now = {}, [(0,) * 5, (0,) * 5]

    def step(lane, kind, *key):
        assert key not in before
        before[key] = Count(*now[lane])
        now[lane] = tuple(a + b for a, b in zip(now[lane], STEPS[kind]))

    for b in range(NB):
        step(b % 2, "turn_in", "turn", 1, b)
    for L in range(3):
        if L == 1:
            for b in range(NB):
                step(b % 2, "score", "score", b)
        for b in range(NB):
            step(b % 2, ("edge", "attend", "scale")[L], "msg", L, b)
        before["sums", L] = Count(*now[1])
        for b in range(NB):
            step(b % 2, "rows_out", "table", L, b)
        if L == 0:
            for b in range(NB):
                step(b % 2, "turn_in", "turn", 0, b)
        before["back", L] = Count(*now[1])
        for b in range(NB):
            step(b % 2, "ln", "local", L, b)
        for b in range(NB):
            step(b % 2, "rows_in", "update", L, b)
            step(b % 2, "ln", "other", L, b)
    for b in range(NB):
        step(b % 2, "to_row4", "to4", b)
    for s in range(2):
        if s == 1:
            for b in range(NB):
                step(b % 2, "from_row4", "from4", b)
            before["sums", 3] = before["back", 3] = Count(*now[1])
        for b in range(NB):
            step(b % 2, "mlp", "last", s, b)
            step(b % 2, "final", "final", s, b)
    return before, now


def build(nc, x, src, dst, ea16, ea32, ew, w1a, b1a, w2a, b2a, watt, fcw, fcb, batt, wz, wzt, eps, wg, bg, out):
    ctx = ExitStack()
    with ctx:
        def sb(name, shape, dt=F32):
            return ctx.enter_context(nc.sbuf_tensor(name, shape, dt))

        def sem(name):
            return ctx.enter_context(nc.semaphore(name))

        def dram(name, shape, dt=F32):
            return nc.dram_tensor(name, shape, dt, kind="Internal").ap()

        attN = dram("attN", (EDGES, ATT))
        attS = dram("attS", (ROWS, ATT))
        row4 = dram("row4", (ROWS, ROW4))
        table = dram("table", (ROWS, F))
        upd = dram("upd", (ROWS, F))
        sorted_d = [dram(f"sorted{i}", (HALF + 2, 1)) for i in range(2)]
        list_d = dram("list", (HALF, 1))
        mask_d = [dram(f"mask{i}", (2, ROWS), U8) for i in range(2)]

        big = sb("big", [P, 4 * J])
        S, D, T1, T2 = (big[:, i * J:(i + 1) * J] for i in range(4))
        rest = sb("rest", [P, J])
        EA = rest[:, :]
        at = [0]

        def part(n):
            a = rest[:, at[0]:at[0] + n]
            at[0] += n
            assert at[0] <= J
            return a

        flips = part(16 * 2 * SC // 4).bitcast(I8).rearrange("p (k w) -> p k w", k=16)
        va, vb, t0, t1, t2, t3 = (part(2 * SC) for _ in range(6))
        srt = [part(SC), part(SC)]
        iop = part(SC)
        nat32, nat16, nat_w = big[0:EP, 0:6400], big[0:EP, 6400:9600], big[0:EP, 9600:9800]
        nat_dst, nat_src = (big[0:EP, a:a + 200].bitcast(I32) for a in (9800, 10000))
        index2, gray = (big[:, a:a + 2 * SC].bitcast(I32) for a in (10240, 10752))
        nat_att = big[0:EP, 2 * J:2 * J + ER * ATT]
        NS, NE, PF, QB = (sb(n, [P, J], U8) for n in ("not_start", "not_end", "first_seg", "last_seg"))
        RI = [sb(f"rows{i}", [P, W]) for i in range(2)]
        AB = [sb(f"arg{i}", [P, W]) for i in range(2)]
        HB = [sb(f"hid{i}", [P, W]) for i in range(2)]
        X3 = [sb(f"res{i}", [P, W]) for i in range(2)]
        RA = sb("edge_rows", [P, KB * C * ATT])
        mask8 = RA[:, 0:98].bitcast(U8).rearrange("p (m f) -> p m f", m=2)
        G = [RA[:, i * BG * F:(i + 1) * BG * F] for i in range(4)]
        ident = sb("ident", [P, P])
        center = sb("center", [P, P])
        mean = sb("mean", [P, P])
        shf = sb("shf", [P, P])
        shb = sb("shb", [P, P])
        ltri = part(P)
        wA = sb("wA", [P, 2, P])
        wE = sb("wE", [64, 2, P])
        wB = sb("wB", [P, 2, P])
        wH = sb("wH", [P, 4, P])
        wSel = sb("wSel", [P, 4, P])
        wSc = sb("wSc", [P, 2, P])
        wZ = sb("wZ", [P, 2, P])
        wG = sb("wG", [P, 2 * GINE, P])
        wX = sb("wX", [P, GINE, P])
        cols = sb("cols", [P, 32])
        zero_c, eps_c, cb_c, fcb_c, b1a_c, b2a_c, batt_c = (cols[:, i:i + 1] for i in range(7))
        carry, ctmp, spare, eps2_c = (cols[:, i:i + 1] for i in range(7, 11))
        bg_c = cols[:, 11:11 + 2 * GINE]
        eps_g = cols[:, 21:21 + GINE]
        rs_c = cols[:, 26:28]
        cy_c = cols[:, 28:30]
        rm_c = cols[:, 30:32]
        fcr = sb("fcr", [P, 2 * F])
        cb_row = sb("cb_row", [P, F])
        wat = sb("wat", [P, 4 * F])
        wtmp = part(4 * F)
        rowb = X3[0][0:1, 0:2 * P + 1]
        sG, dG, jI = (sb(n, [P, C * NT], I32) for n in ("src_id", "dst_id", "src_row"))
        sU = sb("src_end", [P, C * NT], I32)
        dUI = sb("dst_end", [P, C * NT], I32)
        home, frm = sb("home", [P, C * NT], I32), sb("from", [P, C * NT], I32)
        pos1, eid = sb("position", [P, C * NT], I32), sb("edge_id", [P, C * NT], I32)
        eI = frm

        ps = [[ctx.enter_context(nc.psum_tensor(f"ps{l}{u}", [P, 1024], F32)) for u in range(2)] for l in range(2)]
        pi = ps[1][1]
        pc = ps[1][1][:, 1000:1008]
        dR, dA, dH, dX = ([S[:, (4 * l + i) * DW:(4 * l + i + 1) * DW] for l in range(DL)] for i in range(4))
        dP = [[(ps[0][0], ps[0][1], ps[1][0])[l][:, u * DW:(u + 1) * DW] for u in range(2)] for l in range(DL)]
        inv = sb("inverse", [P, max(DL * 4 * DR, 2 * KB * C)])

        consts = sem("consts")
        w_zero = sem("weights_cleared")
        w_in = sem("weights_in")
        src_in = sem("src_in")
        nat_in = sem("natural_in")
        nat_rows = sem("natural_rows")
        attn_out = sem("attn_out")
        ready = sem("weights_ready")
        wz_mm = sem("wz_mm")
        turn_rdy, turned = sem("turn_ready"), sem("turned")
        small_rdy, small_mm = sem("small_ready"), sem("small_mm")
        dchain = sem("dve_chain")
        srt_rdy = sem("sorted_ready")
        srt_out = sem("sorted_out")
        nb_in = sem("neighbours_in")
        mask_rdy, mask_out, mask_in = sem("mask_ready"), sem("mask_out"), sem("mask_in")
        idx_rdy = sem("index_ready")
        pool_ok = sem("pool_chain")
        ga = [sem("att_rows0"), sem("att_rows1")]
        dcol = sem("dst_col")
        atts_out = [sem("atts_out0"), sem("atts_out1")]
        gx = [sem("x_src_rows"), sem("x_dst_rows")]
        pe_n = [sem("pe_lane0"), sem("pe_lane1")]
        act_n = [sem("act_lane0"), sem("act_lane1")]
        dve_n = [sem("dve_lane0"), sem("dve_lane1")]
        ld_n = [sem("load_lane0"), sem("load_lane1")]
        st_n = [sem("store_lane0"), sem("store_lane1")]
        ra_in = sem("edge_rows_in")
        dpe, dact, ddve, dld, dst_ = ([sem(f"dense_{n}{l}") for l in range(DL)] for n in ("pe", "act", "dve", "load", "store"))
        e_rdy, e_exp = sem("exp_ready"), sem("exp_done")
        att_rdy = sem("att_ready")
        fix_n = sem("prefix_ready")
        tot_n = sem("total_ready")
        cr_rdy, cr_mm, cr_used = sem("carry_ready"), sem("carry_shifted"), sem("carry_used")
        gs = [sem(f"picked_in{i}") for i in range(C * NT // BG)]
        ss = [sem(f"put_out{i}") for i in range(C * NT // BG)]
        upd_n = sem("updates_out")
        zeroed = sem("zeroed")
        r4_out = [sem("row4_out0"), sem("row4_out1")]
        table_out = sem("table_out")
        g4 = [sem("row4_in0"), sem("row4_in1")]
        fin = sem("final_put")

        block = ctx.enter_context(nc.Block())

        def blk(t, b):
            return t[:, b * W:(b + 1) * W]

        def rows128(t, b):
            return t.rearrange("(b k p c) w -> b p k (c w)", b=NB, k=KB, p=P, c=C)[b]

        def xrows(t, i):
            j0 = min(i * DW, DJ - DW)
            return t.rearrange("(j c) f -> j (c f)", c=C)[j0:j0 + DW, :].rearrange("(p r) q -> p (r q)", r=DR)

        NA = KB * C * ATT
        att_buf = [T1[:, i * NA:(i + 1) * NA] for i in range(2)]
        N4 = KB * C * ROW4
        r4_buf = [T1[:, i * N4:(i + 1) * N4] for i in range(2)]
        g4_buf = [T2[:, i * N4:(i + 1) * N4] for i in range(2)]
        before, _ = count_steps()
        order = dense_order()

        def kview(t):
            return t.rearrange("p (k w) -> p k w", k=KB)

        def dense_blocks(l):
            return -(-(ND - l) // DL)

        def uses(b):
            return b // 2

        @block.sync
        def _(sp):
            sp.dma_start(nat_src, src.rearrange("(p r) -> p r", r=ER)).then_inc(src_in, 16)
            sp.dma_start(nat_dst, dst.rearrange("(p r) -> p r", r=ER)).then_inc(nat_in, 16)
            sp.dma_start(nat_w, ew.rearrange("(p r) -> p r", r=ER)).then_inc(nat_in, 16)
            sp.dma_start(nat16, ea16.rearrange("(p r) w -> p (r w)", r=ER)).then_inc(nat_in, 16)
            sp.dma_start(nat32, ea32.rearrange("(p r) w -> p (r w)", r=ER)).then_inc(nat_in, 16)
            sp.wait_ge(consts, N_CONST)
            sp.wait_ge(w_zero, 1)
            n = 0

            def win(o, i):
                nonlocal n
                sp.dma_start(o, i).then_inc(w_in, 16)
                n += 1

            def column(v):
                return v.rearrange("(f o) -> f o", o=1)

            with nc.allow_non_contiguous_dma(reason="small weights"):
                for c in range(C):
                    q = slice(F * c, F * c + F)
                    g, h = divmod(c, 2)
                    win(wA[q, g, HID * h:HID * h + HID], w1a[0:F, :])
                    win(wE[16 * c:16 * c + 16, g, HID * h:HID * h + HID], w1a[F:F + 16, :])
                    win(wB[HID * h:HID * h + HID, g, q], w2a)
                    win(wat[q, :], watt.rearrange("f h o -> f (h o)"))
                    win(wZ[q, 0, q], wzt)
                    win(wG[q, :, q], wg[:, 8:10, :])
                    win(bg_c[q, :], bg[:, 8:10])
                    win(b2a_c[q, :], column(b2a))
                    win(batt_c[q, :], column(batt))
                for h in range(2):
                    win(b1a_c[HID * h:HID * h + HID, :], column(b1a))
                win(fcr[:, :], fcw.to_broadcast([P, 2 * F]))
                win(fcb_c, fcb.rearrange("(o w) -> o w", o=1).to_broadcast([P, 1]))
                win(eps_g, eps.rearrange("(o w) -> o w", o=1)[:, 4:5].to_broadcast([P, GINE]))
            assert n == NW

            sp.wait_ge(nat_rows, 4)
            sp.dma_start(attN.rearrange("(p r) w -> p (r w)", r=ER), nat_att).then_inc(attn_out, 16)
            for b in range(NB):
                sp.dma_start(upd.rearrange("(b p r) w -> b p (r w)", b=NB, p=P)[b], RI[0][:, :]).then_inc(zeroed, 16)
            with nc.allow_non_contiguous_dma(reason="end marks"):
                for i in range(2):
                    sp.dma_start(sorted_d[i][0:1, :], zero_c[0:1, :]).then_inc(zeroed, 16)
                    sp.dma_start(sorted_d[i][HALF + 1:HALF + 2, :], zero_c[0:1, :]).then_inc(zeroed, 16)
            sp.wait_ge(zeroed, 16 * (NB + 4))

            def after_sort(i, k):
                sp.wait_ge(srt_rdy, k)
                sp.dma_start(sorted_d[i][1:HALF + 1, :].rearrange("(p f) o -> p (f o)", p=P), srt[i]).then_inc(srt_out, 16)
                sp.wait_ge(srt_out, 16 * k)
                base = sorted_d[i].rearrange("n o -> (n o)")
                for off, o in ((1, t0), (2, t1)):
                    sp.dma_start(o[0:98, 0:256].rearrange("q (g p) -> q g p", g=2),
                                 base[off:off + ROWS].rearrange("(g q p) -> q g p", g=2, q=98)).then_inc(nb_in, 16)
                for off, o in ((0, t2[:, 0:196]), (1, t2[:, 256:452]), (2, t3[:, 0:196])):
                    sp.dma_start(o, base[off:off + ROWS].rearrange("(p f) -> p f", p=P)).then_inc(nb_in, 16)

            def masks_out(i):
                sp.wait_ge(mask_rdy, i + 1)
                with nc.allow_non_contiguous_dma(reason="rows of 196 bytes"):
                    sp.dma_start(mask_d[i].rearrange("m (p f) -> p m f", p=P), mask8).then_inc(mask_out, 16)
                sp.wait_ge(mask_out, 16 * (i + 1))

            def masks_in(i):
                for m, o in ((0, NS), (1, NE)):
                    for c in range(C):
                        sp.dma_start(o[F * c:F * c + F, :],
                                     mask_d[i][m:m + 1, c * J:(c + 1) * J].to_broadcast([F, J])).then_inc(mask_in, 16)

            def after_list(i, k):
                sp.wait_ge(srt_rdy, k)
                sp.dma_start(list_d.rearrange("(p f) o -> p (f o)", p=P), t0[:, 0:256]).then_inc(srt_out, 16)
                sp.wait_ge(srt_out, 16 * k)
                sp.dma_start(t1[0:98, 0:256].rearrange("q (g p) -> q g p", g=2),
                             list_d.rearrange("n o -> (n o)")[0:ROWS].rearrange("(g q p) -> q g p", g=2, q=98)).then_inc(nb_in, 16)

            after_sort(0, 1)
            masks_out(0)
            masks_in(0)
            for b in range(NB):
                sp.wait_ge(ga[b % 2], 16 * C * KB * (uses(b) + 1))
                sp.dma_start(rows128(attS, b), kview(att_buf[b % 2])).then_inc(atts_out[b % 2], 16)
            after_sort(1, 2)
            masks_out(1)
            after_list(0, 3)
            for i in range(2):
                sp.wait_ge(atts_out[i], 16 * uses(NB + 1 - i))

            def lane_done(l, n):
                if n.pe:
                    sp.wait_ge(pe_n[l], n.pe)
                if n.act:
                    sp.wait_ge(act_n[l], n.act)
                if n.store:
                    sp.wait_ge(st_n[l], 16 * n.store)

            def load(l, n, ap):
                lane_done(l, n)
                sp.dma_start(kview(RI[l][:, :]) if len(ap.shape) == 3 else RI[l][:, :], ap).then_inc(ld_n[l], 16)

            def store(l, n, ap):
                sp.wait_ge(act_n[l], n.act + 1)
                sp.dma_start(ap, kview(RI[l][:, :]) if len(ap.shape) == 3 else RI[l][:, :]).then_inc(st_n[l], 16)

            def edge_rows(b, free):
                free(b)
                sp.dma_start(kview(RA[:, :]), rows128(attS, b)).then_inc(ra_in, 16)

            for L in range(3):
                def read_before(b):
                    if b:
                        sp.wait_ge(act_n[(b - 1) % 2], before["msg", L, b - 1].act + 1)
                if L in (0, 2):
                    for b in range(NB):
                        edge_rows(b, read_before)
                for b in range(NB):
                    store(b % 2, before["table", L, b], rows128(table, b))
                for b in range(2):
                    sp.wait_ge(st_n[b], 16 * (before["table", L, NB - 2 + (NB - b) % 2].store + 1))
                sp.sem_inc(table_out, 1)
                sp.wait_ge(upd_n, L + 1)
                for b in range(NB):
                    load(b % 2, before["update", L, b], rows128(upd, b))

            def read4(b):
                if b:
                    sp.wait_ge(dve_n[(b - 1) % 2], before["to4", b - 1].dve + 1)
                else:
                    sp.wait_ge(act_n[(NB - 1) % 2], before["msg", 2, NB - 1].act + 1)
            for b in range(NB):
                edge_rows(b, read4)
                sp.wait_ge(act_n[b % 2], before["to4", b].act + 2)
                sp.dma_start(rows128(row4, b), kview(r4_buf[b % 2])).then_inc(r4_out[b % 2], 16)
            masks_in(1)
            sp.wait_ge(fin, 16 * 2 * C * NT)

        @block.gpsimd
        def _(pool):
            done = [0]

            def const(i):
                done[0] += 1
                i.then_inc(consts, 1)
                pool.wait_ge(consts, done[0])

            def bands(t, c, value):
                q = slice(F * c, F * c + F)
                const(nc.gpsimd.memset(t[q, q], value))

            for i, (t, value) in enumerate(((ident, 0.0), (ltri, 1.0), (mean, 0.0))):
                nc.gpsimd.memset(t[:, :], value).then_inc(pool_ok, 1)
                pool.wait_ge(pool_ok, i + 1)
            const(nc.gpsimd.affine_select(out=ident[:, :], in_=ident[:, :], compare_op=ALU.not_equal, fill=1.0,
                                          base=0, pattern=[[-1, P]], channel_multiplier=1))
            const(nc.gpsimd.affine_select(out=ltri[:, :], in_=ltri[:, :], compare_op=ALU.is_gt, fill=0.0,
                                          base=0, pattern=[[1, P]], channel_multiplier=-1))
            for c in range(C):
                bands(mean, c, 1.0 / F)
            const(nc.gpsimd.iota(index2[:, 0:SC], pattern=[[1, SC]], base=0, channel_multiplier=SC))
            const(nc.gpsimd.iota(index2[:, SC:2 * SC], pattern=[[1, SC]], base=HALF, channel_multiplier=SC))
            const(nc.gpsimd.iota(pos1[:, :], pattern=[[P, C * NT]], base=1, channel_multiplier=1))
            const(nc.gpsimd.iota(eid[:, :], pattern=[[1, C * NT]], base=0, channel_multiplier=ER))
            const(nc.gpsimd.iota(frm[:, 0:4], pattern=[[1, 4]], base=ER - 4, channel_multiplier=ER))
            const(nc.gpsimd.memset(cols[:, :], 0.0))
            assert done[0] == N_CONST

            def gather(o, t, index, m, signal):
                nc.gpsimd.indirect_dma_start(
                    out=o, out_offset=None, in_=t, in_offset=bass.IndirectOffsetOnAxis(ap=index[:, m:m + 1], axis=0),
                    bounds_check=t.shape[0] - 1, oob_is_err=False).then_inc(signal, 16)

            def scatter(t, index, m, i, signal):
                nc.gpsimd.indirect_dma_start(
                    out=t, out_offset=bass.IndirectOffsetOnAxis(ap=index[:, m:m + 1], axis=0), in_=i, in_offset=None,
                    bounds_check=t.shape[0] - 1, oob_is_err=False).then_inc(signal, 16)

            def tiles(b):
                return [(k * C + c, c * NT + b * KB + k) for k in range(KB) for c in range(C)]

            pool.wait_ge(attn_out, 16)
            pool.wait_ge(idx_rdy, 1)
            for b in range(NB):
                if b >= 2:
                    pool.wait_ge(atts_out[b % 2], 16 * uses(b))
                    pool.wait_ge(dcol, b - 1)
                for i, m in tiles(b):
                    gather(att_buf[b % 2][:, i * ATT:(i + 1) * ATT], attN, eI, m, ga[b % 2])
            pool.wait_ge(dcol, NB + 1)
            for b in range(NB):
                for i, m in tiles(b):
                    gather(D[:, b * W + i * F:b * W + (i + 1) * F], x, dG, m, gx[1])
            for b in range(NB):
                for i, m in tiles(b):
                    gather(T2[:, b * W + i * F:b * W + (i + 1) * F], x, sG, m, gx[0])

            first = []

            def updates(L):
                pool.wait_ge(table_out, L + 1)
                nb = C * NT // BG
                if L == 0:
                    pool.wait_ge(idx_rdy, 3)
                    for i in range(nb):
                        first.append(pool.value_load(home[0:1, i * BG:i * BG + 1], min_val=0, max_val=65535))
                for i in range(nb + 2):
                    if i < nb:
                        with pool.If(first[i] < ROWS):
                            if i >= 4:
                                pool.wait_ge(ss[i - 4], 16 * BG * (L + 1))
                            for m in range(BG):
                                gather(G[i % 4][:, m * F:(m + 1) * F], table, frm, i * BG + m, gs[i])
                    if i >= 2:
                        with pool.If(first[i - 2] < ROWS):
                            pool.wait_ge(gs[i - 2], 16 * BG * (L + 1))
                            for m in range(BG):
                                scatter(upd, home, (i - 2) * BG + m, G[(i - 2) % 4][:, m * F:(m + 1) * F], ss[i - 2])
                for i in range(nb):
                    with pool.If(first[i] < ROWS):
                        pool.wait_ge(ss[i], 16 * BG * (L + 1))
                pool.sem_inc(upd_n, 1)

            for L in range(3):
                updates(L)
            for b in range(2):
                pool.wait_ge(r4_out[b], 16 * uses(NB + 1 - b))
            for b in range(NB):
                if b >= 2:
                    pool.wait_ge(act_n[b % 2], before["from4", b - 2].act + 2)
                for i, m in tiles(b):
                    gather(g4_buf[b % 2][:, i * ROW4:(i + 1) * ROW4], row4, jI, m, g4[b % 2])
            for l in range(DL):
                pool.wait_ge(dst_[l], 16 * dense_blocks(l))
            for s, t, index in ((0, S, sU), (1, D, dUI)):
                if s:
                    pool.wait_ge(fin, 16 * C * NT)
                for b in range(NB):
                    pool.wait_ge(dve_n[b % 2], before["final", s, b].dve + 2)
                    for i, m in tiles(b):
                        scatter(out, index, m, t[:, b * W + i * F:b * W + (i + 1) * F], fin)

        @block.scalar
        def _(act):
            def one(i, l):
                i.then_inc(act_n[l], 1)

            def wait_pe(l, v):
                act.wait_ge(pe_n[l], v)

            def copy(l, o, i):
                one(nc.scalar.activation(o, i, ACT.Copy), l)

            def act_rows_in(l, n, o):
                wait_pe(l, n.pe + 1)
                copy(l, o, ps[l][0][:, 0:W])

            def act_rows_out(l, n, free=None):
                wait_pe(l, n.pe + 1)
                if n.store:
                    act.wait_ge(st_n[l], 16 * n.store)
                copy(l, RI[l][:, :], ps[l][1][:, 0:W])

            def act_ln(l, n, shift):
                wait_pe(l, n.pe + 1)
                one(nc.scalar.activation(HB[l][:, :], ps[l][0][:, 0:W], ACT.Square, bias=shift), l)
                wait_pe(l, n.pe + 2)
                one(nc.scalar.activation(HB[l][:, :], ps[l][1][:, 0:W], ACT.Ln, bias=eps_c), l)
                act.wait_ge(act_n[l], n.act + 2)
                one(nc.scalar.activation(HB[l][:, :], HB[l][:, :], ACT.Exp, scale=-0.5), l)

            def act_relu(l, v, o, u, bias):
                wait_pe(l, v)
                one(nc.scalar.activation(o, ps[l][u][:, 0:W], ACT.Relu, bias=bias), l)

            act.preload_act_table_set("natural_log_exp_and_others")

            act.wait_ge(nat_in, 16 * 4)
            rows = nat_att.rearrange("p (r w) -> p r w", w=ATT)
            nc.scalar.activation(rows[:, :, 0:16], nat16.rearrange("p (r w) -> p r w", w=16), ACT.Copy).then_inc(nat_rows, 1)
            nc.scalar.activation(rows[:, :, 16:48], nat32.rearrange("p (r w) -> p r w", w=32), ACT.Copy).then_inc(nat_rows, 1)
            nc.scalar.activation(rows[:, :, 48], nat_w, ACT.Copy).then_inc(nat_rows, 1)
            nc.scalar.activation(rows[:, :, 49], nat_dst, ACT.Copy).then_inc(nat_rows, 1)
            act.wait_ge(nat_rows, 4)
            for i in range(DL):
                act.dma_start(dR[i], xrows(x, i)).then_inc(dld[i], 16)
            act.wait_ge(ready, 2)

            def dense_store(i):
                l, u = i % DL, i // DL
                act.wait_ge(ddve[l], D_DVE * (u + 1))
                if i == ND - 1:
                    act.wait_ge(dst_[(i - 1) % DL], 16 * ((i - 1) // DL + 1))
                act.dma_start(xrows(out, i), dX[l]).then_inc(dst_[l], 16)

            def dense(i, n):
                l, u = i % DL, i // DL
                A, H, q = dA[l], dH[l], dP[l]
                pe0, act0, dve0 = D_PE * u, D_ACT * u, D_DVE * u

                def go(o, i_, f, **k):
                    nc.scalar.activation(o, i_, f, **k).then_inc(dact[l], 1)

                def power(scale, add):
                    v = inv[:, l * 4 * DR:(l + 1) * 4 * DR]
                    go(v, v, ACT.Ln, bias=add, scale=scale)
                    act.wait_ge(dact[l], act0 + (2, 5, 11)[(1, 3, 8).index(n)])
                    go(v, v, ACT.Exp, scale=-0.5)

                if n == 0:
                    if u:
                        dense_store(i - DL)
                    act.wait_ge(ddve[l], dve0 + 2)
                    if i + DL < ND:
                        act.dma_start(dR[l], xrows(x, i + DL)).then_inc(dld[l], 16)
                    go(H, A, ACT.Square)
                elif n == 1:
                    act.wait_ge(ddve[l], dve0 + 3)
                    power(1.0 / F, eps_c)
                elif n == 2:
                    act.wait_ge(ddve[l], dve0 + 5)
                    go(H, A, ACT.Square)
                elif n == 3:
                    act.wait_ge(ddve[l], dve0 + 6)
                    power((1.0 + EPS) / F, eps2_c)
                elif n == 4:
                    act.wait_ge(dpe[l], pe0 + 1)
                    if u:
                        act.wait_ge(dst_[l], 16 * u)
                    go(dX[l], q[0], ACT.Copy)
                elif n == 5:
                    act.wait_ge(dpe[l], pe0 + 2)
                    go(H, q[1], ACT.Relu, bias=bg_c[:, 0:1])
                elif n == 6:
                    act.wait_ge(dpe[l], pe0 + 3)
                    go(A, q[0], ACT.Relu, bias=bg_c[:, 1:2])
                elif n == 7:
                    act.wait_ge(dpe[l], pe0 + 4)
                    go(H, q[1], ACT.Square)
                elif n == 8:
                    act.wait_ge(ddve[l], dve0 + 8)
                    power(1.0 / F, eps_c)

            for i, n in order:
                dense(i, n)
            for i in range(ND - DL, ND):
                dense_store(i)

            def turn_in(s, o):
                for b in range(NB):
                    act_rows_in(b % 2, before["turn", s, b], blk(o, b))

            turn_in(1, D)
            for L in range(3):
                if L == 1:
                    for b in range(NB):
                        l, n = b % 2, before["score", b]
                        wait_pe(l, n.pe + 1)
                        one(nc.scalar.activation(AB[l][:, :], ps[l][0][:, 0:W], ACT.Identity, bias=fcb_c), l)
                    for b in range(NB):
                        act.wait_ge(e_rdy, b + 1)
                        nc.scalar.activation(blk(T1, b), blk(T1, b), ACT.Exp).then_inc(e_exp, 1)
                for b in range(NB):
                    l, n = b % 2, before["msg", L, b]
                    if L != 1:
                        wait_pe(l, n.pe)
                        act.wait_ge(dve_n[l], n.dve)
                    if L == 0:
                        act.wait_ge(ra_in, 16 * (b + 1))
                        copy(l, HB[l][:, 0:KB * 64].rearrange("p (m w) -> p m w", w=16),
                             RA[:, :].rearrange("p (m w) -> p m w", w=ATT)[:, :, 0:16])
                        wait_pe(l, n.pe + 1)
                        copy(l, AB[l][0:64, :], ps[l][0][0:64, 0:W])
                        act_relu(l, n.pe + 2, HB[l][:, :], 1, b1a_c)
                        act_relu(l, n.pe + 3, X3[l][:, :], 0, b1a_c)
                    elif L == 2:
                        act.wait_ge(ra_in, 16 * (NB + b + 1))
                        copy(l, HB[l][:, :].rearrange("p (m f) -> p m f", f=F),
                             RA[:, :].rearrange("p (m w) -> p m w", w=ATT)[:, :, 48:49].to_broadcast([P, KB * C, F]))
                for b in range(NB):
                    act_rows_out(b % 2, before["table", L, b])
                if L == 0:
                    for l in range(DL):
                        act.wait_ge(dst_[l], 16 * dense_blocks(l))
                    turn_in(0, S)
                shift = cb_c if L == 1 else zero_c
                for b in range(NB):
                    act_ln(b % 2, before["local", L, b], shift)
                for b in range(NB):
                    act_rows_in(b % 2, before["update", L, b], AB[b % 2][:, :])
                    act_ln(b % 2, before["other", L, b], shift)
            for b in range(NB):
                l, n = b % 2, before["to4", b]
                o = r4_buf[l].rearrange("p (m w) -> p m w", w=ROW4)
                wait_pe(l, n.pe + 2)
                if b >= 2:
                    act.wait_ge(r4_out[l], 16 * uses(b))
                copy(l, o[:, :, F:2 * F], ps[l][1][:, 0:W].rearrange("p (m f) -> p m f", f=F))
                act.wait_ge(dve_n[l], n.dve + 1)
                one(nc.scalar.activation(o[:, :, 0:F], o[:, :, 0:F], ACT.Relu), l)
            for s in range(2):
                if s == 1:
                    for b in range(NB):
                        l, n = b % 2, before["from4", b]
                        wait_pe(l, n.pe)
                        act.wait_ge(dve_n[l], n.dve)
                        act.wait_ge(g4[l], 16 * C * KB * (uses(b) + 1))
                        for v, o in enumerate((HB[l], X3[l])):
                            copy(l, o[:, :].rearrange("p (m f) -> p m f", f=F),
                                 g4_buf[l].rearrange("p (m w) -> p m w", w=ROW4)[:, :, v * F:(v + 1) * F])
                        for v, o in enumerate((T1, D)):
                            wait_pe(l, n.pe + v + 1)
                            copy(l, blk(o, b), ps[l][v][:, 0:W])
                for b in range(NB):
                    l = b % 2
                    act_relu(l, before["last", s, b].pe + 1, HB[l][:, :], 0, bg_c[:, 0:1])
                    n = before["final", s, b]
                    v = inv[:, l * KB * C:(l + 1) * KB * C]
                    wait_pe(l, n.pe + 1)
                    one(nc.scalar.activation(HB[l][:, :], ps[l][0][:, 0:W], ACT.Square), l)
                    act.wait_ge(dve_n[l], n.dve + 1)
                    one(nc.scalar.activation(v, v, ACT.Ln, bias=eps_c, scale=1.0 / F), l)
                    act.wait_ge(act_n[l], n.act + 2)
                    one(nc.scalar.activation(v, v, ACT.Exp, scale=-0.5), l)

        @block.tensor
        def _(pe):
            def mm(o, w, i, start=True, stop=True):
                for a, e in ((0, 512), (512, W)):
                    r = nc.tensor.matmul(o[:, a:e], w, i[:, a:e], start=start, stop=stop)
                return r

            def begin(l, n):
                if n.act:
                    pe.wait_ge(act_n[l], n.act)
                if n.dve:
                    pe.wait_ge(dve_n[l], n.dve)

            def turn_tiles(l, u, tile, rows=P):
                for k in range(KB):
                    r = nc.tensor.transpose(ps[l][u][0:rows, k * P:(k + 1) * P], tile(k), ident[:, :])
                r.then_inc(pe_n[l], 1)

            def pe_rows_in(l, n):
                begin(l, n)
                pe.wait_ge(ld_n[l], 16 * (n.load + 1))
                turn_tiles(l, 0, lambda k: RI[l][:, k * P:(k + 1) * P])

            def pe_rows_out(l, n, t):
                begin(l, n)
                turn_tiles(l, 1, lambda k: t[:, k * P:(k + 1) * P])

            def pe_ln(l, n, t, a=None, wa=None):
                begin(l, n)
                r = mm(ps[l][0], center[:, :], t, stop=a is None)
                if a is not None:
                    r = mm(ps[l][0], wa, a, start=False)
                r.then_inc(pe_n[l], 1)
                pe.wait_ge(act_n[l], n.act + 1)
                mm(ps[l][1], mean[:, :], HB[l][:, :]).then_inc(pe_n[l], 1)

            def pe_mlp(l, n, g, t, a=None):
                begin(l, n)
                r = mm(ps[l][0], wX[:, g, :], t, stop=a is None)
                if a is not None:
                    r = mm(ps[l][0], wG[:, 2 * g, :], a, start=False)
                r.then_inc(pe_n[l], 1)
                pe.wait_ge(act_n[l], n.act + 1)
                mm(ps[l][1], wG[:, 2 * g + 1, :], HB[l][:, :]).then_inc(pe_n[l], 1)

            def dense(i, n):
                l, u = i % DL, i // DL
                q = dP[l]
                act0, dve0 = D_ACT * u, D_DVE * u
                if n == 4:
                    pe.wait_ge(ddve[l], dve0 + 7)
                    for k in range(DR):
                        r = nc.tensor.transpose(q[0][:, k * P:(k + 1) * P], dA[l][:, k * P:(k + 1) * P], ident[:, :])
                elif n == 5:
                    pe.wait_ge(dact[l], act0 + 7)
                    r = nc.tensor.matmul(q[1], wX[:, 0, :], dX[l], start=True, stop=True)
                elif n == 6:
                    pe.wait_ge(dact[l], act0 + 8)
                    r = nc.tensor.matmul(q[0], wG[:, 1, :], dH[l], start=True, stop=True)
                elif n == 7:
                    pe.wait_ge(dact[l], act0 + 9)
                    for k in range(DR):
                        o = q[1][:, k * P:(k + 1) * P]
                        nc.tensor.matmul(o, dX[l][:, k * P:(k + 1) * P], center[:, :], start=True, stop=False)
                        r = nc.tensor.matmul(o, dA[l][:, k * P:(k + 1) * P], center[:, :], start=False, stop=True)
                else:
                    return
                r.then_inc(dpe[l], 1)

            at = [0]

            def dense_some(k):
                for i, n in order[at[0]:at[0] + k]:
                    dense(i, n)
                at[0] += k

            def pe_final(l, n, t, a):
                begin(l, n)
                for k in range(KB):
                    o = ps[l][0][:, k * P:(k + 1) * P]
                    nc.tensor.matmul(o, t[:, k * P:(k + 1) * P], center[:, :], start=True, stop=False)
                    r = nc.tensor.matmul(o, a[:, k * P:(k + 1) * P], center[:, :], start=False, stop=True)
                r.then_inc(pe_n[l], 1)

            turns = [0]

            def net_turn(t, w):
                turns[0] += 1
                pe.wait_ge(turn_rdy, turns[0])
                for a in range(0, w, P):
                    r = nc.tensor.transpose(pi[:, a:a + P], t[:, a:a + P], ident[:, :])
                r.then_inc(turned, 1)
                dense_some(FILL[0] if turns[0] <= 14 else FILL[2])

            def net_sort(h, top):
                cur, other = va, vb
                for k in range(1, top + 1):
                    if k == 16:
                        cur, other = other, cur
                    n1 = min(k, 15) - 8
                    if k > 8:
                        net_turn(cur, h * SC)
                        cur, other = (other, cur) if n1 % 2 == 0 else (cur, other)
                        net_turn(cur, h * SC)
                        cur, other = other, cur
                    elif k % 2:
                        cur, other = other, cur
                return cur

            small = [0]

            def small_wait():
                small[0] += 1
                pe.wait_ge(small_rdy, small[0])

            def index_tiles(arrays):
                small_wait()
                for o, t in enumerate(arrays):
                    for g in range(2):
                        r = nc.tensor.transpose(pi[:, 256 * o + 98 * g:256 * o + 98 * g + 98],
                                                t[0:98, g * P:(g + 1) * P], ident[0:98, 0:98])
                r.then_inc(small_mm, 1)

            def net_join():
                net_turn(va, SC)
                net_turn(va, SC)
                net_turn(va, 2 * SC)
                net_turn(va, 2 * SC)
                small_wait()
                nc.tensor.matmul(pi[:, 0:2], ltri[:, :], rs_c, start=True, stop=True)
                nc.tensor.matmul(pi[:, 2:3], shf[:, :], rs_c[:, 0:1], start=True, stop=True)
                for h in range(2):
                    r = nc.tensor.matmul(pi[0:1, 256 + h * P:256 + (h + 1) * P], rm_c[:, h:h + 1], ident[:, :], start=True, stop=True)
                r.then_inc(small_mm, 1)
                small_wait()
                for h in range(2):
                    r = nc.tensor.matmul(pi[:, 512 + h:513 + h], rowb[0:1, h * P:(h + 1) * P], ident[0:1, 0:1], start=True, stop=True)
                r.then_inc(small_mm, 1)

            pe.wait_ge(consts, N_CONST)
            net_sort(1, 15)
            index_tiles((t0, t1, t2))
            pe.wait_ge(idx_rdy, 1)
            pe.wait_ge(ready, 1)
            nc.tensor.matmul(pi[:, 0:P], wZ[:, 0, :], center[:, :], start=True, stop=True)
            nc.tensor.matmul(pi[:, 2 * P:2 * P + F], wtmp[:, :], center[:, 0:F], start=True, stop=True)
            nc.tensor.matmul(pi[:, P:P + 1], center[:, :], batt_c, start=True, stop=True).then_inc(wz_mm, 1)
            pe.wait_ge(ready, 2)
            for b in range(NB):
                dense_some(FILL[1])
            net_sort(1, 15)
            index_tiles((t0, t1, t2))
            net_join()
            net_sort(2, 16)
            index_tiles((t0, t2))
            dense_some(len(order))
            pe.wait_ge(idx_rdy, 3)
            pe.wait_ge(ready, 3)
            for l in range(DL):
                pe.wait_ge(dact[l], D_ACT * dense_blocks(l))
                pe.wait_ge(ddve[l], D_DVE * dense_blocks(l))

            def turn_in(s, rows):
                pe.wait_ge(gx[s], 16 * C * NT)
                for b in range(NB):
                    begin(b % 2, before["turn", s, b])
                    turn_tiles(b % 2, 0, lambda k: rows[:, b * W + k * P:b * W + (k + 1) * P])

            turn_in(1, D)

            shifts = [0]

            def carries(w):
                for i in range(C - 1):
                    if shifts[0]:
                        pe.wait_ge(cr_used, shifts[0])
                    shifts[0] += 1
                    pe.wait_ge(cr_rdy, shifts[0])
                    nc.tensor.matmul(pc[:, 0:1], w[:, :], ctmp, start=True, stop=True).then_inc(cr_mm, 1)
                pe.wait_ge(cr_used, shifts[0])

            for L in range(3):
                fb, bb = (T2, T1) if L == 1 else (T1, T2)
                if L == 1:
                    for b in range(NB):
                        l = b % 2
                        begin(l, before["score", b])
                        mm(ps[l][0], wSc[:, 0, :], blk(S, b), stop=False)
                        mm(ps[l][0], wSc[:, 1, :], blk(D, b), start=False).then_inc(pe_n[l], 1)
                    begin(1, before["msg", L, 1])
                    for w in (shf, shb, shf, shb):
                        carries(w)
                for b in range(NB):
                    l, n = b % 2, before["msg", L, b]
                    if L == 0:
                        begin(l, n)
                        pe.wait_ge(act_n[l], n.act + 1)
                        turn_tiles(l, 0, lambda k: HB[l][:, k * 64:(k + 1) * 64], 64)
                        for g in range(2):
                            o = ps[l][1 - g]
                            pe.wait_ge(act_n[l], n.act + 2)
                            mm(o, wA[:, g, :], blk(D, b), stop=False)
                            mm(o, wE[:, g, :], AB[l][0:64, :], start=False).then_inc(pe_n[l], 1)
                        pe.wait_ge(act_n[l], n.act + 4)
                        mm(ps[l][1], wB[:, 0, :], HB[l][:, :], stop=False)
                        mm(ps[l][1], wB[:, 1, :], X3[l][:, :], start=False).then_inc(pe_n[l], 1)
                    elif L == 1:
                        begin(l, n)
                        pe.wait_ge(att_rdy, b + 1)
                        for h in range(4):
                            if h:
                                pe.wait_ge(dve_n[l], n.dve + h)
                            mm(ps[l][0], wSel[:, h, :], blk(T1, b)).then_inc(pe_n[l], 1)
                            pe.wait_ge(dve_n[l], n.dve + h + 1)
                            mm(ps[l][1], wH[:, h, :], HB[l][:, :], start=(h == 0), stop=(h == 3)).then_inc(pe_n[l], 1)
                    elif L == 2:
                        begin(l, n)
                        pe.wait_ge(act_n[l], n.act + 1)
                        turn_tiles(l, 0, lambda k: HB[l][:, k * P:(k + 1) * P])
                begin(1, before["sums", L])
                carries(shf)
                for b in range(NB):
                    pe.wait_ge(fix_n, L * NB + b + 1)
                    pe_rows_out(b % 2, before["table", L, b], blk(fb, b))
                if L == 0:
                    turn_in(0, T2)
                begin(1, before["back", L])
                carries(shb)
                wa = wZ[:, 1, :] if L == 2 else center[:, :]
                for b in range(NB):
                    pe.wait_ge(tot_n, L * NB + b + 1)
                    pe_ln(b % 2, before["local", L, b], blk(S, b), blk(bb, b), wa)
                for b in range(NB):
                    pe_rows_in(b % 2, before["update", L, b])
                    pe_ln(b % 2, before["other", L, b], blk(D, b), AB[b % 2][:, :], wa)
            for b in range(NB):
                l = b % 2
                begin(l, before["to4", b])
                for u, t in enumerate((S, D)):
                    turn_tiles(l, u, lambda k: t[:, b * W + k * P:b * W + (k + 1) * P])
            for s, t in enumerate((S, D)):
                if s == 1:
                    for b in range(NB):
                        l, n = b % 2, before["from4", b]
                        begin(l, n)
                        pe.wait_ge(act_n[l], n.act + 2)
                        for v, rows in enumerate((HB[l], X3[l])):
                            turn_tiles(l, v, lambda k: rows[:, k * P:(k + 1) * P])
                    begin(1, before["sums", 3])
                    carries(shf)
                    carries(shb)
                for b in range(NB):
                    l, n = b % 2, before["last", s, b]
                    if s == 1:
                        pe.wait_ge(tot_n, 3 * NB + b + 1)
                    pe_mlp(l, n, 0, blk(t, b), blk(T2, b) if s else None)
                    pe_final(l, before["final", s, b], blk(t, b), AB[l])

        @block.vector
        def _(dve):
            v = nc.vector
            chain = [0]

            def link(i):
                chain[0] += 1
                i.then_inc(dchain, 1)
                dve.wait_ge(dchain, chain[0])

            for t in (wA, wE, wB, wH, wSc, wZ, wG):
                v.memset(t[:, :, :], 0.0)
            link(v.memset(RI[0][:, :], 0.0))
            dve.sem_inc(w_zero, 1)
            dve.wait_ge(consts, N_CONST)
            link(v.tensor_scalar(gray, index2, 1, None, ALU.logical_shift_right))
            link(v.tensor_tensor(gray, gray, index2, ALU.bitwise_xor))
            for k in range(1, 17):
                i, s = (index2, 1) if k == 1 else (gray, k - 1)
                link(v.tensor_scalar(t0.bitcast(I32), i, s, 1, ALU.logical_shift_right, ALU.bitwise_and))
                link(v.tensor_scalar(flips[:, k - 1, :], t0.bitcast(I32), -2.0, 1.0, ALU.mult, ALU.add))
            link(v.tensor_scalar(iop, index2[:, 0:SC], 1.0, None, ALU.add))

            def pack(field, low, o):
                link(v.tensor_copy(o.bitcast(I32), field))
                link(v.tensor_copy(low.bitcast(I32), low))
                link(v.tensor_scalar(o.bitcast(I32), o.bitcast(I32), 15, None, ALU.logical_shift_left))
                link(v.tensor_tensor(o.bitcast(I32), o.bitcast(I32), low.bitcast(I32), ALU.bitwise_or))

            def encode(key, pay, o, a, b):
                link(v.tensor_scalar(a, key, SPLIT, None, ALU.is_lt))
                link(v.tensor_scalar(b, key, -2.0, 181559.0, ALU.mult, ALU.add))
                link(v.tensor_tensor(b, b, a, ALU.mult))
                link(v.scalar_tensor_tensor(out=key, in0=key, scalar=-50744.0, in1=b, op0=ALU.add, op1=ALU.add))
                link(v.tensor_scalar(b, pay, -2.0, 32767.0, ALU.mult, ALU.add))
                link(v.tensor_tensor(b, b, a, ALU.mult))
                link(v.tensor_tensor(pay, pay, b, ALU.add))
                pack(key, pay, o)

            def field_of(bits, o):
                link(v.tensor_scalar(o.bitcast(I32), bits.bitcast(I32), 15, None, ALU.logical_shift_right))
                link(v.tensor_copy(o, o.bitcast(I32)))

            def decode(bits, field, low, a, b):
                field_of(bits, field)
                link(v.tensor_scalar(low.bitcast(I32), bits.bitcast(I32), 32767, None, ALU.bitwise_and))
                link(v.tensor_copy(low, low.bitcast(I32)))
                link(v.tensor_scalar(a, field, 65536.0, None, ALU.is_ge))
                link(v.tensor_scalar(b, low, -2.0, 32767.0, ALU.mult, ALU.add))
                link(v.tensor_tensor(b, b, a, ALU.mult))
                link(v.tensor_tensor(low, low, b, ALU.add))
                link(v.tensor_scalar(b, field, -2.0, 80071.0, ALU.mult, ALU.add))
                link(v.tensor_tensor(b, b, a, ALU.mult))
                link(v.scalar_tensor_tensor(out=field, in0=field, scalar=50744.0, in1=b, op0=ALU.add, op1=ALU.add))

            def to_row(pos, o, a):
                link(v.tensor_scalar(o, pos, 4.0, None, ALU.mult))
                for c in range(1, C):
                    link(v.tensor_scalar(a, pos, float(c * J), float(C * J - 1), ALU.is_ge, ALU.mult))
                    link(v.tensor_tensor(o, o, a, ALU.subtract))

            def dense(i, n):
                l, u = i % DL, i // DL
                A, H, X, q = dA[l], dH[l], dX[l], dP[l]
                act0, dve0 = D_ACT * u, D_DVE * u
                s_ = inv[:, l * 4 * DR:(l + 1) * 4 * DR]
                spread = s_.rearrange("p (m o) -> p m o", o=1).to_broadcast([P, C * DR, F])

                def by_row(t):
                    return t.rearrange("p (m f) -> p m f", f=F)

                def go(i_):
                    i_.then_inc(ddve[l], 1)

                if n == 0:
                    dve.wait_ge(dld[l], 16 * (u + 1))
                    if u:
                        dve.wait_ge(ddve[l], dve0)
                    go(v.tensor_reduce(s_, by_row(dR[l]), AXX, ALU.add))
                    dve.wait_ge(ddve[l], dve0 + 1)
                    go(v.scalar_tensor_tensor(out=by_row(A), in0=spread, scalar=-1.0 / F, in1=by_row(dR[l]), op0=ALU.mult, op1=ALU.add))
                elif n in (1, 3, 8):
                    dve.wait_ge(dact[l], act0 + {1: 1, 3: 4, 8: 10}[n])
                    go(v.tensor_reduce(s_, by_row(H), AXX, ALU.add))
                elif n == 2:
                    dve.wait_ge(dact[l], act0 + 3)
                    go(v.tensor_tensor(by_row(A), by_row(A), spread, ALU.mult))
                    dve.wait_ge(ddve[l], dve0 + 4)
                    go(v.tensor_tensor(by_row(A), by_row(A), cb_row[:, :].rearrange("p (o f) -> p o f", o=1).to_broadcast([P, C * DR, F]), ALU.add))
                elif n == 4:
                    dve.wait_ge(dact[l], act0 + 6)
                    go(v.tensor_tensor(by_row(A), by_row(A), spread, ALU.mult))
                elif n == 9:
                    dve.wait_ge(dact[l], act0 + 12)
                    go(v.tensor_tensor(by_row(X), by_row(q[1]), spread, ALU.mult))

            at, owed = [0], [0]

            def dense_some(k):
                for i, n in order[at[0]:at[0] + k]:
                    dense(i, n)
                at[0] += k

            turns = [0]

            def net_turn(cur, o, w):
                turns[0] += 1
                dve.sem_inc(turn_rdy, 1)
                dense_some(owed[0])
                owed[0] = FILL[0] if turns[0] <= 14 else FILL[2]
                dve.wait_ge(turned, turns[0])
                link(v.tensor_copy(o[:, 0:w], pi[:, 0:w]))

            def compare(i, o, w, s):
                a = i[:, 0:w].rearrange("p (g two s) -> p g two s", two=2, s=s)
                b = o[:, 0:w].rearrange("p (g two s) -> p g two s", two=2, s=s)
                v.tensor_tensor(b[:, :, 0, :], a[:, :, 0, :], a[:, :, 1, :], ALU.min)
                link(v.tensor_tensor(b[:, :, 1, :], a[:, :, 0, :], a[:, :, 1, :], ALU.max))
                if owed[0]:
                    dense_some(1)
                    owed[0] -= 1

            def merge_bits(cur, o, w, nbits):
                net_turn(cur, o, w)
                cur, o = o, cur
                for s in reversed(range(nbits)):
                    compare(cur, o, w, 2 ** s)
                    cur, o = o, cur
                net_turn(cur, o, w)
                cur, o = o, cur
                for s in reversed(range(8)):
                    compare(cur, o, w, 2 ** s)
                    cur, o = o, cur
                return cur, o

            def net_sort(h, top):
                w = h * SC
                cur, o = va, vb
                for k in range(1, top + 1):
                    link(v.tensor_tensor(cur[:, 0:w], cur[:, 0:w], flips[:, k - 1, 0:w], ALU.mult))
                    if k == 16:
                        v.tensor_tensor(o[:, 0:SC], cur[:, 0:SC], cur[:, SC:w], ALU.min)
                        link(v.tensor_tensor(o[:, SC:w], cur[:, 0:SC], cur[:, SC:w], ALU.max))
                        cur, o = o, cur
                    if k > 8:
                        cur, o = merge_bits(cur, o, w, min(k, 15) - 8)
                    else:
                        for s in reversed(range(k)):
                            compare(cur, o, w, 2 ** s)
                            cur, o = o, cur
                return cur

            small = [0]

            def small_mms():
                dense_some(owed[0])
                owed[0] = 0
                small[0] += 1
                dve.sem_inc(small_rdy, 1)
                dve.wait_ge(small_mm, small[0])

            dve.wait_ge(src_in, 16)
            key, pay = t0[:, 0:SC], t1[:, 0:SC]
            link(v.memset(key, PAD))
            link(v.tensor_scalar(key[0:EP, 0:ER], nat_src, 1000.0, None, ALU.add))
            link(v.memset(pay, 0.0))
            link(v.tensor_copy(pay[:, 0:C * NT], eid[:, :]))
            link(v.tensor_copy(pay[:, ER - 4:ER], frm[:, 0:4]))
            encode(key, pay, va[:, 0:SC], t2[:, 0:SC], t3[:, 0:SC])
            r = net_sort(1, 15)
            link(v.tensor_copy(srt[0], r[:, 0:SC]))
            dve.sem_inc(srt_rdy, 1)

            def after_sort(i, loads):
                dve.wait_ge(nb_in, 16 * loads)
                cur, prv, nxt = va[:, 0:196], va[:, 256:452], vb[:, 0:196]
                field_of(t2[:, 256:452], cur)
                field_of(t2[:, 0:196], prv)
                field_of(t3[:, 0:196], nxt)
                link(v.tensor_tensor(mask8[:, 0, :], cur, prv, ALU.is_equal))
                link(v.tensor_tensor(mask8[:, 1, :], cur, nxt, ALU.is_equal))
                dve.sem_inc(mask_rdy, 1)
                k, low, a, b = va[0:98, 0:SC], va[0:98, SC:2 * SC], vb[0:98, 0:SC], vb[0:98, SC:2 * SC]
                end = t3[0:98, 0:SC]
                field_of(t0[0:98, 0:SC], k)
                field_of(t1[0:98, 0:SC], a)
                link(v.tensor_tensor(end, k, a, ALU.not_equal))
                decode(t0[0:98, 0:SC], k, low, a, b)
                key, uniq, p_ = t0[0:98, 0:SC], t1[0:98, 0:SC], t2[0:98, 0:SC]
                link(v.tensor_scalar(key, k, -1000.0, None, ALU.add))
                link(v.tensor_scalar(uniq, key, -500000.0, None, ALU.add))
                link(v.tensor_tensor(uniq, uniq, end, ALU.mult))
                link(v.tensor_scalar(uniq, uniq, 500000.0, None, ALU.add))
                link(v.tensor_scalar(key, key, float(NODES - 1), None, ALU.min))
                if i == 0:
                    link(v.tensor_scalar(p_, low, float(EDGES - 1), None, ALU.min))
                else:
                    link(v.tensor_scalar(low, low, -1.0, 0.0, ALU.add, ALU.max))
                    to_row(low, p_, a)
                small_mms()

            after_sort(0, 5)
            v.tensor_copy(sG[:, :], pi[:, 0:196])
            v.tensor_copy(sU[:, :], pi[:, 256:452])
            link(v.tensor_copy(eI[:, :], pi[:, 512:708]))
            dve.sem_inc(idx_rdy, 1)

            dve.wait_ge(w_in, 16 * NW)
            v.memset(eps_c, EPS)
            v.memset(eps2_c, EPS * EPS)
            v.tensor_tensor(center[:, :], ident[:, :], mean[:, :], ALU.subtract)
            v.memset(shf[:, :], 1.0)
            for h in range(4):
                for c in range(C):
                    q = slice(F * c, F * c + F)
                    v.tensor_scalar(wH[q, h, q], wat[q, F * h:F * h + F], 0.25, None, ALU.mult)
                link(v.tensor_copy(wSel[:, h, :].rearrange("p (c f) -> p c f", f=F),
                                   ident[:, :].rearrange("p (c f) -> p c f", f=F)[:, :, h:h + 1].to_broadcast([P, C, F])))
            for s in range(2):
                link(v.tensor_tensor(wtmp[:, :].rearrange("p (h o) -> p h o", h=4), wat[:, :].rearrange("p (h o) -> p h o", h=4),
                                     fcr[:, s * F:(s + 1) * F].rearrange("p (h o) -> p h o", h=1).to_broadcast([P, 4, F]), ALU.mult))
                link(v.tensor_reduce(inv[:, 0:4], wtmp[:, :].rearrange("p (h o) -> p h o", h=4), AXX, ALU.add))
                for c in range(C):
                    q = slice(F * c, F * c + F)
                    link(v.tensor_copy(wSc[q, s, F * c:F * c + 4], inv[q, 0:4]))
            link(v.tensor_scalar(eps_g, eps_g, 1.0, None, ALU.add))
            for g in range(GINE):
                link(v.tensor_scalar(wX[:, g, :], wG[:, 2 * g, :], eps_g[:, g:g + 1], None, ALU.mult))
            link(v.tensor_copy(wtmp[:, :], batt_c.to_broadcast([P, P])))
            link(v.memset(shb[:, :], 0.0))
            link(v.tensor_copy(shb[:, 0:P - F], ident[:, F:P]))
            dve.sem_inc(ready, 1)
            dve.wait_ge(wz_mm, 1)
            v.tensor_copy(wZ[:, 1, :], pi[:, 0:P])
            v.tensor_copy(cb_row[:, :], pi[:, 2 * P:2 * P + F])
            link(v.tensor_copy(cb_c, pi[:, P:P + 1]))
            dve.sem_inc(ready, 1)

            def read_masks(i):
                dve.wait_ge(mask_in, 16 * 2 * C * (i + 1))
                link(v.memset(NE[P - F:P, J - 1:J], 0.0))
                v.tensor_tensor_scan(PF[:, :], NS[:, :], NS[:, :], 1.0, ALU.mult, ALU.min)
                link(v.tensor_tensor_scan(QB[:, ::-1], NE[:, ::-1], NE[:, ::-1], 1.0, ALU.mult, ALU.min))

            read_masks(0)

            dense_some(owed[0])
            owed[0] = 0
            dstf = home[:, :].bitcast(F32)
            for b in range(NB):
                dve.wait_ge(ga[b % 2], 16 * C * KB * (uses(b) + 1))
                v.tensor_copy(dstf.rearrange("p (c k) -> p k c", c=C)[:, b * KB:(b + 1) * KB, :],
                              att_buf[b % 2].rearrange("p (k c w) -> p k c w", k=KB, c=C)[:, :, :, ATT - 1]).then_inc(dcol, 1)
                dense_some(FILL[1])
            dve.wait_ge(dcol, NB)
            v.tensor_copy(dG[:, :], dstf).then_inc(dcol, 1)
            dve.wait_ge(dcol, NB + 1)

            link(v.memset(key, PAD))
            link(v.tensor_scalar(key[:, 0:C * NT], dstf, 1000.0, None, ALU.add))
            last = key[:, C * NT - 1:C * NT]
            link(v.tensor_scalar(spare, pos1[:, C * NT - 1:C * NT], float(EDGES), None, ALU.is_gt))
            link(v.tensor_scalar(ctmp, last, -1.0, PAD, ALU.mult, ALU.add))
            link(v.tensor_tensor(ctmp, ctmp, spare, ALU.mult))
            link(v.tensor_tensor(last, last, ctmp, ALU.add))
            link(v.memset(pay, 0.0))
            link(v.tensor_copy(pay[:, 0:C * NT], pos1[:, :]))
            encode(key, pay, va[:, 0:SC], t2[:, 0:SC], t3[:, 0:SC])
            r = net_sort(1, 15)
            link(v.tensor_copy(srt[1], r[:, 0:SC]))
            dve.sem_inc(srt_rdy, 1)
            after_sort(1, 10)
            v.tensor_copy(dUI[:, :], pi[:, 256:452])
            link(v.tensor_copy(jI[:, :], pi[:, 512:708]))
            dve.sem_inc(idx_rdy, 1)

            def net_join(tab, query, i, loads):
                x0 = t0[:, 0:SC]
                link(v.tensor_scalar(t1[:, 0:SC].bitcast(I32), tab.bitcast(I32), 31, 32767, ALU.arith_shift_right, ALU.bitwise_and))
                link(v.tensor_scalar(x0.bitcast(I32), tab.bitcast(I32), 15, None, ALU.logical_shift_right))
                link(v.tensor_scalar(x0.bitcast(I32), x0.bitcast(I32), 15, None, ALU.logical_shift_left))
                link(v.tensor_tensor(x0.bitcast(I32), x0.bitcast(I32), t1[:, 0:SC].bitcast(I32), ALU.bitwise_or))
                link(v.tensor_copy(va[:, 0:SC], query[:, ::-1]))
                net_turn(va, vb, SC)
                link(v.tensor_copy(va[:, 0:P], vb[:, 0:P][:, ::-1]))
                link(v.tensor_copy(va[:, P:SC], vb[:, P:SC][:, ::-1]))
                net_turn(va, vb, SC)
                v.tensor_tensor(va[:, 0:SC], x0, vb[:, 0:SC], ALU.min)
                link(v.tensor_tensor(va[:, SC:2 * SC], x0, vb[:, 0:SC], ALU.max))
                cur, o = merge_bits(va, vb, 2 * SC, 7)
                k, low = t0, t1
                decode(cur, k, low, o, t3)
                link(v.tensor_scalar(t2, low, 0.0, None, ALU.is_equal))
                link(v.tensor_scalar(cur, k, 1.0, None, ALU.add))
                link(v.tensor_tensor(cur, cur, t2, ALU.mult))
                link(v.tensor_scalar(cur, cur, -1.0, None, ALU.add))
                for h in range(2):
                    q = slice(h * SC, (h + 1) * SC)
                    link(v.tensor_tensor_scan(o[:, q], t2[:, q], t2[:, q], 0.0, ALU.add, ALU.max))
                    link(v.tensor_tensor_scan(t3[:, q], cur[:, q], cur[:, q], -1.0, ALU.max, ALU.max))
                    v.tensor_copy(rs_c[:, h:h + 1], o[:, (h + 1) * SC - 1:(h + 1) * SC])
                    link(v.tensor_copy(rm_c[:, h:h + 1], t3[:, (h + 1) * SC - 1:(h + 1) * SC]))
                small_mms()
                link(v.tensor_copy(cy_c, pi[:, 0:2]))
                link(v.tensor_tensor(cy_c[:, 1:2], cy_c[:, 1:2], pi[:, 2:3], ALU.add))
                link(v.memset(rowb[0:1, 0:1], -1.0))
                link(v.tensor_copy(cur[0:1, 0:2 * P], pi[0:1, 256:512]))
                link(v.tensor_tensor_scan(rowb[0:1, 1:2 * P + 1], cur[0:1, 0:2 * P], cur[0:1, 0:2 * P], -1.0, ALU.max, ALU.max))
                small_mms()
                link(v.tensor_copy(rm_c, pi[:, 512:514]))
                for h in range(2):
                    q = slice(h * SC, (h + 1) * SC)
                    link(v.tensor_scalar(o[:, q], o[:, q], cy_c[:, h:h + 1], -1.0, ALU.add, ALU.add))
                    link(v.tensor_scalar(t3[:, q], t3[:, q], rm_c[:, h:h + 1], None, ALU.max))
                link(v.tensor_tensor(t3, t3, k, ALU.is_equal))
                link(v.scalar_tensor_tensor(out=t3, in0=t2, scalar=0.0, in1=t3, op0=ALU.is_equal, op1=ALU.mult))
                link(v.scalar_tensor_tensor(out=t2, in0=k, scalar=105000.0, in1=t3, op0=ALU.is_lt, op1=ALU.mult))
                link(v.tensor_scalar(low, low, -1.0, None, ALU.add))
                to_row(low, t0, t3)
                to_row(o, cur, t3)
                link(v.tensor_scalar(t0, t0, 256.0 - 60000.0, None, ALU.add))
                link(v.tensor_tensor(t0, t0, t2, ALU.mult))
                link(v.tensor_scalar(t0, t0, 60000.0, None, ALU.add))
                link(v.tensor_scalar(t1, cur, -FAR, None, ALU.add))
                link(v.tensor_tensor(t1, t1, t2, ALU.mult))
                link(v.tensor_scalar(t1, t1, FAR, None, ALU.add))
                pack(t0, t1, va)
                r = net_sort(2, 16)
                link(v.tensor_copy(t0[:, 0:SC], r[:, 0:SC]))
                dve.sem_inc(srt_rdy, 1)
                dve.wait_ge(nb_in, 16 * loads)
                bits = t1[0:98, 0:SC]
                field_of(bits, t0[0:98, 0:SC])
                link(v.tensor_scalar(t0[0:98, 0:SC], t0[0:98, 0:SC], -256.0, None, ALU.add))
                link(v.tensor_scalar(t2[0:98, 0:SC].bitcast(I32), bits.bitcast(I32), 32767, None, ALU.bitwise_and))
                link(v.tensor_copy(t2[0:98, 0:SC], t2[0:98, 0:SC].bitcast(I32)))
                small_mms()
                v.tensor_copy(home[:, :], pi[:, 0:196])
                link(v.tensor_copy(frm[:, :], pi[:, 256:452]))
                dve.sem_inc(idx_rdy, 1)

            net_join(srt[0], srt[1], 0, 11)
            link(v.memset(shf[:, :], 0.0))
            link(v.tensor_copy(shf[:, F:P], ident[:, 0:P - F]))
            dve.sem_inc(ready, 1)
            dense_some(len(order))

            def one(i, l):
                i.then_inc(dve_n[l], 1)

            def ln_out(l, n, o, shift):
                dve.wait_ge(act_n[l], n.act + 3)
                one(v.scalar_tensor_tensor(out=o, in0=ps[l][0][:, 0:W], scalar=shift, in1=HB[l][:, :],
                                           op0=ALU.add, op1=ALU.mult), l)

            def mlp_out(l, n, g, o):
                dve.wait_ge(pe_n[l], n.pe + 2)
                one(v.tensor_scalar(o, ps[l][1][:, 0:W], bg_c[:, 2 * g + 1:2 * g + 2], 0.0, ALU.add, ALU.max), l)

            shifts = [0]

            def carries(end, prod, largest):
                for i in range(C - 1):
                    if i == 0:
                        link(v.tensor_copy(ctmp, end))
                    elif largest:
                        link(v.tensor_scalar(spare, prod, -NEG, NEG, ALU.mult, ALU.add))
                        link(v.tensor_tensor(spare, spare, carry, ALU.add))
                        link(v.tensor_tensor(ctmp, spare, end, ALU.max))
                    else:
                        link(v.scalar_tensor_tensor(out=ctmp, in0=prod, scalar=carry, in1=end, op0=ALU.mult, op1=ALU.add))
                    shifts[0] += 1
                    dve.sem_inc(cr_rdy, 1)
                    dve.wait_ge(cr_mm, shifts[0])
                    link(v.tensor_copy(carry, pc[:, 0:1]))
                    dve.sem_inc(cr_used, 1)

            def scan_block(o, i, mask, b, back):
                d = slice(None, None, -1) if back else slice(None)
                first = b == (NB - 1 if back else 0)
                at = (b + 1) * W if back else b * W - 1
                link(v.tensor_tensor_scan(blk(o, b)[:, d], blk(mask, b)[:, d], blk(i, b)[:, d],
                                          0.0 if first else o[:, at:at + 1], ALU.mult, ALU.add))

            def max_block(o, i, mask, b, back):
                d = slice(None, None, -1) if back else slice(None)
                first = b == (NB - 1 if back else 0)
                at = (b + 1) * W if back else b * W - 1
                link(v.tensor_scalar(X3[0][:, :], blk(mask, b), -NEG, NEG, ALU.mult, ALU.add))
                link(v.tensor_tensor_scan(blk(o, b)[:, d], X3[0][:, d], blk(i, b)[:, d],
                                          NEG if first else o[:, at:at + 1], ALU.add, ALU.max))

            def max_fix(o, prod, b):
                link(v.tensor_scalar(X3[0][:, :], blk(prod, b), -NEG, NEG, ALU.mult, ALU.add))
                link(v.scalar_tensor_tensor(out=blk(o, b), in0=X3[0][:, :], scalar=carry, in1=blk(o, b), op0=ALU.add, op1=ALU.max))

            def sum_fix(o, prod, b):
                return v.scalar_tensor_tensor(out=blk(o, b), in0=blk(prod, b), scalar=carry, in1=blk(o, b),
                                              op0=ALU.mult, op1=ALU.add)

            def back_sums(o, i):
                for b in reversed(range(NB)):
                    link(v.scalar_tensor_tensor(out=blk(o, b), in0=blk(NE, b), scalar=0.0, in1=blk(i, b),
                                                op0=ALU.is_equal, op1=ALU.mult))
                    scan_block(o, o, NE, b, True)
                carries(o[:, 0:1], QB[:, 0:1], False)

            def finals(s, t):
                for b in range(NB):
                    l = b % 2
                    mlp_out(l, before["last", s, b], 0, AB[l][:, :])
                    n = before["final", s, b]
                    s_ = inv[:, l * KB * C:(l + 1) * KB * C]
                    dve.wait_ge(act_n[l], n.act + 1)
                    one(v.tensor_reduce(s_, HB[l][:, :].rearrange("p (m f) -> p m f", f=F), AXX, ALU.add), l)
                    dve.wait_ge(act_n[l], n.act + 3)
                    one(v.tensor_tensor(blk(t, b).rearrange("p (m f) -> p m f", f=F), ps[l][0][:, 0:W].rearrange("p (m f) -> p m f", f=F),
                                        s_.rearrange("p (m o) -> p m o", o=1).to_broadcast([P, KB * C, F]), ALU.mult), l)

            for L in range(4):
                fb, bb = (T2, T1) if L == 1 else (T1, T2)
                if L == 1:
                    for b in range(NB):
                        l, n = b % 2, before["score", b]
                        dve.wait_ge(act_n[l], n.act + 1)
                        one(v.scalar_tensor_tensor(out=blk(T1, b), in0=AB[l][:, :], scalar=0.2, in1=AB[l][:, :],
                                                   op0=ALU.mult, op1=ALU.max), l)
                    for l in range(2):
                        n = before["score", NB - 2 + (l + NB) % 2]
                        dve.wait_ge(dve_n[l], n.dve + 1)
                    for b in range(NB):
                        max_block(T2, T1, NS, b, False)
                    carries(T2[:, J - 1:J], PF[:, J - 1:J], True)
                    for b in range(NB):
                        max_fix(T2, PF, b)
                    for b in reversed(range(NB)):
                        max_block(T2, T2, NE, b, True)
                    carries(T2[:, 0:1], QB[:, 0:1], True)
                    for b in range(NB):
                        max_fix(T2, QB, b)
                        v.tensor_tensor(blk(T1, b), blk(T1, b), blk(T2, b), ALU.subtract).then_inc(e_rdy, 1)
                    for b in range(NB):
                        dve.wait_ge(e_exp, b + 1)
                        scan_block(T2, T1, NS, b, False)
                    carries(T2[:, J - 1:J], PF[:, J - 1:J], False)
                    for b in range(NB):
                        link(sum_fix(T2, PF, b))
                    back_sums(T2, T2)
                    for b in range(NB):
                        link(sum_fix(T2, QB, b))
                        link(v.reciprocal(blk(T2, b), blk(T2, b)))
                        v.tensor_tensor(blk(T1, b), blk(T1, b), blk(T2, b), ALU.mult).then_inc(att_rdy, 1)
                for b in range(NB):
                    l, n = b % 2, before["msg", L, b] if L < 3 else None
                    if L == 0:
                        dve.wait_ge(pe_n[l], n.pe + 4)
                        one(v.tensor_scalar(blk(T1, b), ps[l][1][:, 0:W], b2a_c, None, ALU.add), l)
                        dve.wait_ge(dve_n[l], n.dve + 1)
                    elif L == 1:
                        for h in range(4):
                            dve.wait_ge(pe_n[l], n.pe + 2 * h + 1)
                            one(v.tensor_tensor(HB[l][:, :], blk(D, b), ps[l][0][:, 0:W], ALU.mult), l)
                        dve.wait_ge(pe_n[l], n.pe + 8)
                        one(v.tensor_copy(blk(T2, b), ps[l][1][:, 0:W]), l)
                        dve.wait_ge(dve_n[l], n.dve + 5)
                    elif L == 2:
                        dve.wait_ge(pe_n[l], n.pe + 1)
                        one(v.tensor_tensor(blk(T1, b), blk(D, b), ps[l][0][:, 0:W], ALU.mult), l)
                        dve.wait_ge(dve_n[l], n.dve + 1)
                    else:
                        dve.wait_ge(act_n[l], before["from4", b].act + 3)
                    scan_block(fb, fb, NS, b, False)
                carries(fb[:, J - 1:J], PF[:, J - 1:J], False)
                for b in range(NB):
                    sum_fix(fb, PF, b).then_inc(fix_n, 1)
                dve.wait_ge(fix_n, (L + 1) * NB)
                if L == 0:
                    for l in range(2):
                        dve.wait_ge(pe_n[l], before["turn", 0, NB - 2 + (l + NB) % 2].pe + 1)
                back_sums(bb, fb)
                for b in range(NB):
                    sum_fix(bb, QB, b).then_inc(tot_n, 1)
                if L == 3:
                    break
                shift = cb_c if L == 1 else zero_c
                for name, t in (("local", S), ("other", D)):
                    for b in range(NB):
                        ln_out(b % 2, before[name, L, b], blk(t, b), shift)
                for l in range(2):
                    dve.wait_ge(dve_n[l], before["other", L, NB - 2 + (l + NB) % 2].dve + 1)
                if L == 2:
                    for b in range(NB):
                        l, n = b % 2, before["to4", b]
                        dve.wait_ge(pe_n[l], n.pe + 1)
                        if b >= 2:
                            dve.wait_ge(r4_out[l], 16 * uses(b))
                        dve.wait_ge(ra_in, 16 * (2 * NB + b + 1))
                        one(v.tensor_tensor(r4_buf[l].rearrange("p (m w) -> p m w", w=ROW4)[:, :, 0:F],
                                            ps[l][0][:, 0:W].rearrange("p (m f) -> p m f", f=F),
                                            RA[:, :].rearrange("p (m w) -> p m w", w=ATT)[:, :, 16:16 + F], ALU.add), l)
                    finals(0, S)
                    read_masks(1)
            finals(1, D)


def kernel(**inputs):
    import numpy as _np
    import concourse.bacc as _bacc
    from concourse import mybir as _mybir
    from concourse.bass_utils import run_bass_kernel_spmd as _run

    a = {k: _np.asarray(v) for k, v in inputs.items()}
    gine = _np.stack([a["L3_gnn_W1"], a["L3_gnn_W2"]], axis=1).reshape(2 * 5, 32, 32)
    laid = [
        ("x", a["x"]), ("src", a["src"]), ("dst", a["dst"]), ("ea16", a["edge_attr_16"]), ("ea32", a["edge_attr_32"]),
        ("ew", a["edge_weight"]), ("w1a", a["L0_gnn_W1"]), ("b1a", a["L0_gnn_b1"]), ("w2a", a["L0_gnn_W2"]),
        ("b2a", a["L0_gnn_b2"]), ("watt", a["L1_gnn_w"].transpose(1, 0, 2)), ("fcw", a["L1_gnn_fc_w"]),
        ("fcb", a["L1_gnn_fc_b"]), ("batt", a["L1_gnn_bias"]), ("wz", a["L2_gnn_weight"]),
        ("wzt", a["L2_gnn_weight"].T), ("eps", a["L3_gnn_eps"]), ("wg", gine.transpose(2, 0, 1)),
        ("bg", _np.stack([a["L3_gnn_b1"], a["L3_gnn_b2"]], axis=1).reshape(10, 32).T),
    ]
    nc = _bacc.Bacc("TRN2", target_bir_lowering=False, num_devices=1)
    arrays, args = {}, []
    for name, v in laid:
        v = _np.ascontiguousarray(v)
        arrays[f"in_{name}"] = v
        args.append(nc.dram_tensor(f"in_{name}", v.shape, _mybir.dt.from_np(v.dtype), kind="ExternalInput").ap())
    args.append(nc.dram_tensor("out_0", (NODES, F), F32, kind="ExternalOutput").ap())
    build(nc, *args)
    r = _run(nc, [arrays], core_ids=[0])
    return r.results[0]["out_0"]
```

```python
from contextlib import ExitStack

import concourse.bass as bass
from concourse import mybir

F32 = mybir.dt.float32
I32 = mybir.dt.int32
U8 = mybir.dt.uint8
I8 = mybir.dt.int8
BF16 = mybir.dt.bfloat16
ALU = mybir.AluOpType
ACT = mybir.ActivationFunctionType
AXX = mybir.AxisListType.X

P = 128
NODES, EDGES, F = 100000, 25000, 32
C = P // F
NT = -(-EDGES // (C * P))
J = NT * P
ROWS = C * J
KB = 7
NB = NT // KB
W = KB * P
SUB = 8
SW = J // SUB
HEADS = 4
PARTS = 3
HALF = 32768
SC = HALF // P
EP, ER = 125, 200
ATT = 16 + 32 + 1 + 1
ROW4 = 2 * F
NEG = -1.0e30
EPS = 1e-5
SPLIT, PAD, FAR = 51000.0, 110000.0, 30000.0
HID = 64
GINE = 1
LAST_GINE = 4
DJ = NODES // C
DW = 512
DR = DW // P
ND = -(-DJ // DW)
EARLY = 4
DL = 3
BG = 7
NW = 9 * C + 5
N_CONST = 12
assert SUB * HEADS == F and SW * SUB == J and NT % KB == 0 and ROWS % (P * BG) == 0


STEPS = {
    "turn_in": (1, 1, 0, 0, 0), "ln_rows": (2, 3, 1, 1, 0), "rows_out": (1, 1, 0, 0, 1), "ln": (2, 3, 1, 0, 0),
    "mlp": (2, 1, 1, 0, 0), "edge": (4, 4, 1, 0, 0), "score": (1, 1, 0, 0, 0), "attend": (8, 0, 5, 0, 0),
    "scale": (1, 1, 1, 0, 0), "to_row4": (2, 2, 1, 0, 0), "from_row4": (2, 4, 0, 0, 0), "final": (1, 3, 2, 0, 0),
}


D_PE, D_ACT, D_DVE, D_STEPS = 4, 12, 9, 10


def dense_order():
    order = []
    for k in range(D_STEPS * (-(-ND // DL)) + 6):
        for lane in range(DL):
            u, n = divmod(k - 3 * lane, D_STEPS)
            if u >= 0 and DL * u + lane < ND:
                order.append((DL * u + lane, n))
    return order


FILL = (0, 50, 5)


class Count:

    def __init__(self, pe=0, act=0, dve=0, load=0, store=0):
        self.pe, self.act, self.dve, self.load, self.store = pe, act, dve, load, store


def count_steps():
    before, now = {}, [(0,) * 5, (0,) * 5]

    def step(lane, kind, *key):
        assert key not in before
        before[key] = Count(*now[lane])
        now[lane] = tuple(a + b for a, b in zip(now[lane], STEPS[kind]))

    for b in range(NB):
        step(b % 2, "turn_in", "turn", 1, b)
    for L in range(3):
        if L == 1:
            step(0, "score", "score", 0)
        for b in range(SUB if L == 1 else NB):
            step(b % 2, ("edge", "attend", "scale")[L], "msg", L, b)
        before["sums", L] = Count(*now[1])
        for b in range(NB):
            step(b % 2, "rows_out", "table", L, b)
        if L == 0:
            for b in range(NB):
                step(b % 2, "turn_in", "turn", 0, b)
        before["back", L] = Count(*now[1])
        for b in range(NB):
            step(b % 2, "ln", "local", L, b)
        if L == 2:
            for b in range(NB):
                step(b % 2, "mlp", "last", 0, b)
                step(b % 2, "final", "final", 0, b)
        for b in range(NB):
            step(b % 2, "ln_rows", "other", L, b)
            if L == 2:
                step(b % 2, "to_row4", "to4", b)
    for b in range(NB):
        step(b % 2, "from_row4", "from4", b)
    before["sums", 3] = before["back", 3] = Count(*now[1])
    for b in range(NB):
        step(b % 2, "mlp", "last", 1, b)
        step(b % 2, "final", "final", 1, b)
    return before, now


def build(nc, x, src, dst, ea16, ea32, ew, w1a, b1a, w2a, b2a, watt, fcw, fcb, batt, wzt, eps, wg, bg, out):
    ctx = ExitStack()
    with ctx:
        def sb(name, shape, dt=F32):
            return ctx.enter_context(nc.sbuf_tensor(name, shape, dt))

        def sem(name):
            return ctx.enter_context(nc.semaphore(name))

        def dram(name, shape, dt=F32):
            return nc.dram_tensor(name, shape, dt, kind="Internal").ap()

        attN = dram("attN", (EDGES, ATT))
        attS = dram("attS", (ROWS, ATT))
        row4 = dram("row4", (ROWS, ROW4))
        table = dram("table", (ROWS, F))
        upd = dram("upd", (ROWS, F))
        att_d = dram("att_parts", (P, PARTS, SW), BF16)
        sorted_d = [dram(f"sorted{i}", (HALF + 2, 1)) for i in range(2)]
        list_d = dram("list", (HALF, 1))
        mask_d = [dram(f"mask{i}", (2, ROWS), U8) for i in range(2)]

        big = sb("big", [P, 4 * J])
        S, D, T1, T2 = (big[:, i * J:(i + 1) * J] for i in range(4))
        rest = sb("rest", [P, J])
        final_s = rest[:, :]
        at = [0]

        def part(n):
            a = rest[:, at[0]:at[0] + n]
            at[0] += n
            assert at[0] <= J
            return a

        flips = part(16 * 2 * SC // 4).bitcast(I8).rearrange("p (k w) -> p k w", k=16)
        va, vb, t0, t1, t2, t3 = (part(2 * SC) for _ in range(6))
        srt = [part(SC), part(SC)]
        iop = part(SC)
        nat32, nat16, nat_w = big[0:EP, 0:6400], big[0:EP, 6400:9600], big[0:EP, 9600:9800]
        nat_dst, nat_src = (big[0:EP, a:a + 200].bitcast(I32) for a in (9800, 10000))
        index2, gray = (big[:, a:a + 2 * SC].bitcast(I32) for a in (10240, 10752))
        nat_att = big[0:EP, 2 * J:2 * J + ER * ATT]
        NS, NE, PF, QB = (sb(n, [P, J], U8) for n in ("not_start", "not_end", "first_seg", "last_seg"))
        RI = [sb(f"rows{i}", [P, W]) for i in range(2)]
        AB = [sb(f"arg{i}", [P, W]) for i in range(2)]
        HB = [sb(f"hid{i}", [P, W]) for i in range(2)]
        X3 = [sb(f"res{i}", [P, W]) for i in range(2)]
        RA = sb("edge_rows", [P, KB * C * ATT])
        mask8 = RA[:, 0:98].bitcast(U8).rearrange("p (m f) -> p m f", m=2)
        G = [RA[:, i * BG * F:(i + 1) * BG * F] for i in range(4)]
        ident = sb("ident", [P, P])
        center = sb("center", [P, P])
        mean = sb("mean", [P, P])
        shf = sb("shf", [P, P])
        shb = sb("shb", [P, P])
        ltri = part(P)
        wA = sb("wA", [P, 2, P])
        wE = sb("wE", [64, 2, P])
        wB = sb("wB", [P, 2, P])
        wH = sb("wH", [P, 4, P])
        wSc = rest[:, 0:2 * SUB * P].rearrange("p (s q m) -> p s q m", s=2, q=SUB)
        wSel = rest[0:PARTS * C * HEADS, 2 * SUB * P:2 * SUB * P + HEADS * P // 2].bitcast(BF16).rearrange("p (h m) -> p h m", h=HEADS)
        marks = rest[0:PARTS * C * HEADS, 3 * SUB * P:3 * SUB * P + C * HEADS]
        proj = sb("proj", [P, 2 * HEADS])
        e32, hm, hmt = sb("piece_marks", [P, F]), sb("head_marks", [P, HEADS]), sb("head_rows", [HEADS, P])
        ends, run = sb("ends", [P, 2 * F]), sb("running", [HEADS, 3 * F + 1])
        wZ = sb("wZ", [P, 2, P])
        wG = sb("wG", [P, 2 * GINE, P])
        wX = sb("wX", [P, GINE, P])
        cols = sb("cols", [P, 32])
        zero_c, eps_c, cb_c, fcb_c, b1a_c, b2a_c, batt_c = (cols[:, i:i + 1] for i in range(7))
        carry, ctmp, spare, eps2_c = (cols[:, i:i + 1] for i in range(7, 11))
        bg_c = cols[:, 11:11 + 2 * GINE]
        eps_g = cols[:, 21:21 + GINE]
        rs_c = cols[:, 26:28]
        cy_c = cols[:, 28:30]
        rm_c = cols[:, 30:32]
        fcr = sb("fcr", [P, 2 * F])
        cb_row = sb("cb_row", [P, F])
        wat = sb("wat", [P, 4 * F])
        wtmp = part(4 * F)
        packed = X3[0][:, 0:SW].bitcast(U8).rearrange("p (m w) -> p m w", m=4)
        ns8, ne8, pf8, qb8 = (packed[:, m, :] for m in range(4))
        sc_, mx_, tm_, sm_ = (T1[:, m * SW:(m + 1) * SW] for m in range(4))
        cut = T1[:, SW:SW + PARTS * SW // 2].bitcast(BF16).rearrange("p (a w) -> p a w", a=PARTS)
        parts = T1[0:PARTS * C * HEADS, 4 * SW:4 * SW + SUB * SW // 2].bitcast(BF16).rearrange("p (k w) -> p k w", k=SUB)
        rowb = X3[0][0:1, 0:2 * P + 1]
        sG, dG, jI = (sb(n, [P, C * NT], I32) for n in ("src_id", "dst_id", "src_row"))
        sU = sb("src_end", [P, C * NT], I32)
        dUI = sb("dst_end", [P, C * NT], I32)
        home, frm = sb("home", [P, C * NT], I32), sb("from", [P, C * NT], I32)
        pos1, eid = sb("position", [P, C * NT], I32), sb("edge_id", [P, C * NT], I32)
        eI = frm

        ps = [[ctx.enter_context(nc.psum_tensor(f"ps{l}{u}", [P, 1024], F32)) for u in range(2)] for l in range(2)]
        pi = ps[1][1]
        pc = ps[1][1][:, W:W + P]
        dR, dA, dH, dX = ([S[:, (4 * l + i) * DW:(4 * l + i + 1) * DW] for l in range(DL)] for i in range(4))
        dP = [[(ps[0][0], ps[0][1], ps[1][0])[l][:, u * DW:(u + 1) * DW] for u in range(2)] for l in range(DL)]
        inv = sb("inverse", [P, max(DL * 4 * DR, 2 * KB * C)])

        consts = sem("consts")
        w_zero = sem("weights_cleared")
        w_in = sem("weights_in")
        src_in = sem("src_in")
        nat_in = sem("natural_in")
        nat_rows = sem("natural_rows")
        attn_out = sem("attn_out")
        ready = sem("weights_ready")
        wz_mm = sem("wz_mm")
        turn_rdy, turned = sem("turn_ready"), sem("turned")
        small_rdy, small_mm = sem("small_ready"), sem("small_mm")
        dchain = sem("dve_chain")
        srt_rdy = sem("sorted_ready")
        srt_out = sem("sorted_out")
        nb_in = sem("neighbours_in")
        pieces_in = sem("pieces_in")
        mask_rdy, mask_out, mask_in = sem("mask_ready"), sem("mask_out"), sem("mask_in")
        idx_rdy = sem("index_ready")
        pool_ok = sem("pool_chain")
        ga = [sem("att_rows0"), sem("att_rows1")]
        dcol = sem("dst_col")
        atts_out = [sem("atts_out0"), sem("atts_out1")]
        gx = [sem("x_src_rows"), sem("x_dst_rows")]
        pe_n = [sem("pe_lane0"), sem("pe_lane1")]
        act_n = [sem("act_lane0"), sem("act_lane1")]
        dve_n = [sem("dve_lane0"), sem("dve_lane1")]
        ld_n = [sem("load_lane0"), sem("load_lane1")]
        st_n = [sem("store_lane0"), sem("store_lane1")]
        ra_in = sem("edge_rows_in")
        dpe, dact, ddve, dld, dst_ = ([sem(f"dense_{n}{l}") for l in range(DL)] for n in ("pe", "act", "dve", "load", "store"))
        e_rdy, e_exp = sem("exp_ready"), sem("exp_done")
        att_rdy, parts_out, parts_in = sem("att_ready"), sem("att_parts_out"), sem("att_parts_in")
        fix_n = sem("prefix_ready")
        tot_n = sem("total_ready")
        cr_rdy, cr_mm, cr_used = sem("carry_ready"), sem("carry_shifted"), sem("carry_used")
        gs = [sem(f"picked_in{i}") for i in range(C * NT // BG)]
        ss = [sem(f"put_out{i}") for i in range(C * NT // BG)]
        upd_n = sem("updates_out")
        zeroed = sem("zeroed")
        r4_out = [sem("row4_out0"), sem("row4_out1")]
        table_out = sem("table_out")
        g4 = [sem("row4_in0"), sem("row4_in1")]
        fin = sem("final_put")

        block = ctx.enter_context(nc.Block())

        def blk(t, b, w=W):
            return t[:, b * w:(b + 1) * w]

        def rows128(t, b):
            return t.rearrange("(b k p c) w -> b p k (c w)", b=NB, k=KB, p=P, c=C)[b]

        def xrows(t, i):
            j0 = min(i * DW, DJ - DW)
            return t.rearrange("(j c) f -> j (c f)", c=C)[j0:j0 + DW, :].rearrange("(p r) q -> p (r q)", r=DR)

        NA = KB * C * ATT
        att_buf = [T1[:, i * NA:(i + 1) * NA] for i in range(2)]
        N4 = KB * C * ROW4
        r4_buf = [T1[:, i * N4:(i + 1) * N4] for i in range(2)]
        g4_buf = [T2[:, i * N4:(i + 1) * N4] for i in range(2)]
        before, _ = count_steps()
        order = dense_order()

        def kview(t):
            return t.rearrange("p (k w) -> p k w", k=KB)

        def dense_blocks(l):
            return -(-(ND - l) // DL)

        def uses(b):
            return b // 2

        @block.sync
        def _(sp):
            sp.dma_start(nat_src, src.rearrange("(p r) -> p r", r=ER)).then_inc(src_in, 16)
            sp.dma_start(nat_dst, dst.rearrange("(p r) -> p r", r=ER)).then_inc(nat_in, 16)
            sp.dma_start(nat_w, ew.rearrange("(p r) -> p r", r=ER)).then_inc(nat_in, 16)
            sp.dma_start(nat16, ea16.rearrange("(p r) w -> p (r w)", r=ER)).then_inc(nat_in, 16)
            sp.dma_start(nat32, ea32.rearrange("(p r) w -> p (r w)", r=ER)).then_inc(nat_in, 16)
            sp.wait_ge(consts, N_CONST)
            sp.wait_ge(w_zero, 1)
            n = 0

            def win(o, i):
                nonlocal n
                sp.dma_start(o, i).then_inc(w_in, 16)
                n += 1

            def column(v):
                return v.rearrange("(f o) -> f o", o=1)

            with nc.allow_non_contiguous_dma(reason="small weights"):
                for c in range(C):
                    q = slice(F * c, F * c + F)
                    g, h = divmod(c, 2)
                    win(wA[q, g, HID * h:HID * h + HID], w1a[0:F, :])
                    win(wE[16 * c:16 * c + 16, g, HID * h:HID * h + HID], w1a[F:F + 16, :])
                    win(wB[HID * h:HID * h + HID, g, q], w2a)
                    win(wat[q, :], watt.rearrange("f h o -> f (h o)"))
                    win(wZ[q, 0, q], wzt)
                    win(wG[q, :, q], wg[:, 2 * LAST_GINE:2 * LAST_GINE + 2, :])
                    win(bg_c[q, :], bg[:, 2 * LAST_GINE:2 * LAST_GINE + 2])
                    win(b2a_c[q, :], column(b2a))
                    win(batt_c[q, :], column(batt))
                for h in range(2):
                    win(b1a_c[HID * h:HID * h + HID, :], column(b1a))
                win(fcr[:, :], fcw.to_broadcast([P, 2 * F]))
                win(fcb_c, fcb.rearrange("(o w) -> o w", o=1).to_broadcast([P, 1]))
                win(eps_g, eps.rearrange("(o w) -> o w", o=1)[:, LAST_GINE:LAST_GINE + 1].to_broadcast([P, GINE]))
            assert n == NW

            sp.wait_ge(nat_rows, 4)
            sp.dma_start(attN.rearrange("(p r) w -> p (r w)", r=ER), nat_att).then_inc(attn_out, 16)
            for b in range(NB):
                sp.dma_start(upd.rearrange("(b p r) w -> b p (r w)", b=NB, p=P)[b], RI[0][:, :]).then_inc(zeroed, 16)
            with nc.allow_non_contiguous_dma(reason="end marks"):
                for i in range(2):
                    sp.dma_start(sorted_d[i][0:1, :], zero_c[0:1, :]).then_inc(zeroed, 16)
                    sp.dma_start(sorted_d[i][HALF + 1:HALF + 2, :], zero_c[0:1, :]).then_inc(zeroed, 16)
            sp.wait_ge(zeroed, 16 * (NB + 4))

            def after_sort(i, k):
                sp.wait_ge(srt_rdy, k)
                sp.dma_start(sorted_d[i][1:HALF + 1, :].rearrange("(p f) o -> p (f o)", p=P), srt[i]).then_inc(srt_out, 16)
                sp.wait_ge(srt_out, 16 * k)
                base = sorted_d[i].rearrange("n o -> (n o)")
                for off, o in ((1, t0), (2, t1)):
                    sp.dma_start(o[0:98, 0:256].rearrange("q (g p) -> q g p", g=2),
                                 base[off:off + ROWS].rearrange("(g q p) -> q g p", g=2, q=98)).then_inc(nb_in, 16)
                for off, o in ((0, t2[:, 0:196]), (1, t2[:, 256:452]), (2, t3[:, 0:196])):
                    sp.dma_start(o, base[off:off + ROWS].rearrange("(p f) -> p f", p=P)).then_inc(nb_in, 16)

            def masks_out(i):
                sp.wait_ge(mask_rdy, i + 1)
                with nc.allow_non_contiguous_dma(reason="rows of 196 bytes"):
                    sp.dma_start(mask_d[i].rearrange("m (p f) -> p m f", p=P), mask8).then_inc(mask_out, 16)
                sp.wait_ge(mask_out, 16 * (i + 1))

            def masks_in(i):
                for m, o in ((0, NS), (1, NE)):
                    for c in range(C):
                        sp.dma_start(o[F * c:F * c + F, :],
                                     mask_d[i][m:m + 1, c * J:(c + 1) * J].to_broadcast([F, J])).then_inc(mask_in, 16)

            def after_list(i, k):
                sp.wait_ge(srt_rdy, k)
                sp.dma_start(list_d.rearrange("(p f) o -> p (f o)", p=P), t0[:, 0:256]).then_inc(srt_out, 16)
                sp.wait_ge(srt_out, 16 * k)
                sp.dma_start(t1[0:98, 0:256].rearrange("q (g p) -> q g p", g=2),
                             list_d.rearrange("n o -> (n o)")[0:ROWS].rearrange("(g q p) -> q g p", g=2, q=98)).then_inc(nb_in, 16)

            after_sort(0, 1)
            masks_out(0)
            masks_in(0)
            for b in range(NB):
                sp.wait_ge(ga[b % 2], 16 * C * KB * (uses(b) + 1))
                sp.dma_start(rows128(attS, b), kview(att_buf[b % 2])).then_inc(atts_out[b % 2], 16)
            after_sort(1, 2)
            masks_out(1)
            after_list(0, 3)
            for i in range(2):
                sp.wait_ge(atts_out[i], 16 * uses(NB + 1 - i))

            def lane_done(l, n):
                if n.pe:
                    sp.wait_ge(pe_n[l], n.pe)
                if n.act:
                    sp.wait_ge(act_n[l], n.act)
                if n.store:
                    sp.wait_ge(st_n[l], 16 * n.store)

            def load(l, n, ap):
                lane_done(l, n)
                sp.dma_start(kview(RI[l][:, :]) if len(ap.shape) == 3 else RI[l][:, :], ap).then_inc(ld_n[l], 16)

            def store(l, n, ap):
                sp.wait_ge(act_n[l], n.act + 1)
                sp.dma_start(ap, kview(RI[l][:, :]) if len(ap.shape) == 3 else RI[l][:, :]).then_inc(st_n[l], 16)

            def edge_rows(b, free):
                free(b)
                sp.dma_start(kview(RA[:, :]), rows128(attS, b)).then_inc(ra_in, 16)

            def read4(b):
                if b:
                    sp.wait_ge(dve_n[(b - 1) % 2], before["to4", b - 1].dve + 1)
                else:
                    sp.wait_ge(pe_n[1], before["other", 2, 1].pe)

            for L in range(3):
                def read_before(b):
                    if b:
                        sp.wait_ge(act_n[(b - 1) % 2], before["msg", L, b - 1].act + 1)
                if L in (0, 2):
                    for b in range(NB):
                        edge_rows(b, read_before)
                else:
                    sp.wait_ge(att_rdy, 1)
                    sp.dma_start(att_d, cut).then_inc(parts_out, 16)
                    sp.wait_ge(parts_out, 16)
                    for a in range(PARTS):
                        for c in range(C):
                            row = (a * C + c) * HEADS
                            sp.dma_start(parts[row:row + HEADS, :, :],
                                         att_d[F * c:F * c + F, a, :].rearrange("(k h) w -> h k w", h=HEADS)).then_inc(parts_in, 16)
                for b in range(NB):
                    store(b % 2, before["table", L, b], rows128(table, b))
                for b in range(2):
                    sp.wait_ge(st_n[b], 16 * (before["table", L, NB - 2 + (NB - b) % 2].store + 1))
                sp.sem_inc(table_out, 1)
                if L == 0:
                    for m, o in ((0, ns8), (1, ne8)):
                        sp.dma_start(o, mask_d[0][m].rearrange("(k o w) -> k o w", o=1, w=SW).to_broadcast([F, HEADS, SW])).then_inc(pieces_in, 16)
                sp.wait_ge(upd_n, L + 1)
                for b in range(NB):
                    if L == 2:
                        edge_rows(b, read4)
                    if L < 2 or b < 2:
                        load(b % 2, before["other", L, b], rows128(upd, b))
                    if L == 2:
                        sp.wait_ge(act_n[b % 2], before["to4", b].act + 2)
                        sp.dma_start(rows128(row4, b), kview(r4_buf[b % 2])).then_inc(r4_out[b % 2], 16)
                        if b + 2 < NB:
                            sp.wait_ge(pe_n[b % 2], before["other", L, b].pe + 1)
                            sp.dma_start(kview(RI[b % 2][:, :]), rows128(upd, b + 2)).then_inc(ld_n[b % 2], 16)
            masks_in(1)
            sp.wait_ge(fin, 16 * 2 * C * NT)

        @block.gpsimd
        def _(pool):
            done = [0]

            def const(i):
                done[0] += 1
                i.then_inc(consts, 1)
                pool.wait_ge(consts, done[0])

            def bands(t, c, value):
                q = slice(F * c, F * c + F)
                const(nc.gpsimd.memset(t[q, q], value))

            for i, (t, value) in enumerate(((ident, 0.0), (ltri, 1.0), (mean, 0.0))):
                nc.gpsimd.memset(t[:, :], value).then_inc(pool_ok, 1)
                pool.wait_ge(pool_ok, i + 1)
            const(nc.gpsimd.affine_select(out=ident[:, :], in_=ident[:, :], compare_op=ALU.not_equal, fill=1.0,
                                          base=0, pattern=[[-1, P]], channel_multiplier=1))
            const(nc.gpsimd.affine_select(out=ltri[:, :], in_=ltri[:, :], compare_op=ALU.is_gt, fill=0.0,
                                          base=0, pattern=[[1, P]], channel_multiplier=-1))
            for c in range(C):
                bands(mean, c, 1.0 / F)
            const(nc.gpsimd.iota(index2[:, 0:SC], pattern=[[1, SC]], base=0, channel_multiplier=SC))
            const(nc.gpsimd.iota(index2[:, SC:2 * SC], pattern=[[1, SC]], base=HALF, channel_multiplier=SC))
            const(nc.gpsimd.iota(pos1[:, :], pattern=[[P, C * NT]], base=1, channel_multiplier=1))
            const(nc.gpsimd.iota(eid[:, :], pattern=[[1, C * NT]], base=0, channel_multiplier=ER))
            const(nc.gpsimd.iota(frm[:, 0:4], pattern=[[1, 4]], base=ER - 4, channel_multiplier=ER))
            const(nc.gpsimd.memset(cols[:, :], 0.0))
            assert done[0] == N_CONST

            def gather(o, t, index, m, signal):
                nc.gpsimd.indirect_dma_start(
                    out=o, out_offset=None, in_=t, in_offset=bass.IndirectOffsetOnAxis(ap=index[:, m:m + 1], axis=0),
                    bounds_check=t.shape[0] - 1, oob_is_err=False).then_inc(signal, 16)

            def scatter(t, index, m, i, signal):
                nc.gpsimd.indirect_dma_start(
                    out=t, out_offset=bass.IndirectOffsetOnAxis(ap=index[:, m:m + 1], axis=0), in_=i, in_offset=None,
                    bounds_check=t.shape[0] - 1, oob_is_err=False).then_inc(signal, 16)

            def tiles(b):
                return [(k * C + c, c * NT + b * KB + k) for k in range(KB) for c in range(C)]

            pool.wait_ge(attn_out, 16)
            pool.wait_ge(idx_rdy, 1)
            for b in range(NB):
                if b >= 2:
                    pool.wait_ge(atts_out[b % 2], 16 * uses(b))
                    pool.wait_ge(dcol, b - 1)
                for i, m in tiles(b):
                    gather(att_buf[b % 2][:, i * ATT:(i + 1) * ATT], attN, eI, m, ga[b % 2])
            pool.wait_ge(dcol, NB + 1)
            for b in range(NB):
                for i, m in tiles(b):
                    gather(D[:, b * W + i * F:b * W + (i + 1) * F], x, dG, m, gx[1])
            for b in range(NB):
                for i, m in tiles(b):
                    gather(T2[:, b * W + i * F:b * W + (i + 1) * F], x, sG, m, gx[0])

            first = []

            def updates(L):
                pool.wait_ge(table_out, L + 1)
                nb = C * NT // BG
                if L == 0:
                    pool.wait_ge(idx_rdy, 3)
                    for i in range(nb):
                        first.append(pool.value_load(home[0:1, i * BG:i * BG + 1], min_val=0, max_val=65535))
                for i in range(nb + 2):
                    if i < nb:
                        with pool.If(first[i] < ROWS):
                            if i >= 4:
                                pool.wait_ge(ss[i - 4], 16 * BG * (L + 1))
                            for m in range(BG):
                                gather(G[i % 4][:, m * F:(m + 1) * F], table, frm, i * BG + m, gs[i])
                    if i >= 2:
                        with pool.If(first[i - 2] < ROWS):
                            pool.wait_ge(gs[i - 2], 16 * BG * (L + 1))
                            for m in range(BG):
                                scatter(upd, home, (i - 2) * BG + m, G[(i - 2) % 4][:, m * F:(m + 1) * F], ss[i - 2])
                for i in range(nb):
                    with pool.If(first[i] < ROWS):
                        pool.wait_ge(ss[i], 16 * BG * (L + 1))
                pool.sem_inc(upd_n, 1)

            for L in range(3):
                updates(L)
            def put(s, t, index, blocks):
                for b in blocks:
                    pool.wait_ge(dve_n[b % 2], before["final", s, b].dve + 2)
                    for i, m in tiles(b):
                        scatter(out, index, m, t[:, b * W + i * F:b * W + (i + 1) * F], fin)

            for l in range(DL):
                pool.wait_ge(dst_[l], 16 * dense_blocks(l))
            put(0, final_s, sU, range(EARLY))
            for b in range(2):
                pool.wait_ge(r4_out[b], 16 * uses(NB + 1 - b))
            for b in range(NB):
                if b >= 2:
                    pool.wait_ge(act_n[b % 2], before["from4", b - 2].act + 2)
                for i, m in tiles(b):
                    gather(g4_buf[b % 2][:, i * ROW4:(i + 1) * ROW4], row4, jI, m, g4[b % 2])
            put(0, final_s, sU, range(EARLY, NB))
            pool.wait_ge(fin, 16 * C * NT)
            put(1, D, dUI, range(NB))

        @block.scalar
        def _(act):
            def one(i, l):
                i.then_inc(act_n[l], 1)

            def wait_pe(l, v):
                act.wait_ge(pe_n[l], v)

            def copy(l, o, i):
                one(nc.scalar.activation(o, i, ACT.Copy), l)

            def act_rows_in(l, n, o):
                wait_pe(l, n.pe + 1)
                copy(l, o, ps[l][0][:, 0:W])

            def act_rows_out(l, n, free=None):
                wait_pe(l, n.pe + 1)
                if n.store:
                    act.wait_ge(st_n[l], 16 * n.store)
                copy(l, RI[l][:, :], ps[l][1][:, 0:W])

            def act_ln(l, n, shift):
                wait_pe(l, n.pe + 1)
                one(nc.scalar.activation(HB[l][:, :], ps[l][0][:, 0:W], ACT.Square, bias=shift), l)
                wait_pe(l, n.pe + 2)
                one(nc.scalar.activation(HB[l][:, :], ps[l][1][:, 0:W], ACT.Ln, bias=eps_c), l)
                act.wait_ge(act_n[l], n.act + 2)
                one(nc.scalar.activation(HB[l][:, :], HB[l][:, :], ACT.Exp, scale=-0.5), l)

            def act_relu(l, v, o, u, bias):
                wait_pe(l, v)
                one(nc.scalar.activation(o, ps[l][u][:, 0:W], ACT.Relu, bias=bias), l)

            act.preload_act_table_set("natural_log_exp_and_others")

            act.wait_ge(nat_in, 16 * 4)
            rows = nat_att.rearrange("p (r w) -> p r w", w=ATT)
            nc.scalar.activation(rows[:, :, 0:16], nat16.rearrange("p (r w) -> p r w", w=16), ACT.Copy).then_inc(nat_rows, 1)
            nc.scalar.activation(rows[:, :, 16:48], nat32.rearrange("p (r w) -> p r w", w=32), ACT.Copy).then_inc(nat_rows, 1)
            nc.scalar.activation(rows[:, :, 48], nat_w, ACT.Copy).then_inc(nat_rows, 1)
            nc.scalar.activation(rows[:, :, 49], nat_dst, ACT.Copy).then_inc(nat_rows, 1)
            act.wait_ge(nat_rows, 4)
            for i in range(DL):
                act.dma_start(dR[i], xrows(x, i)).then_inc(dld[i], 16)
            act.wait_ge(ready, 2)

            def dense_store(i):
                l, u = i % DL, i // DL
                act.wait_ge(ddve[l], D_DVE * (u + 1))
                if i == ND - 1:
                    act.wait_ge(dst_[(i - 1) % DL], 16 * ((i - 1) // DL + 1))
                act.dma_start(xrows(out, i), dX[l]).then_inc(dst_[l], 16)

            def dense(i, n):
                l, u = i % DL, i // DL
                A, H, q = dA[l], dH[l], dP[l]
                pe0, act0, dve0 = D_PE * u, D_ACT * u, D_DVE * u

                def go(o, i_, f, **k):
                    nc.scalar.activation(o, i_, f, **k).then_inc(dact[l], 1)

                def power(scale, add):
                    v = inv[:, l * 4 * DR:(l + 1) * 4 * DR]
                    go(v, v, ACT.Ln, bias=add, scale=scale)
                    act.wait_ge(dact[l], act0 + (2, 5, 11)[(1, 3, 8).index(n)])
                    go(v, v, ACT.Exp, scale=-0.5)

                if n == 0:
                    if u:
                        dense_store(i - DL)
                    act.wait_ge(ddve[l], dve0 + 2)
                    if i + DL < ND:
                        act.dma_start(dR[l], xrows(x, i + DL)).then_inc(dld[l], 16)
                    go(H, A, ACT.Square)
                elif n == 1:
                    act.wait_ge(ddve[l], dve0 + 3)
                    power(1.0 / F, eps_c)
                elif n == 2:
                    act.wait_ge(ddve[l], dve0 + 5)
                    go(H, A, ACT.Square)
                elif n == 3:
                    act.wait_ge(ddve[l], dve0 + 6)
                    power((1.0 + EPS) / F, eps2_c)
                elif n == 4:
                    act.wait_ge(dpe[l], pe0 + 1)
                    if u:
                        act.wait_ge(dst_[l], 16 * u)
                    go(dX[l], q[0], ACT.Copy)
                elif n == 5:
                    act.wait_ge(dpe[l], pe0 + 2)
                    go(H, q[1], ACT.Relu, bias=bg_c[:, 0:1])
                elif n == 6:
                    act.wait_ge(dpe[l], pe0 + 3)
                    go(A, q[0], ACT.Relu, bias=bg_c[:, 1:2])
                elif n == 7:
                    act.wait_ge(dpe[l], pe0 + 4)
                    go(H, q[1], ACT.Square)
                elif n == 8:
                    act.wait_ge(ddve[l], dve0 + 8)
                    power(1.0 / F, eps_c)

            for i, n in order:
                dense(i, n)
            for i in range(ND - DL, ND):
                dense_store(i)

            def turn_in(s, o):
                for b in range(NB):
                    act_rows_in(b % 2, before["turn", s, b], blk(o, b))

            def act_to4(b):
                l, n = b % 2, before["to4", b]
                o = r4_buf[l].rearrange("p (m w) -> p m w", w=ROW4)
                wait_pe(l, n.pe + 2)
                if b >= 2:
                    act.wait_ge(r4_out[l], 16 * uses(b))
                copy(l, o[:, :, F:2 * F], ps[l][1][:, 0:W].rearrange("p (m f) -> p m f", f=F))
                act.wait_ge(dve_n[l], n.dve + 1)
                one(nc.scalar.activation(o[:, :, 0:F], o[:, :, 0:F], ACT.Relu), l)

            def act_last(s, b):
                l = b % 2
                act_relu(l, before["last", s, b].pe + 1, HB[l][:, :], 0, bg_c[:, 0:1])
                n = before["final", s, b]
                v = inv[:, l * KB * C:(l + 1) * KB * C]
                wait_pe(l, n.pe + 1)
                one(nc.scalar.activation(HB[l][:, :], ps[l][0][:, 0:W], ACT.Square), l)
                act.wait_ge(dve_n[l], n.dve + 1)
                one(nc.scalar.activation(v, v, ACT.Ln, bias=eps_c, scale=1.0 / F), l)
                act.wait_ge(act_n[l], n.act + 2)
                one(nc.scalar.activation(v, v, ACT.Exp, scale=-0.5), l)

            turn_in(1, D)
            for L in range(3):
                if L == 1:
                    wait_pe(0, before["score", 0].pe + 1)
                    one(nc.scalar.activation(sc_, ps[0][0][:, 0:SW], ACT.Identity, bias=fcb_c), 0)
                    act.wait_ge(e_rdy, 1)
                    nc.scalar.activation(sc_, sc_, ACT.Exp).then_inc(e_exp, 1)
                for b in range(NB if L != 1 else 0):
                    l, n = b % 2, before["msg", L, b]
                    wait_pe(l, n.pe)
                    act.wait_ge(dve_n[l], n.dve)
                    if L == 0:
                        act.wait_ge(ra_in, 16 * (b + 1))
                        copy(l, HB[l][:, 0:KB * 64].rearrange("p (m w) -> p m w", w=16),
                             RA[:, :].rearrange("p (m w) -> p m w", w=ATT)[:, :, 0:16])
                        wait_pe(l, n.pe + 1)
                        copy(l, AB[l][0:64, :], ps[l][0][0:64, 0:W])
                        act_relu(l, n.pe + 2, HB[l][:, :], 1, b1a_c)
                        act_relu(l, n.pe + 3, X3[l][:, :], 0, b1a_c)
                    elif L == 2:
                        act.wait_ge(ra_in, 16 * (NB + b + 1))
                        copy(l, HB[l][:, :].rearrange("p (m f) -> p m f", f=F),
                             RA[:, :].rearrange("p (m w) -> p m w", w=ATT)[:, :, 48:49].to_broadcast([P, KB * C, F]))
                for b in range(NB):
                    act_rows_out(b % 2, before["table", L, b])
                if L == 0:
                    for l in range(DL):
                        act.wait_ge(dst_[l], 16 * dense_blocks(l))
                    turn_in(0, S)
                shift = cb_c if L == 1 else zero_c
                for b in range(NB):
                    act_ln(b % 2, before["local", L, b], shift)
                if L == 2:
                    for b in range(NB):
                        act_last(0, b)
                for b in range(NB):
                    act_ln(b % 2, before["other", L, b], shift)
                    if L == 2:
                        act_to4(b)
            for b in range(NB):
                l, n = b % 2, before["from4", b]
                wait_pe(l, n.pe)
                act.wait_ge(dve_n[l], n.dve)
                act.wait_ge(g4[l], 16 * C * KB * (uses(b) + 1))
                for v, o in enumerate((HB[l], X3[l])):
                    copy(l, o[:, :].rearrange("p (m f) -> p m f", f=F),
                         g4_buf[l].rearrange("p (m w) -> p m w", w=ROW4)[:, :, v * F:(v + 1) * F])
                for v, o in enumerate((T1, D)):
                    wait_pe(l, n.pe + v + 1)
                    copy(l, blk(o, b), ps[l][v][:, 0:W])
            for b in range(NB):
                act_last(1, b)

        @block.tensor
        def _(pe):
            def mm(o, w, i, start=True, stop=True):
                for a, e in ((0, 512), (512, i.shape[-1])):
                    r = nc.tensor.matmul(o[:, a:e], w, i[:, a:e], start=start, stop=stop)
                return r

            def begin(l, n):
                if n.act:
                    pe.wait_ge(act_n[l], n.act)
                if n.dve:
                    pe.wait_ge(dve_n[l], n.dve)

            def turn_tiles(l, u, tile, rows=P):
                for k in range(KB):
                    r = nc.tensor.transpose(ps[l][u][0:rows, k * P:(k + 1) * P], tile(k), ident[:, :])
                r.then_inc(pe_n[l], 1)

            def pe_rows_out(l, n, t, w):
                begin(l, n)
                for k in range(KB):
                    r = nc.tensor.matmul(ps[l][1][:, k * P:(k + 1) * P], t[:, k * P:(k + 1) * P], w, start=True, stop=True)
                r.then_inc(pe_n[l], 1)

            def pe_ln_rows(l, n, t):
                begin(l, n)
                mm(ps[l][0], center[:, :], t, stop=False)
                pe.wait_ge(ld_n[l], 16 * (n.load + 1))
                for k in range(KB):
                    r = nc.tensor.matmul(ps[l][0][:, k * P:(k + 1) * P], RI[l][:, k * P:(k + 1) * P], ident[:, :],
                                         start=False, stop=k in (3, KB - 1))
                r.then_inc(pe_n[l], 1)
                pe.wait_ge(act_n[l], n.act + 1)
                mm(ps[l][1], mean[:, :], HB[l][:, :]).then_inc(pe_n[l], 1)

            def pe_ln(l, n, t, a=None, wa=None):
                begin(l, n)
                r = mm(ps[l][0], center[:, :], t, stop=a is None)
                if a is not None:
                    r = mm(ps[l][0], wa, a, start=False)
                r.then_inc(pe_n[l], 1)
                pe.wait_ge(act_n[l], n.act + 1)
                mm(ps[l][1], mean[:, :], HB[l][:, :]).then_inc(pe_n[l], 1)

            def pe_mlp(l, n, g, t, a=None):
                begin(l, n)
                r = mm(ps[l][0], wX[:, g, :], t, stop=a is None)
                if a is not None:
                    r = mm(ps[l][0], wG[:, 2 * g, :], a, start=False)
                r.then_inc(pe_n[l], 1)
                pe.wait_ge(act_n[l], n.act + 1)
                mm(ps[l][1], wG[:, 2 * g + 1, :], HB[l][:, :]).then_inc(pe_n[l], 1)

            def dense(i, n):
                l, u = i % DL, i // DL
                q = dP[l]
                act0, dve0 = D_ACT * u, D_DVE * u
                if n == 4:
                    pe.wait_ge(ddve[l], dve0 + 7)
                    for k in range(DR):
                        r = nc.tensor.transpose(q[0][:, k * P:(k + 1) * P], dA[l][:, k * P:(k + 1) * P], ident[:, :])
                elif n == 5:
                    pe.wait_ge(dact[l], act0 + 7)
                    r = nc.tensor.matmul(q[1], wX[:, 0, :], dX[l], start=True, stop=True)
                elif n == 6:
                    pe.wait_ge(dact[l], act0 + 8)
                    r = nc.tensor.matmul(q[0], wG[:, 1, :], dH[l], start=True, stop=True)
                elif n == 7:
                    pe.wait_ge(dact[l], act0 + 9)
                    for k in range(DR):
                        o = q[1][:, k * P:(k + 1) * P]
                        nc.tensor.matmul(o, dX[l][:, k * P:(k + 1) * P], center[:, :], start=True, stop=False)
                        r = nc.tensor.matmul(o, dA[l][:, k * P:(k + 1) * P], center[:, :], start=False, stop=True)
                else:
                    return
                r.then_inc(dpe[l], 1)

            at = [0]

            def dense_some(k):
                for i, n in order[at[0]:at[0] + k]:
                    dense(i, n)
                at[0] += k

            def pe_final(l, n, t, a):
                begin(l, n)
                for k in range(KB):
                    o = ps[l][0][:, k * P:(k + 1) * P]
                    nc.tensor.matmul(o, t[:, k * P:(k + 1) * P], center[:, :], start=True, stop=False)
                    r = nc.tensor.matmul(o, a[:, k * P:(k + 1) * P], center[:, :], start=False, stop=True)
                r.then_inc(pe_n[l], 1)

            turns = [0]

            def net_turn(t, w):
                turns[0] += 1
                pe.wait_ge(turn_rdy, turns[0])
                for a in range(0, w, P):
                    r = nc.tensor.transpose(pi[:, a:a + P], t[:, a:a + P], ident[:, :])
                r.then_inc(turned, 1)
                dense_some(FILL[0] if turns[0] <= 14 else FILL[2])

            def net_sort(h, top):
                cur, other = va, vb
                for k in range(1, top + 1):
                    if k == 16:
                        cur, other = other, cur
                    n1 = min(k, 15) - 8
                    if k > 8:
                        net_turn(cur, h * SC)
                        cur, other = (other, cur) if n1 % 2 == 0 else (cur, other)
                        net_turn(cur, h * SC)
                        cur, other = other, cur
                    elif k % 2:
                        cur, other = other, cur
                return cur

            small = [0]

            def small_wait():
                small[0] += 1
                pe.wait_ge(small_rdy, small[0])

            def index_tiles(arrays):
                small_wait()
                for o, t in enumerate(arrays):
                    for g in range(2):
                        r = nc.tensor.transpose(pi[:, 256 * o + 98 * g:256 * o + 98 * g + 98],
                                                t[0:98, g * P:(g + 1) * P], ident[0:98, 0:98])
                r.then_inc(small_mm, 1)

            def net_join():
                net_turn(va, SC)
                net_turn(va, SC)
                net_turn(va, 2 * SC)
                net_turn(va, 2 * SC)
                small_wait()
                nc.tensor.matmul(pi[:, 0:2], ltri[:, :], rs_c, start=True, stop=True)
                nc.tensor.matmul(pi[:, 2:3], shf[:, :], rs_c[:, 0:1], start=True, stop=True)
                for h in range(2):
                    r = nc.tensor.matmul(pi[0:1, 256 + h * P:256 + (h + 1) * P], rm_c[:, h:h + 1], ident[:, :], start=True, stop=True)
                r.then_inc(small_mm, 1)
                small_wait()
                for h in range(2):
                    r = nc.tensor.matmul(pi[:, 512 + h:513 + h], rowb[0:1, h * P:(h + 1) * P], ident[0:1, 0:1], start=True, stop=True)
                r.then_inc(small_mm, 1)

            pe.wait_ge(consts, N_CONST)
            net_sort(1, 15)
            index_tiles((t0, t1, t2))
            pe.wait_ge(idx_rdy, 1)
            pe.wait_ge(ready, 1)
            nc.tensor.matmul(pi[:, 0:P], wZ[:, 0, :], center[:, :], start=True, stop=True)
            nc.tensor.matmul(pi[:, 2 * P:2 * P + F], wtmp[:, :], center[:, 0:F], start=True, stop=True)
            nc.tensor.matmul(pi[:, P:P + 1], center[:, :], batt_c, start=True, stop=True).then_inc(wz_mm, 1)
            pe.wait_ge(ready, 2)
            for b in range(NB):
                dense_some(FILL[1])
            net_sort(1, 15)
            index_tiles((t0, t1, t2))
            net_join()
            net_sort(2, 16)
            index_tiles((t0, t2))
            dense_some(len(order))
            pe.wait_ge(idx_rdy, 3)
            pe.wait_ge(ready, 3)
            for l in range(DL):
                pe.wait_ge(dact[l], D_ACT * dense_blocks(l))
                pe.wait_ge(ddve[l], D_DVE * dense_blocks(l))

            def turn_in(s, rows):
                pe.wait_ge(gx[s], 16 * C * NT)
                for b in range(NB):
                    begin(b % 2, before["turn", s, b])
                    turn_tiles(b % 2, 0, lambda k: rows[:, b * W + k * P:b * W + (k + 1) * P])

            turn_in(1, D)

            shifts = [0]

            def carries(w):
                for i in range(C - 1):
                    if shifts[0]:
                        pe.wait_ge(cr_used, shifts[0])
                    shifts[0] += 1
                    pe.wait_ge(cr_rdy, shifts[0])
                    nc.tensor.matmul(pc[:, 0:1], w[:, :], ctmp, start=True, stop=True).then_inc(cr_mm, 1)
                pe.wait_ge(cr_used, shifts[0])

            def carries_packed(back):
                for turn in range(2):
                    if shifts[0]:
                        pe.wait_ge(cr_used, shifts[0])
                    shifts[0] += 1
                    pe.wait_ge(cr_rdy, shifts[0])
                    if turn == 0:
                        r = nc.tensor.matmul(pc[0:HEADS, 0:2 * F], hm[:, :], ends[:, :], start=True, stop=True)
                    else:
                        r = nc.tensor.matmul(pc[:, 2 * F:3 * F], hmt[:, :], run[:, 2 * F + back:3 * F + back], start=True, stop=True)
                    r.then_inc(cr_mm, 1)
                pe.wait_ge(cr_used, shifts[0])

            for L in range(3):
                fb, bb = (T2, T1) if L == 1 else (T1, T2)
                if L == 1:
                    pe.wait_ge(ready, 4)
                    begin(0, before["score", 0])
                    begin(1, before["msg", 1, 1])
                    for q in range(SUB):
                        for side, t in enumerate((S, D)):
                            r = mm(ps[0][0], wSc[:, side, q, :], blk(t, q, SW), start=q + side == 0, stop=q + side == SUB)
                    r.then_inc(pe_n[0], 1)
                    for back in range(4):
                        carries_packed(back % 2)
                for b in range(SUB if L == 1 else NB):
                    l, n = b % 2, before["msg", L, b]
                    if L == 0:
                        begin(l, n)
                        pe.wait_ge(act_n[l], n.act + 1)
                        turn_tiles(l, 0, lambda k: HB[l][:, k * 64:(k + 1) * 64], 64)
                        for g in range(2):
                            o = ps[l][1 - g]
                            pe.wait_ge(act_n[l], n.act + 2)
                            mm(o, wA[:, g, :], blk(D, b), stop=False)
                            mm(o, wE[:, g, :], AB[l][0:64, :], start=False).then_inc(pe_n[l], 1)
                        pe.wait_ge(act_n[l], n.act + 4)
                        mm(ps[l][1], wB[:, 0, :], HB[l][:, :], stop=False)
                        mm(ps[l][1], wB[:, 1, :], X3[l][:, :], start=False).then_inc(pe_n[l], 1)
                    elif L == 1:
                        begin(l, n)
                        pe.wait_ge(parts_in, 16 * PARTS * C)
                        for h in range(HEADS + 1):
                            if h:
                                pe.wait_ge(dve_n[l], n.dve + h)
                            if h < HEADS:
                                mm(ps[l][0], wSel[:, h, :], parts[:, b, :]).then_inc(pe_n[l], 1)
                            if h:
                                mm(ps[l][1], wH[:, h - 1, :], (HB, AB)[(h - 1) % 2][l][:, 0:SW], start=h == 1, stop=h == HEADS).then_inc(pe_n[l], 1)
                    elif L == 2:
                        begin(l, n)
                        pe.wait_ge(act_n[l], n.act + 1)
                        turn_tiles(l, 0, lambda k: HB[l][:, k * P:(k + 1) * P])
                wa = wZ[:, 1, :] if L == 2 else center[:, :]
                begin(1, before["sums", L])
                carries(shf)
                for b in range(NB):
                    pe.wait_ge(fix_n, L * NB + b + 1)
                    pe_rows_out(b % 2, before["table", L, b], blk(fb, b), wa)
                if L == 0:
                    turn_in(0, T2)
                begin(1, before["back", L])
                carries(shb)
                for b in range(NB):
                    pe.wait_ge(tot_n, L * NB + b + 1)
                    pe_ln(b % 2, before["local", L, b], blk(S, b), blk(bb, b), wa)
                if L == 2:
                    for b in range(NB):
                        pe_mlp(b % 2, before["last", 0, b], 0, blk(S, b))
                        pe_final(b % 2, before["final", 0, b], blk(S, b), AB[b % 2])
                for b in range(NB):
                    pe_ln_rows(b % 2, before["other", L, b], blk(D, b))
                    if L == 2:
                        l = b % 2
                        begin(l, before["to4", b])
                        for u, t in enumerate((S, D)):
                            turn_tiles(l, u, lambda k: t[:, b * W + k * P:b * W + (k + 1) * P])
            for b in range(NB):
                l, n = b % 2, before["from4", b]
                begin(l, n)
                pe.wait_ge(act_n[l], n.act + 2)
                for v, rows in enumerate((HB[l], X3[l])):
                    turn_tiles(l, v, lambda k: rows[:, k * P:(k + 1) * P])
            begin(1, before["sums", 3])
            carries(shf)
            carries(shb)
            for b in range(NB):
                l = b % 2
                pe.wait_ge(tot_n, 3 * NB + b + 1)
                pe_mlp(l, before["last", 1, b], 0, blk(D, b), blk(T2, b))
                pe_final(l, before["final", 1, b], blk(D, b), AB[l])

        @block.vector
        def _(dve):
            v = nc.vector
            chain = [0]

            def link(i):
                chain[0] += 1
                i.then_inc(dchain, 1)
                dve.wait_ge(dchain, chain[0])

            for t in (wA, wE, wB, wH, wZ, wG):
                v.memset(t[:, :, :], 0.0)
            link(v.memset(RI[0][:, :], 0.0))
            dve.sem_inc(w_zero, 1)
            dve.wait_ge(consts, N_CONST)
            link(v.tensor_scalar(gray, index2, 1, None, ALU.logical_shift_right))
            link(v.tensor_tensor(gray, gray, index2, ALU.bitwise_xor))
            for k in range(1, 17):
                i, s = (index2, 1) if k == 1 else (gray, k - 1)
                link(v.tensor_scalar(t0.bitcast(I32), i, s, 1, ALU.logical_shift_right, ALU.bitwise_and))
                link(v.tensor_scalar(flips[:, k - 1, :], t0.bitcast(I32), -2.0, 1.0, ALU.mult, ALU.add))
            link(v.tensor_scalar(iop, index2[:, 0:SC], 1.0, None, ALU.add))

            def pack(field, low, o):
                link(v.tensor_copy(o.bitcast(I32), field))
                link(v.tensor_copy(low.bitcast(I32), low))
                link(v.tensor_scalar(o.bitcast(I32), o.bitcast(I32), 15, None, ALU.logical_shift_left))
                link(v.tensor_tensor(o.bitcast(I32), o.bitcast(I32), low.bitcast(I32), ALU.bitwise_or))

            def encode(key, pay, o, a, b):
                link(v.tensor_scalar(a, key, SPLIT, None, ALU.is_lt))
                link(v.tensor_scalar(b, key, -2.0, 181559.0, ALU.mult, ALU.add))
                link(v.tensor_tensor(b, b, a, ALU.mult))
                link(v.scalar_tensor_tensor(out=key, in0=key, scalar=-50744.0, in1=b, op0=ALU.add, op1=ALU.add))
                link(v.tensor_scalar(b, pay, -2.0, 32767.0, ALU.mult, ALU.add))
                link(v.tensor_tensor(b, b, a, ALU.mult))
                link(v.tensor_tensor(pay, pay, b, ALU.add))
                pack(key, pay, o)

            def field_of(bits, o):
                link(v.tensor_scalar(o.bitcast(I32), bits.bitcast(I32), 15, None, ALU.logical_shift_right))
                link(v.tensor_copy(o, o.bitcast(I32)))

            def decode(bits, field, low, a, b):
                field_of(bits, field)
                link(v.tensor_scalar(low.bitcast(I32), bits.bitcast(I32), 32767, None, ALU.bitwise_and))
                link(v.tensor_copy(low, low.bitcast(I32)))
                link(v.tensor_scalar(a, field, 65536.0, None, ALU.is_ge))
                link(v.tensor_scalar(b, low, -2.0, 32767.0, ALU.mult, ALU.add))
                link(v.tensor_tensor(b, b, a, ALU.mult))
                link(v.tensor_tensor(low, low, b, ALU.add))
                link(v.tensor_scalar(b, field, -2.0, 80071.0, ALU.mult, ALU.add))
                link(v.tensor_tensor(b, b, a, ALU.mult))
                link(v.scalar_tensor_tensor(out=field, in0=field, scalar=50744.0, in1=b, op0=ALU.add, op1=ALU.add))

            def to_row(pos, o, a):
                link(v.tensor_scalar(o, pos, 4.0, None, ALU.mult))
                for c in range(1, C):
                    link(v.tensor_scalar(a, pos, float(c * J), float(C * J - 1), ALU.is_ge, ALU.mult))
                    link(v.tensor_tensor(o, o, a, ALU.subtract))

            def dense(i, n):
                l, u = i % DL, i // DL
                A, H, X, q = dA[l], dH[l], dX[l], dP[l]
                act0, dve0 = D_ACT * u, D_DVE * u
                s_ = inv[:, l * 4 * DR:(l + 1) * 4 * DR]
                spread = s_.rearrange("p (m o) -> p m o", o=1).to_broadcast([P, C * DR, F])

                def by_row(t):
                    return t.rearrange("p (m f) -> p m f", f=F)

                def go(i_):
                    i_.then_inc(ddve[l], 1)

                if n == 0:
                    dve.wait_ge(dld[l], 16 * (u + 1))
                    if u:
                        dve.wait_ge(ddve[l], dve0)
                    go(v.tensor_reduce(s_, by_row(dR[l]), AXX, ALU.add))
                    dve.wait_ge(ddve[l], dve0 + 1)
                    go(v.scalar_tensor_tensor(out=by_row(A), in0=spread, scalar=-1.0 / F, in1=by_row(dR[l]), op0=ALU.mult, op1=ALU.add))
                elif n in (1, 3, 8):
                    dve.wait_ge(dact[l], act0 + {1: 1, 3: 4, 8: 10}[n])
                    go(v.tensor_reduce(s_, by_row(H), AXX, ALU.add))
                elif n == 2:
                    dve.wait_ge(dact[l], act0 + 3)
                    go(v.tensor_tensor(by_row(A), by_row(A), spread, ALU.mult))
                    dve.wait_ge(ddve[l], dve0 + 4)
                    go(v.tensor_tensor(by_row(A), by_row(A), cb_row[:, :].rearrange("p (o f) -> p o f", o=1).to_broadcast([P, C * DR, F]), ALU.add))
                elif n == 4:
                    dve.wait_ge(dact[l], act0 + 6)
                    go(v.tensor_tensor(by_row(A), by_row(A), spread, ALU.mult))
                elif n == 9:
                    dve.wait_ge(dact[l], act0 + 12)
                    go(v.tensor_tensor(by_row(X), by_row(q[1]), spread, ALU.mult))

            at, owed = [0], [0]

            def dense_some(k):
                for i, n in order[at[0]:at[0] + k]:
                    dense(i, n)
                at[0] += k

            turns = [0]

            def net_turn(cur, o, w):
                turns[0] += 1
                dve.sem_inc(turn_rdy, 1)
                dense_some(owed[0])
                owed[0] = FILL[0] if turns[0] <= 14 else FILL[2]
                dve.wait_ge(turned, turns[0])
                link(v.tensor_copy(o[:, 0:w], pi[:, 0:w]))

            def compare(i, o, w, s):
                a = i[:, 0:w].rearrange("p (g two s) -> p g two s", two=2, s=s)
                b = o[:, 0:w].rearrange("p (g two s) -> p g two s", two=2, s=s)
                v.tensor_tensor(b[:, :, 0, :], a[:, :, 0, :], a[:, :, 1, :], ALU.min)
                link(v.tensor_tensor(b[:, :, 1, :], a[:, :, 0, :], a[:, :, 1, :], ALU.max))
                if owed[0]:
                    dense_some(1)
                    owed[0] -= 1

            def merge_bits(cur, o, w, nbits):
                net_turn(cur, o, w)
                cur, o = o, cur
                for s in reversed(range(nbits)):
                    compare(cur, o, w, 2 ** s)
                    cur, o = o, cur
                net_turn(cur, o, w)
                cur, o = o, cur
                for s in reversed(range(8)):
                    compare(cur, o, w, 2 ** s)
                    cur, o = o, cur
                return cur, o

            def net_sort(h, top):
                w = h * SC
                cur, o = va, vb
                for k in range(1, top + 1):
                    link(v.tensor_tensor(cur[:, 0:w], cur[:, 0:w], flips[:, k - 1, 0:w], ALU.mult))
                    if k == 16:
                        v.tensor_tensor(o[:, 0:SC], cur[:, 0:SC], cur[:, SC:w], ALU.min)
                        link(v.tensor_tensor(o[:, SC:w], cur[:, 0:SC], cur[:, SC:w], ALU.max))
                        cur, o = o, cur
                    if k > 8:
                        cur, o = merge_bits(cur, o, w, min(k, 15) - 8)
                    else:
                        for s in reversed(range(k)):
                            compare(cur, o, w, 2 ** s)
                            cur, o = o, cur
                return cur

            small = [0]

            def small_mms():
                dense_some(owed[0])
                owed[0] = 0
                small[0] += 1
                dve.sem_inc(small_rdy, 1)
                dve.wait_ge(small_mm, small[0])

            dve.wait_ge(src_in, 16)
            key, pay = t0[:, 0:SC], t1[:, 0:SC]
            link(v.memset(key, PAD))
            link(v.tensor_scalar(key[0:EP, 0:ER], nat_src, 1000.0, None, ALU.add))
            link(v.memset(pay, 0.0))
            link(v.tensor_copy(pay[:, 0:C * NT], eid[:, :]))
            link(v.tensor_copy(pay[:, ER - 4:ER], frm[:, 0:4]))
            encode(key, pay, va[:, 0:SC], t2[:, 0:SC], t3[:, 0:SC])
            r = net_sort(1, 15)
            link(v.tensor_copy(srt[0], r[:, 0:SC]))
            dve.sem_inc(srt_rdy, 1)

            def after_sort(i, loads):
                dve.wait_ge(nb_in, 16 * loads)
                cur, prv, nxt = va[:, 0:196], va[:, 256:452], vb[:, 0:196]
                field_of(t2[:, 256:452], cur)
                field_of(t2[:, 0:196], prv)
                field_of(t3[:, 0:196], nxt)
                link(v.tensor_tensor(mask8[:, 0, :], cur, prv, ALU.is_equal))
                link(v.tensor_tensor(mask8[:, 1, :], cur, nxt, ALU.is_equal))
                dve.sem_inc(mask_rdy, 1)
                k, low, a, b = va[0:98, 0:SC], va[0:98, SC:2 * SC], vb[0:98, 0:SC], vb[0:98, SC:2 * SC]
                end = t3[0:98, 0:SC]
                field_of(t0[0:98, 0:SC], k)
                field_of(t1[0:98, 0:SC], a)
                link(v.tensor_tensor(end, k, a, ALU.not_equal))
                decode(t0[0:98, 0:SC], k, low, a, b)
                key, uniq, p_ = t0[0:98, 0:SC], t1[0:98, 0:SC], t2[0:98, 0:SC]
                link(v.tensor_scalar(key, k, -1000.0, None, ALU.add))
                link(v.tensor_scalar(uniq, key, -500000.0, None, ALU.add))
                link(v.tensor_tensor(uniq, uniq, end, ALU.mult))
                link(v.tensor_scalar(uniq, uniq, 500000.0, None, ALU.add))
                link(v.tensor_scalar(key, key, float(NODES - 1), None, ALU.min))
                if i == 0:
                    link(v.tensor_scalar(p_, low, float(EDGES - 1), None, ALU.min))
                else:
                    link(v.tensor_scalar(low, low, -1.0, 0.0, ALU.add, ALU.max))
                    to_row(low, p_, a)
                small_mms()

            after_sort(0, 5)
            v.tensor_copy(sG[:, :], pi[:, 0:196])
            v.tensor_copy(sU[:, :], pi[:, 256:452])
            link(v.tensor_copy(eI[:, :], pi[:, 512:708]))
            dve.sem_inc(idx_rdy, 1)

            dve.wait_ge(w_in, 16 * NW)
            v.memset(eps_c, EPS)
            v.memset(eps2_c, EPS * EPS)
            v.tensor_tensor(center[:, :], ident[:, :], mean[:, :], ALU.subtract)
            v.memset(shf[:, :], 1.0)
            for h in range(4):
                for c in range(C):
                    q = slice(F * c, F * c + F)
                    v.tensor_scalar(wH[q, h, q], wat[q, F * h:F * h + F], 0.25, None, ALU.mult)
            for s in range(2):
                link(v.tensor_tensor(wtmp[:, :].rearrange("p (h o) -> p h o", h=4), wat[:, :].rearrange("p (h o) -> p h o", h=4),
                                     fcr[:, s * F:(s + 1) * F].rearrange("p (h o) -> p h o", h=1).to_broadcast([P, 4, F]), ALU.mult))
                link(v.tensor_reduce(proj[:, s * HEADS:(s + 1) * HEADS], wtmp[:, :].rearrange("p (h o) -> p h o", h=4), AXX, ALU.add))
            link(v.tensor_scalar(eps_g, eps_g, 1.0, None, ALU.add))
            for g in range(GINE):
                link(v.tensor_scalar(wX[:, g, :], wG[:, 2 * g, :], eps_g[:, g:g + 1], None, ALU.mult))
            link(v.tensor_copy(wtmp[:, :], batt_c.to_broadcast([P, P])))
            link(v.memset(shb[:, :], 0.0))
            link(v.tensor_copy(shb[:, 0:P - F], ident[:, F:P]))
            dve.sem_inc(ready, 1)
            dve.wait_ge(wz_mm, 1)
            v.tensor_copy(wZ[:, 1, :], pi[:, 0:P])
            v.tensor_copy(cb_row[:, :], pi[:, 2 * P:2 * P + F])
            link(v.tensor_copy(cb_c, pi[:, P:P + 1]))
            dve.sem_inc(ready, 1)

            def read_masks(i):
                dve.wait_ge(mask_in, 16 * 2 * C * (i + 1))
                link(v.memset(NE[P - F:P, J - 1:J], 0.0))
                v.tensor_tensor_scan(PF[:, :], NS[:, :], NS[:, :], 1.0, ALU.mult, ALU.min)
                link(v.tensor_tensor_scan(QB[:, ::-1], NE[:, ::-1], NE[:, ::-1], 1.0, ALU.mult, ALU.min))

            read_masks(0)

            dense_some(owed[0])
            owed[0] = 0
            dstf = home[:, :].bitcast(F32)
            for b in range(NB):
                dense_some(FILL[1])
                dve.wait_ge(ga[b % 2], 16 * C * KB * (uses(b) + 1))
                v.tensor_copy(dstf.rearrange("p (c k) -> p k c", c=C)[:, b * KB:(b + 1) * KB, :],
                              att_buf[b % 2].rearrange("p (k c w) -> p k c w", k=KB, c=C)[:, :, :, ATT - 1]).then_inc(dcol, 1)
            dve.wait_ge(dcol, NB)
            v.tensor_copy(dG[:, :], dstf).then_inc(dcol, 1)
            dve.wait_ge(dcol, NB + 1)

            link(v.memset(key, PAD))
            link(v.tensor_scalar(key[:, 0:C * NT], dstf, 1000.0, None, ALU.add))
            last = key[:, C * NT - 1:C * NT]
            link(v.tensor_scalar(spare, pos1[:, C * NT - 1:C * NT], float(EDGES), None, ALU.is_gt))
            link(v.tensor_scalar(ctmp, last, -1.0, PAD, ALU.mult, ALU.add))
            link(v.tensor_tensor(ctmp, ctmp, spare, ALU.mult))
            link(v.tensor_tensor(last, last, ctmp, ALU.add))
            link(v.memset(pay, 0.0))
            link(v.tensor_copy(pay[:, 0:C * NT], pos1[:, :]))
            encode(key, pay, va[:, 0:SC], t2[:, 0:SC], t3[:, 0:SC])
            r = net_sort(1, 15)
            link(v.tensor_copy(srt[1], r[:, 0:SC]))
            dve.sem_inc(srt_rdy, 1)
            after_sort(1, 10)
            v.tensor_copy(dUI[:, :], pi[:, 256:452])
            link(v.tensor_copy(jI[:, :], pi[:, 512:708]))
            dve.sem_inc(idx_rdy, 1)

            def net_join(tab, query, i, loads):
                x0 = t0[:, 0:SC]
                link(v.tensor_scalar(t1[:, 0:SC].bitcast(I32), tab.bitcast(I32), 31, 32767, ALU.arith_shift_right, ALU.bitwise_and))
                link(v.tensor_scalar(x0.bitcast(I32), tab.bitcast(I32), 15, None, ALU.logical_shift_right))
                link(v.tensor_scalar(x0.bitcast(I32), x0.bitcast(I32), 15, None, ALU.logical_shift_left))
                link(v.tensor_tensor(x0.bitcast(I32), x0.bitcast(I32), t1[:, 0:SC].bitcast(I32), ALU.bitwise_or))
                link(v.tensor_copy(va[:, 0:SC], query[:, ::-1]))
                net_turn(va, vb, SC)
                link(v.tensor_copy(va[:, 0:P], vb[:, 0:P][:, ::-1]))
                link(v.tensor_copy(va[:, P:SC], vb[:, P:SC][:, ::-1]))
                net_turn(va, vb, SC)
                v.tensor_tensor(va[:, 0:SC], x0, vb[:, 0:SC], ALU.min)
                link(v.tensor_tensor(va[:, SC:2 * SC], x0, vb[:, 0:SC], ALU.max))
                cur, o = merge_bits(va, vb, 2 * SC, 7)
                k, low = t0, t1
                decode(cur, k, low, o, t3)
                link(v.tensor_scalar(t2, low, 0.0, None, ALU.is_equal))
                link(v.tensor_scalar(cur, k, 1.0, None, ALU.add))
                link(v.tensor_tensor(cur, cur, t2, ALU.mult))
                link(v.tensor_scalar(cur, cur, -1.0, None, ALU.add))
                for h in range(2):
                    q = slice(h * SC, (h + 1) * SC)
                    link(v.tensor_tensor_scan(o[:, q], t2[:, q], t2[:, q], 0.0, ALU.add, ALU.max))
                    link(v.tensor_tensor_scan(t3[:, q], cur[:, q], cur[:, q], -1.0, ALU.max, ALU.max))
                    v.tensor_copy(rs_c[:, h:h + 1], o[:, (h + 1) * SC - 1:(h + 1) * SC])
                    link(v.tensor_copy(rm_c[:, h:h + 1], t3[:, (h + 1) * SC - 1:(h + 1) * SC]))
                small_mms()
                link(v.tensor_copy(cy_c, pi[:, 0:2]))
                link(v.tensor_tensor(cy_c[:, 1:2], cy_c[:, 1:2], pi[:, 2:3], ALU.add))
                link(v.memset(rowb[0:1, 0:1], -1.0))
                link(v.tensor_copy(cur[0:1, 0:2 * P], pi[0:1, 256:512]))
                link(v.tensor_tensor_scan(rowb[0:1, 1:2 * P + 1], cur[0:1, 0:2 * P], cur[0:1, 0:2 * P], -1.0, ALU.max, ALU.max))
                small_mms()
                link(v.tensor_copy(rm_c, pi[:, 512:514]))
                for h in range(2):
                    q = slice(h * SC, (h + 1) * SC)
                    link(v.tensor_scalar(o[:, q], o[:, q], cy_c[:, h:h + 1], -1.0, ALU.add, ALU.add))
                    link(v.tensor_scalar(t3[:, q], t3[:, q], rm_c[:, h:h + 1], None, ALU.max))
                link(v.tensor_tensor(t3, t3, k, ALU.is_equal))
                link(v.scalar_tensor_tensor(out=t3, in0=t2, scalar=0.0, in1=t3, op0=ALU.is_equal, op1=ALU.mult))
                link(v.scalar_tensor_tensor(out=t2, in0=k, scalar=105000.0, in1=t3, op0=ALU.is_lt, op1=ALU.mult))
                link(v.tensor_scalar(low, low, -1.0, None, ALU.add))
                to_row(low, t0, t3)
                to_row(o, cur, t3)
                link(v.tensor_scalar(t0, t0, 256.0 - 60000.0, None, ALU.add))
                link(v.tensor_tensor(t0, t0, t2, ALU.mult))
                link(v.tensor_scalar(t0, t0, 60000.0, None, ALU.add))
                link(v.tensor_scalar(t1, cur, -FAR, None, ALU.add))
                link(v.tensor_tensor(t1, t1, t2, ALU.mult))
                link(v.tensor_scalar(t1, t1, FAR, None, ALU.add))
                pack(t0, t1, va)
                r = net_sort(2, 16)
                link(v.tensor_copy(t0[:, 0:SC], r[:, 0:SC]))
                dve.sem_inc(srt_rdy, 1)
                dve.wait_ge(nb_in, 16 * loads)
                bits = t1[0:98, 0:SC]
                field_of(bits, t0[0:98, 0:SC])
                link(v.tensor_scalar(t0[0:98, 0:SC], t0[0:98, 0:SC], -256.0, None, ALU.add))
                link(v.tensor_scalar(t2[0:98, 0:SC].bitcast(I32), bits.bitcast(I32), 32767, None, ALU.bitwise_and))
                link(v.tensor_copy(t2[0:98, 0:SC], t2[0:98, 0:SC].bitcast(I32)))
                small_mms()
                v.tensor_copy(home[:, :], pi[:, 0:196])
                link(v.tensor_copy(frm[:, :], pi[:, 256:452]))
                dve.sem_inc(idx_rdy, 1)

            net_join(srt[0], srt[1], 0, 11)
            link(v.memset(shf[:, :], 0.0))
            link(v.tensor_copy(shf[:, F:P], ident[:, 0:P - F]))
            dve.sem_inc(ready, 1)
            dense_some(len(order))
            link(v.tensor_reduce(marks, ident[0:PARTS * C * HEADS, 0:PARTS * C * HEADS].rearrange("p (a m) -> p m a", a=PARTS), AXX, ALU.add))
            v.tensor_copy(wSel.rearrange("p h (c f) -> p c h f", f=F),
                          marks.rearrange("p (c h o) -> p c h o", c=C, o=1).to_broadcast([PARTS * C * HEADS, C, HEADS, F]))
            link(v.memset(wSc[:, :, :, :], 0.0))
            for side in range(2):
                for c in range(C):
                    q = slice(F * c, F * c + F)
                    for k in range(SUB):
                        a = F * c + HEADS * k
                        v.tensor_copy(wSc[q, side, k, a:a + HEADS], proj[q, side * HEADS:(side + 1) * HEADS])
            v.tensor_reduce(e32[:, :], ident[:, :].rearrange("p (k h) -> p k h", h=HEADS), AXX, ALU.add)
            v.tensor_reduce(hm[:, :], ident[:, :].rearrange("p (k h) -> p h k", h=HEADS), AXX, ALU.add)
            link(v.tensor_copy(hmt[:, :].rearrange("p (k h) -> p k h", h=HEADS),
                               ident[0:HEADS, 0:HEADS].rearrange("p (o h) -> p o h", o=1).to_broadcast([HEADS, F, HEADS])))
            dve.sem_inc(ready, 1)

            def one(i, l):
                i.then_inc(dve_n[l], 1)

            def ln_out(l, n, o, shift):
                dve.wait_ge(act_n[l], n.act + 3)
                one(v.scalar_tensor_tensor(out=o, in0=ps[l][0][:, 0:W], scalar=shift, in1=HB[l][:, :],
                                           op0=ALU.add, op1=ALU.mult), l)

            def mlp_out(l, n, g, o):
                dve.wait_ge(pe_n[l], n.pe + 2)
                one(v.tensor_scalar(o, ps[l][1][:, 0:W], bg_c[:, 2 * g + 1:2 * g + 2], 0.0, ALU.add, ALU.max), l)

            shifts = [0]

            def carries(end, prod, largest):
                for i in range(C - 1):
                    if i == 0:
                        link(v.tensor_copy(ctmp, end))
                    elif largest:
                        link(v.tensor_scalar(spare, prod, -NEG, NEG, ALU.mult, ALU.add))
                        link(v.tensor_tensor(spare, spare, carry, ALU.add))
                        link(v.tensor_tensor(ctmp, spare, end, ALU.max))
                    else:
                        link(v.scalar_tensor_tensor(out=ctmp, in0=prod, scalar=carry, in1=end, op0=ALU.mult, op1=ALU.add))
                    shifts[0] += 1
                    dve.sem_inc(cr_rdy, 1)
                    dve.wait_ge(cr_mm, shifts[0])
                    link(v.tensor_copy(carry, pc[:, 0:1]))
                    dve.sem_inc(cr_used, 1)

            def scan_block(o, i, mask, b, back, w=W):
                d = slice(None, None, -1) if back else slice(None)
                first = b == (NB - 1 if back else 0)
                at = (b + 1) * w if back else b * w - 1
                link(v.tensor_tensor_scan(blk(o, b, w)[:, d], blk(mask, b, w)[:, d], blk(i, b, w)[:, d],
                                          0.0 if first else o[:, at:at + 1], ALU.mult, ALU.add))

            def lift(mask, o):
                link(v.tensor_scalar(o, mask, -NEG, NEG, ALU.mult, ALU.add))

            def packed_scan(o, i, mask, prod, largest, back):
                d = slice(None, None, -1) if back else slice(None)
                at = slice(0, 1) if back else slice(SW - 1, SW)
                none = NEG if largest else 0.0
                ops = (ALU.add, ALU.max) if largest else (ALU.mult, ALU.add)
                if largest:
                    lift(mask, tm_)
                    mask = tm_
                link(v.tensor_tensor_scan(o[:, d], mask[:, d], i[:, d], none, *ops))
                v.tensor_scalar(ends[:, 0:F], e32[:, :], o[:, at], None, ALU.mult)
                link(v.tensor_copy(ctmp, prod[:, at]))
                link(v.tensor_scalar(ends[:, F:2 * F], e32[:, :], ctmp, None, ALU.mult))
                shifts[0] += 1
                dve.sem_inc(cr_rdy, 1)
                dve.wait_ge(cr_mm, shifts[0])
                link(v.tensor_copy(run[:, 0:2 * F], pc[0:HEADS, 0:2 * F]))
                dve.sem_inc(cr_used, 1)
                if largest:
                    lift(run[:, F:2 * F], run[:, F:2 * F])
                first = 3 * F if back else 2 * F
                link(v.memset(run[:, first:first + 1], none))
                r = run[:, 2 * F:3 * F] if back else run[:, 2 * F + 1:3 * F + 1]
                link(v.tensor_tensor_scan(r[:, d], run[:, F:2 * F][:, d], run[:, 0:F][:, d], none, *ops))
                shifts[0] += 1
                dve.sem_inc(cr_rdy, 1)
                dve.wait_ge(cr_mm, shifts[0])
                link(v.tensor_tensor(ends[:, 0:F], pc[:, 2 * F:3 * F], e32[:, :], ALU.mult))
                dve.sem_inc(cr_used, 1)
                link(v.tensor_reduce(carry, ends[:, 0:F], AXX, ALU.add))
                if largest:
                    lift(prod, tm_)
                    link(v.scalar_tensor_tensor(out=o, in0=tm_, scalar=carry, in1=o, op0=ALU.add, op1=ALU.max))
                else:
                    link(v.scalar_tensor_tensor(out=o, in0=prod, scalar=carry, in1=o, op0=ALU.mult, op1=ALU.add))

            def sum_fix(o, prod, b):
                return v.scalar_tensor_tensor(out=blk(o, b), in0=blk(prod, b), scalar=carry, in1=blk(o, b),
                                              op0=ALU.mult, op1=ALU.add)

            def back_sums(o, i):
                for b in reversed(range(NB)):
                    link(v.scalar_tensor_tensor(out=blk(o, b), in0=blk(NE, b), scalar=0.0, in1=blk(i, b),
                                                op0=ALU.is_equal, op1=ALU.mult))
                    scan_block(o, o, NE, b, True)
                carries(o[:, 0:1], QB[:, 0:1], False)

            def final(s, t, b):
                l = b % 2
                mlp_out(l, before["last", s, b], 0, AB[l][:, :])
                n = before["final", s, b]
                s_ = inv[:, l * KB * C:(l + 1) * KB * C]
                dve.wait_ge(act_n[l], n.act + 1)
                one(v.tensor_reduce(s_, HB[l][:, :].rearrange("p (m f) -> p m f", f=F), AXX, ALU.add), l)
                dve.wait_ge(act_n[l], n.act + 3)
                one(v.tensor_tensor(blk(t, b).rearrange("p (m f) -> p m f", f=F), ps[l][0][:, 0:W].rearrange("p (m f) -> p m f", f=F),
                                    s_.rearrange("p (m o) -> p m o", o=1).to_broadcast([P, KB * C, F]), ALU.mult), l)

            def to4(b):
                l, n = b % 2, before["to4", b]
                dve.wait_ge(pe_n[l], n.pe + 1)
                if b >= 2:
                    dve.wait_ge(r4_out[l], 16 * uses(b))
                dve.wait_ge(ra_in, 16 * (2 * NB + b + 1))
                one(v.tensor_tensor(r4_buf[l].rearrange("p (m w) -> p m w", w=ROW4)[:, :, 0:F],
                                    ps[l][0][:, 0:W].rearrange("p (m f) -> p m f", f=F),
                                    RA[:, :].rearrange("p (m w) -> p m w", w=ATT)[:, :, 16:16 + F], ALU.add), l)

            for L in range(4):
                fb, bb = (T2, T1) if L == 1 else (T1, T2)
                if L == 1:
                    dve.wait_ge(pieces_in, 16 * 2)
                    link(v.tensor_scalar(ctmp, e32[:, F - 1:F], -1.0, 1.0, ALU.mult, ALU.add))
                    link(v.tensor_tensor(ne8[:, SW - 1:SW], ne8[:, SW - 1:SW], ctmp, ALU.mult))
                    v.tensor_tensor_scan(pf8, ns8, ns8, 1.0, ALU.mult, ALU.min)
                    link(v.tensor_tensor_scan(qb8[:, ::-1], ne8[:, ::-1], ne8[:, ::-1], 1.0, ALU.mult, ALU.min))
                    dve.wait_ge(act_n[0], before["score", 0].act + 1)
                    link(v.scalar_tensor_tensor(out=sc_, in0=sc_, scalar=0.2, in1=sc_, op0=ALU.mult, op1=ALU.max))
                    packed_scan(mx_, sc_, ns8, pf8, True, False)
                    packed_scan(mx_, mx_, ne8, qb8, True, True)
                    v.tensor_tensor(sc_, sc_, mx_, ALU.subtract).then_inc(e_rdy, 1)
                    dve.wait_ge(e_exp, 1)
                    packed_scan(sm_, sc_, ns8, pf8, False, False)
                    link(v.scalar_tensor_tensor(out=sm_, in0=ne8, scalar=0.0, in1=sm_, op0=ALU.is_equal, op1=ALU.mult))
                    packed_scan(sm_, sm_, ne8, qb8, False, True)
                    link(v.reciprocal(sm_, sm_))
                    link(v.tensor_tensor(sc_, sc_, sm_, ALU.mult))
                    link(v.tensor_copy(cut[:, 0, :], sc_))
                    link(v.tensor_tensor(sc_, sc_, cut[:, 0, :], ALU.subtract))
                    link(v.tensor_copy(cut[:, 1, :], sc_))
                    v.tensor_tensor(cut[:, 2, :], sc_, cut[:, 1, :], ALU.subtract).then_inc(att_rdy, 1)
                for b in range(SUB if L == 1 else NB):
                    l, n = b % 2, before["msg", L, b] if L < 3 else None
                    if L == 0:
                        dve.wait_ge(pe_n[l], n.pe + 4)
                        one(v.tensor_scalar(blk(T1, b), ps[l][1][:, 0:W], b2a_c, None, ALU.add), l)
                        dve.wait_ge(dve_n[l], n.dve + 1)
                    elif L == 1:
                        for h in range(HEADS):
                            dve.wait_ge(pe_n[l], n.pe + max(2 * h, 1))
                            one(v.tensor_tensor((HB, AB)[h % 2][l][:, 0:SW], blk(D, b, SW), ps[l][0][:, 0:SW], ALU.mult), l)
                        dve.wait_ge(pe_n[l], n.pe + 8)
                        one(v.tensor_copy(blk(T2, b, SW), ps[l][1][:, 0:SW]), l)
                        dve.wait_ge(dve_n[l], n.dve + 5)
                    elif L == 2:
                        dve.wait_ge(pe_n[l], n.pe + 1)
                        one(v.tensor_tensor(blk(T1, b), blk(D, b), ps[l][0][:, 0:W], ALU.mult), l)
                        dve.wait_ge(dve_n[l], n.dve + 1)
                    else:
                        dve.wait_ge(act_n[l], before["from4", b].act + 3)
                    scan_block(fb, fb, NS, b, False, SW if L == 1 else W)
                carries(fb[:, J - 1:J], PF[:, J - 1:J], False)
                for b in range(NB):
                    sum_fix(fb, PF, b).then_inc(fix_n, 1)
                dve.wait_ge(fix_n, (L + 1) * NB)
                if L == 0:
                    for l in range(2):
                        dve.wait_ge(pe_n[l], before["turn", 0, NB - 2 + (l + NB) % 2].pe + 1)
                back_sums(bb, fb)
                for b in range(NB):
                    sum_fix(bb, QB, b).then_inc(tot_n, 1)
                if L == 3:
                    break
                shift = cb_c if L == 1 else zero_c
                for b in range(NB):
                    ln_out(b % 2, before["local", L, b], blk(S, b), shift)
                if L == 2:
                    for b in range(NB):
                        final(0, final_s, b)
                for b in range(NB):
                    ln_out(b % 2, before["other", L, b], blk(D, b), shift)
                    if L == 2:
                        to4(b)
                if L == 2:
                    read_masks(1)
                else:
                    for l in range(2):
                        dve.wait_ge(dve_n[l], before["other", L, NB - 2 + (l + NB) % 2].dve + 1)
            for b in range(NB):
                final(1, D, b)


def kernel(**inputs):
    import numpy as _np
    import concourse.bacc as _bacc
    from concourse import mybir as _mybir
    from concourse.bass_utils import run_bass_kernel_spmd as _run

    a = {k: _np.asarray(v) for k, v in inputs.items()}
    gine = _np.stack([a["L3_gnn_W1"], a["L3_gnn_W2"]], axis=1).reshape(2 * 5, 32, 32)
    laid = [
        ("x", a["x"]), ("src", a["src"]), ("dst", a["dst"]), ("ea16", a["edge_attr_16"]), ("ea32", a["edge_attr_32"]),
        ("ew", a["edge_weight"]), ("w1a", a["L0_gnn_W1"]), ("b1a", a["L0_gnn_b1"]), ("w2a", a["L0_gnn_W2"]),
        ("b2a", a["L0_gnn_b2"]), ("watt", a["L1_gnn_w"].transpose(1, 0, 2)), ("fcw", a["L1_gnn_fc_w"]),
        ("fcb", a["L1_gnn_fc_b"]), ("batt", a["L1_gnn_bias"]), ("wzt", a["L2_gnn_weight"].T), ("eps", a["L3_gnn_eps"]), ("wg", gine.transpose(2, 0, 1)),
        ("bg", _np.stack([a["L3_gnn_b1"], a["L3_gnn_b2"]], axis=1).reshape(10, 32).T),
    ]
    nc = _bacc.Bacc("TRN2", target_bir_lowering=False, num_devices=1)
    arrays, args = {}, []
    for name, v in laid:
        v = _np.ascontiguousarray(v)
        arrays[f"in_{name}"] = v
        args.append(nc.dram_tensor(f"in_{name}", v.shape, _mybir.dt.from_np(v.dtype), kind="ExternalInput").ap())
    args.append(nc.dram_tensor("out_0", (NODES, F), F32, kind="ExternalOutput").ap())
    build(nc, *args)
    r = _run(nc, [arrays], core_ids=[0])
    return r.results[0]["out_0"]
```
